# Optimizing a Trainium2 kernel written in Bass

```python
import numpy as np
import jax
import jax.numpy as jnp

def _softmax(x, axis=-1):
    return jax.nn.softmax(x, axis=axis)

def _gelu(x):
    return jax.nn.gelu(x, approximate=True)

def _silu(x):
    return jax.nn.silu(x)

def _sigmoid(x):
    return jax.nn.sigmoid(x)

def _layernorm(x, axis=-1, eps=1e-05):
    m = jnp.mean(x, axis=axis, keepdims=True)
    v = jnp.var(x, axis=axis, keepdims=True)
    return (x - m) / jnp.sqrt(v + eps)

def _scatter_add(tgt, idx, src, axis=0):
    return tgt.at[idx].add(src)

def _segment_sum(src, seg, n):
    return jax.ops.segment_sum(src, seg, n)
kernel_name = 'mk_audio_tower_d1_tok_audfeat1024_r4_7ee749'

def setup_inputs(seed: int=0):
    np.random.seed(seed)
    _w = jnp.asarray

    def _rec_inputs():
        import jax
        import jax.numpy as jnp
        _rk = jax.random.key(seed)
        x = -0.000392918 + 0.999932 * jax.random.normal(jax.random.fold_in(_rk, 1), (32, 256, 256), jnp.float32)
        return x
    x = _rec_inputs()

    def _L0_tok_setup():
        import jax, jax.numpy as jnp
        import numpy as np
        EMBED_DIM = 256
        ATTN_DIM = 256
        KERNEL = 4
        STRIDE = 4
        LN_EPS = 1e-05
        key = jax.random.key(seed)
        kx, kq, kk, kv = jax.random.split(key, 4)
        B, N = (8, 512)
        x = jax.random.normal(kx, (B, N, EMBED_DIM), dtype=jnp.float32)
        s = 1.0 / np.sqrt(EMBED_DIM)
        Wq = jax.random.normal(kq, (EMBED_DIM, ATTN_DIM), dtype=jnp.float32) * s
        Wk = jax.random.normal(kk, (EMBED_DIM, ATTN_DIM), dtype=jnp.float32) * s
        Wv = jax.random.normal(kv, (EMBED_DIM, ATTN_DIM), dtype=jnp.float32) * s
        gamma = jnp.ones((ATTN_DIM,), dtype=jnp.float32)
        beta = jnp.zeros((ATTN_DIM,), dtype=jnp.float32)
        return {'x': x, 'Wq': Wq, 'Wk': Wk, 'Wv': Wv, 'gamma': gamma, 'beta': beta}
    _L0_tok_all = _L0_tok_setup()
    _L0_tok_in = {k: v for k, v in _L0_tok_all.items() if k in ('Wq', 'Wk', 'Wv', 'gamma', 'beta')}
    del _L0_tok_all

    def _L0_attn_setup():
        import jax, jax.numpy as jnp
        import numpy as np
        B, T, NE, H = (4, 256, 256, 16)
        HS = NE // H
        EPS = 0.00064

        def _forward(x, time_maa_x, time_maa, maa_w1, maa_w2, decay_w1, decay_w2, aaa_w1, aaa_w2, kkk_w1, kkk_w2, gate_w1, gate_w2, ma_w1, ma_w2, mk_w1, mk_w2, time_decay, time_faaaa, time_aaaaa, time_misc_a, time_misc_k, Wr, Wk, Wv, Wo, ln_w, ln_b):
            Bx, Tx, C = x.shape
            xx = jnp.pad(x, ((0, 0), (1, 0), (0, 0)))[:, :Tx] - x
            mix = x + xx * time_maa_x
            lo = jnp.tanh(jnp.einsum('btc,dc->btd', mix, maa_w1)).reshape(Bx, Tx, 4, 32)
            lo = jnp.einsum('btgk,gkc->gbtc', lo, maa_w2)
            xm = x[None] + xx[None] * (lo + time_maa)
            xrg, xwa, xk, xv = (xm[0], xm[1], xm[2], xm[3])
            r = xrg @ Wr.T
            g = jnp.tanh(xrg @ gate_w1.T) @ gate_w2
            k = xk @ Wk.T
            v = xv @ Wv.T
            w2 = jnp.tanh(xwa @ decay_w1.T) @ decay_w2
            w = -jax.nn.softplus(-(time_decay + w2)) - 0.5
            kk = k + jnp.tanh(xk @ kkk_w1.T) @ kkk_w2
            kkh = kk.reshape(Bx, Tx, H, HS)
            kk = (kkh / jnp.maximum(jnp.linalg.norm(kkh, axis=-1, keepdims=True), 1e-12)).reshape(Bx, Tx, C)
            a = jax.nn.sigmoid(time_aaaaa + xwa @ aaa_w1.T @ aaa_w2)
            ma = jax.nn.sigmoid(time_misc_a + xwa @ ma_w1.T @ ma_w2)
            k = k * ma + k * a * (1.0 - ma)
            mk = jax.nn.sigmoid(time_misc_k + xk @ mk_w1.T @ mk_w2)
            k = k * jnp.exp(w * mk)
            b = -kk * a

            def to_th(t):
                return t.reshape(Bx, Tx, H, HS).transpose(1, 0, 2, 3)
            qt, wt, kt, vt, at, bt = map(to_th, (r, w, k, v, kk, b))
            wt = jnp.exp(-jnp.exp(wt))

            def step(s, inp):
                q_, w_, k_, v_, a_, b_ = inp
                sa = jnp.einsum('bhij,bhj->bhi', s, a_)
                s = s * w_[:, :, None, :] + sa[..., None] * b_[:, :, None, :] + v_[..., None] * k_[:, :, None, :]
                return (s, jnp.einsum('bhij,bhj->bhi', s, q_))
            s0 = jnp.zeros((Bx, H, HS, HS), x.dtype)
            _, y = jax.lax.scan(step, s0, (qt, wt, kt, vt, at, bt))
            y = y.transpose(1, 0, 2, 3).reshape(Bx, Tx, C)
            yg = y.reshape(Bx, Tx, H, HS)
            mu = yg.mean(-1, keepdims=True)
            var = ((yg - mu) ** 2).mean(-1, keepdims=True)
            y = ((yg - mu) / jnp.sqrt(var + EPS)).reshape(Bx, Tx, C) * ln_w + ln_b
            rk = (r.reshape(Bx, Tx, H, HS) * k.reshape(Bx, Tx, H, HS) * time_faaaa.reshape(H, HS)).sum(-1, keepdims=True)
            y = y + (rk * v.reshape(Bx, Tx, H, HS)).reshape(Bx, Tx, C)
            return y * g @ Wo.T
        key = jax.random.key(seed)
        ks = jax.random.split(key, 30)

        def rn(k, shape, s):
            return jax.random.normal(k, shape, jnp.float32) * s
        d = {}
        d['x'] = jax.random.normal(ks[0], (B, T, NE), jnp.float32)
        d['time_maa_x'] = jax.random.uniform(ks[1], (NE,), jnp.float32)
        d['time_maa'] = jax.random.uniform(ks[2], (4, 1, 1, NE), jnp.float32)
        d['maa_w1'] = rn(ks[3], (128, NE), 0.02)
        d['maa_w2'] = rn(ks[4], (4, 32, NE), 0.02)
        d['decay_w1'] = rn(ks[5], (64, NE), 0.02)
        d['decay_w2'] = rn(ks[6], (64, NE), 0.02)
        d['aaa_w1'] = rn(ks[7], (16, NE), 0.02)
        d['aaa_w2'] = rn(ks[8], (16, NE), 0.02)
        d['kkk_w1'] = rn(ks[9], (16, NE), 0.02)
        d['kkk_w2'] = rn(ks[10], (16, NE), 0.02)
        d['gate_w1'] = rn(ks[11], (128, NE), 0.02)
        d['gate_w2'] = rn(ks[12], (128, NE), 0.02)
        d['ma_w1'] = rn(ks[13], (16, NE), 0.02)
        d['ma_w2'] = rn(ks[14], (16, NE), 0.02)
        d['mk_w1'] = rn(ks[15], (16, NE), 0.02)
        d['mk_w2'] = rn(ks[16], (16, NE), 0.02)
        d['time_decay'] = jnp.linspace(-6.5, -1.5, NE, dtype=jnp.float32)
        d['time_faaaa'] = rn(ks[17], (NE,), 0.02)
        d['time_aaaaa'] = rn(ks[18], (NE,), 0.02)
        d['time_misc_a'] = rn(ks[19], (NE,), 0.02)
        d['time_misc_k'] = rn(ks[20], (NE,), 0.02)
        d['Wr'] = rn(ks[21], (NE, NE), 0.5 / NE ** 0.5)
        d['Wk'] = rn(ks[22], (NE, NE), 0.05 / NE ** 0.5)
        d['Wv'] = rn(ks[23], (NE, NE), 0.5 / NE ** 0.5)
        d['Wo'] = rn(ks[24], (NE, NE), 1.0 / NE ** 0.5)
        d['ln_w'] = jnp.ones((NE,), jnp.float32)
        d['ln_b'] = jnp.zeros((NE,), jnp.float32)
        return d
    _L0_attn_all = _L0_attn_setup()
    _L0_attn_in = {k: v for k, v in _L0_attn_all.items() if k in ('time_maa_x', 'time_maa', 'maa_w1', 'maa_w2', 'decay_w1', 'decay_w2', 'aaa_w1', 'aaa_w2', 'kkk_w1', 'kkk_w2', 'gate_w1', 'gate_w2', 'ma_w1', 'ma_w2', 'mk_w1', 'mk_w2', 'time_decay', 'time_faaaa', 'time_aaaaa', 'time_misc_a', 'time_misc_k', 'Wr', 'Wk', 'Wv', 'Wo', 'ln_w', 'ln_b')}
    del _L0_attn_all

    def _L0_ffn_setup():
        import jax, jax.numpy as jnp
        import numpy as np
        E = 8
        JITTER = 0.01

        def _sparse_mixer_routing(logits):
            top_vals, top_idx = jax.lax.top_k(logits, 2)
            eidx = jnp.arange(logits.shape[-1])

            def _multiplier(thr, base_logits, idx):
                factor = jnp.maximum(jnp.abs(logits), thr)
                mask = (thr - logits) / factor > 2.0 * JITTER
                probs = jax.nn.softmax(jnp.where(mask, -jnp.inf, base_logits), axis=-1)
                return jnp.take_along_axis(probs, idx, axis=-1)
            mult1 = _multiplier(top_vals[:, :1], logits, top_idx[:, :1])
            scat = jnp.where(eidx[None, :] == top_idx[:, :1], -jnp.inf, logits)
            mult2 = _multiplier(top_vals[:, 1:2], scat, top_idx[:, 1:2])
            return (jnp.concatenate([mult1, mult2], axis=-1), top_idx)
        key = jax.random.key(seed)
        ks = jax.random.split(key, 5)
        H, F = (256, 1024)
        scale = 0.02
        return {'hidden_states': jax.random.normal(ks[0], (1, 512, H), jnp.float32), 'gate_w': jax.random.normal(ks[1], (H, E), jnp.float32) * scale, 'w1': jax.random.normal(ks[2], (E, H, F), jnp.float32) * scale, 'w2': jax.random.normal(ks[3], (E, F, H), jnp.float32) * scale, 'w3': jax.random.normal(ks[4], (E, H, F), jnp.float32) * scale}
    _L0_ffn_all = _L0_ffn_setup()
    _L0_ffn_in = {k: v for k, v in _L0_ffn_all.items() if k in ('gate_w', 'w1', 'w2', 'w3')}
    del _L0_ffn_all
    return {'x': x, 'L0_tok_Wq': _L0_tok_in['Wq'], 'L0_tok_Wk': _L0_tok_in['Wk'], 'L0_tok_Wv': _L0_tok_in['Wv'], 'L0_tok_gamma': _L0_tok_in['gamma'], 'L0_tok_beta': _L0_tok_in['beta'], 'L0_attn_time_maa_x': _L0_attn_in['time_maa_x'], 'L0_attn_time_maa': _L0_attn_in['time_maa'], 'L0_attn_maa_w1': _L0_attn_in['maa_w1'], 'L0_attn_maa_w2': _L0_attn_in['maa_w2'], 'L0_attn_decay_w1': _L0_attn_in['decay_w1'], 'L0_attn_decay_w2': _L0_attn_in['decay_w2'], 'L0_attn_aaa_w1': _L0_attn_in['aaa_w1'], 'L0_attn_aaa_w2': _L0_attn_in['aaa_w2'], 'L0_attn_kkk_w1': _L0_attn_in['kkk_w1'], 'L0_attn_kkk_w2': _L0_attn_in['kkk_w2'], 'L0_attn_gate_w1': _L0_attn_in['gate_w1'], 'L0_attn_gate_w2': _L0_attn_in['gate_w2'], 'L0_attn_ma_w1': _L0_attn_in['ma_w1'], 'L0_attn_ma_w2': _L0_attn_in['ma_w2'], 'L0_attn_mk_w1': _L0_attn_in['mk_w1'], 'L0_attn_mk_w2': _L0_attn_in['mk_w2'], 'L0_attn_time_decay': _L0_attn_in['time_decay'], 'L0_attn_time_faaaa': _L0_attn_in['time_faaaa'], 'L0_attn_time_aaaaa': _L0_attn_in['time_aaaaa'], 'L0_attn_time_misc_a': _L0_attn_in['time_misc_a'], 'L0_attn_time_misc_k': _L0_attn_in['time_misc_k'], 'L0_attn_Wr': _L0_attn_in['Wr'], 'L0_attn_Wk': _L0_attn_in['Wk'], 'L0_attn_Wv': _L0_attn_in['Wv'], 'L0_attn_Wo': _L0_attn_in['Wo'], 'L0_attn_ln_w': _L0_attn_in['ln_w'], 'L0_attn_ln_b': _L0_attn_in['ln_b'], 'L0_ffn_gate_w': _L0_ffn_in['gate_w'], 'L0_ffn_w1': _L0_ffn_in['w1'], 'L0_ffn_w2': _L0_ffn_in['w2'], 'L0_ffn_w3': _L0_ffn_in['w3']}

def reference(x, L0_tok_Wq, L0_tok_Wk, L0_tok_Wv, L0_tok_gamma, L0_tok_beta, L0_attn_time_maa_x, L0_attn_time_maa, L0_attn_maa_w1, L0_attn_maa_w2, L0_attn_decay_w1, L0_attn_decay_w2, L0_attn_aaa_w1, L0_attn_aaa_w2, L0_attn_kkk_w1, L0_attn_kkk_w2, L0_attn_gate_w1, L0_attn_gate_w2, L0_attn_ma_w1, L0_attn_ma_w2, L0_attn_mk_w1, L0_attn_mk_w2, L0_attn_time_decay, L0_attn_time_faaaa, L0_attn_time_aaaaa, L0_attn_time_misc_a, L0_attn_time_misc_k, L0_attn_Wr, L0_attn_Wk, L0_attn_Wv, L0_attn_Wo, L0_attn_ln_w, L0_attn_ln_b, L0_ffn_gate_w, L0_ffn_w1, L0_ffn_w2, L0_ffn_w3):
    import jax
    import jax.numpy as jnp

    def _L0_tok_ref(x, Wq, Wk, Wv, gamma, beta):
        import jax, jax.numpy as jnp
        import numpy as np
        EMBED_DIM = 256
        ATTN_DIM = 256
        KERNEL = 4
        STRIDE = 4
        LN_EPS = 1e-05
        q = jnp.einsum('bne,ea->bna', x, Wq)
        k = jnp.einsum('bne,ea->bna', x, Wk)
        v = jnp.einsum('bne,ea->bna', x, Wv)
        scale = 1.0 / jnp.sqrt(jnp.asarray(q.shape[-1], q.dtype))
        attn_weight = jax.nn.softmax(jnp.einsum('bqa,bka->bqk', q, k) * scale, axis=-1)
        B, N, _ = attn_weight.shape
        pooled = attn_weight.reshape(B, N // STRIDE, KERNEL, N).mean(axis=2)
        attn = jnp.einsum('bpk,bka->bpa', pooled, v)
        mu = attn.mean(axis=-1, keepdims=True)
        var = attn.var(axis=-1, keepdims=True)
        z = (attn - mu) * jax.lax.rsqrt(var + LN_EPS) * gamma + beta
        return z

    def _L0_attn_ref(x, time_maa_x, time_maa, maa_w1, maa_w2, decay_w1, decay_w2, aaa_w1, aaa_w2, kkk_w1, kkk_w2, gate_w1, gate_w2, ma_w1, ma_w2, mk_w1, mk_w2, time_decay, time_faaaa, time_aaaaa, time_misc_a, time_misc_k, Wr, Wk, Wv, Wo, ln_w, ln_b):
        import jax, jax.numpy as jnp
        import numpy as np
        B, T, NE, H = (4, 256, 256, 16)
        HS = NE // H
        EPS = 0.00064

        def _forward(x, time_maa_x, time_maa, maa_w1, maa_w2, decay_w1, decay_w2, aaa_w1, aaa_w2, kkk_w1, kkk_w2, gate_w1, gate_w2, ma_w1, ma_w2, mk_w1, mk_w2, time_decay, time_faaaa, time_aaaaa, time_misc_a, time_misc_k, Wr, Wk, Wv, Wo, ln_w, ln_b):
            Bx, Tx, C = x.shape
            xx = jnp.pad(x, ((0, 0), (1, 0), (0, 0)))[:, :Tx] - x
            mix = x + xx * time_maa_x
            lo = jnp.tanh(jnp.einsum('btc,dc->btd', mix, maa_w1)).reshape(Bx, Tx, 4, 32)
            lo = jnp.einsum('btgk,gkc->gbtc', lo, maa_w2)
            xm = x[None] + xx[None] * (lo + time_maa)
            xrg, xwa, xk, xv = (xm[0], xm[1], xm[2], xm[3])
            r = xrg @ Wr.T
            g = jnp.tanh(xrg @ gate_w1.T) @ gate_w2
            k = xk @ Wk.T
            v = xv @ Wv.T
            w2 = jnp.tanh(xwa @ decay_w1.T) @ decay_w2
            w = -jax.nn.softplus(-(time_decay + w2)) - 0.5
            kk = k + jnp.tanh(xk @ kkk_w1.T) @ kkk_w2
            kkh = kk.reshape(Bx, Tx, H, HS)
            kk = (kkh / jnp.maximum(jnp.linalg.norm(kkh, axis=-1, keepdims=True), 1e-12)).reshape(Bx, Tx, C)
            a = jax.nn.sigmoid(time_aaaaa + xwa @ aaa_w1.T @ aaa_w2)
            ma = jax.nn.sigmoid(time_misc_a + xwa @ ma_w1.T @ ma_w2)
            k = k * ma + k * a * (1.0 - ma)
            mk = jax.nn.sigmoid(time_misc_k + xk @ mk_w1.T @ mk_w2)
            k = k * jnp.exp(w * mk)
            b = -kk * a

            def to_th(t):
                return t.reshape(Bx, Tx, H, HS).transpose(1, 0, 2, 3)
            qt, wt, kt, vt, at, bt = map(to_th, (r, w, k, v, kk, b))
            wt = jnp.exp(-jnp.exp(wt))

            def step(s, inp):
                q_, w_, k_, v_, a_, b_ = inp
                sa = jnp.einsum('bhij,bhj->bhi', s, a_)
                s = s * w_[:, :, None, :] + sa[..., None] * b_[:, :, None, :] + v_[..., None] * k_[:, :, None, :]
                return (s, jnp.einsum('bhij,bhj->bhi', s, q_))
            s0 = jnp.zeros((Bx, H, HS, HS), x.dtype)
            _, y = jax.lax.scan(step, s0, (qt, wt, kt, vt, at, bt))
            y = y.transpose(1, 0, 2, 3).reshape(Bx, Tx, C)
            yg = y.reshape(Bx, Tx, H, HS)
            mu = yg.mean(-1, keepdims=True)
            var = ((yg - mu) ** 2).mean(-1, keepdims=True)
            y = ((yg - mu) / jnp.sqrt(var + EPS)).reshape(Bx, Tx, C) * ln_w + ln_b
            rk = (r.reshape(Bx, Tx, H, HS) * k.reshape(Bx, Tx, H, HS) * time_faaaa.reshape(H, HS)).sum(-1, keepdims=True)
            y = y + (rk * v.reshape(Bx, Tx, H, HS)).reshape(Bx, Tx, C)
            return y * g @ Wo.T
        return _forward(x, time_maa_x, time_maa, maa_w1, maa_w2, decay_w1, decay_w2, aaa_w1, aaa_w2, kkk_w1, kkk_w2, gate_w1, gate_w2, ma_w1, ma_w2, mk_w1, mk_w2, time_decay, time_faaaa, time_aaaaa, time_misc_a, time_misc_k, Wr, Wk, Wv, Wo, ln_w, ln_b)

    def _L0_ffn_ref(hidden_states, gate_w, w1, w2, w3):
        import jax, jax.numpy as jnp
        import numpy as np
        E = 8
        JITTER = 0.01

        def _sparse_mixer_routing(logits):
            top_vals, top_idx = jax.lax.top_k(logits, 2)
            eidx = jnp.arange(logits.shape[-1])

            def _multiplier(thr, base_logits, idx):
                factor = jnp.maximum(jnp.abs(logits), thr)
                mask = (thr - logits) / factor > 2.0 * JITTER
                probs = jax.nn.softmax(jnp.where(mask, -jnp.inf, base_logits), axis=-1)
                return jnp.take_along_axis(probs, idx, axis=-1)
            mult1 = _multiplier(top_vals[:, :1], logits, top_idx[:, :1])
            scat = jnp.where(eidx[None, :] == top_idx[:, :1], -jnp.inf, logits)
            mult2 = _multiplier(top_vals[:, 1:2], scat, top_idx[:, 1:2])
            return (jnp.concatenate([mult1, mult2], axis=-1), top_idx)
        B, S, H = hidden_states.shape
        x = hidden_states.reshape(-1, H)
        logits = x @ gate_w
        mult, sel = _sparse_mixer_routing(logits)
        w = jnp.sum(mult[:, :, None] * (sel[:, :, None] == jnp.arange(E)[None, None, :]), axis=1)
        h = jax.nn.silu(jnp.einsum('th,ehf->etf', x, w1)) * jnp.einsum('th,ehf->etf', x, w3)
        out = jnp.einsum('etf,efh,te->th', h, w2, w)
        return out.reshape(B, S, H)
    h = _L0_tok_ref(x, L0_tok_Wq, L0_tok_Wk, L0_tok_Wv, L0_tok_gamma, L0_tok_beta)
    h = h + _L0_attn_ref(_layernorm(h, axis=-1), L0_attn_time_maa_x, L0_attn_time_maa, L0_attn_maa_w1, L0_attn_maa_w2, L0_attn_decay_w1, L0_attn_decay_w2, L0_attn_aaa_w1, L0_attn_aaa_w2, L0_attn_kkk_w1, L0_attn_kkk_w2, L0_attn_gate_w1, L0_attn_gate_w2, L0_attn_ma_w1, L0_attn_ma_w2, L0_attn_mk_w1, L0_attn_mk_w2, L0_attn_time_decay, L0_attn_time_faaaa, L0_attn_time_aaaaa, L0_attn_time_misc_a, L0_attn_time_misc_k, L0_attn_Wr, L0_attn_Wk, L0_attn_Wv, L0_attn_Wo, L0_attn_ln_w, L0_attn_ln_b)
    h = h + _L0_ffn_ref(_layernorm(h, axis=-1), L0_ffn_gate_w, L0_ffn_w1, L0_ffn_w2, L0_ffn_w3)
    return h

_drawn_inputs = setup_inputs


def setup_inputs(seed=0):
    import zlib

    import numpy as np

    out = dict(_drawn_inputs(seed))
    spreads = {'L0_tok_gamma': (1.0, 0.2),
     'L0_tok_beta': (0.0, 0.1),
     'L0_attn_ln_w': (1.0, 0.6),
     'L0_attn_ln_b': (0.0, 0.8)}
    factors = {'L0_attn_time_maa_x': 8.0,
     'L0_attn_time_maa': 3.95,
     'L0_attn_maa_w1': 8.0,
     'L0_attn_maa_w2': 8.0,
     'L0_attn_decay_w1': 64.0,
     'L0_attn_decay_w2': 64.0,
     'L0_attn_aaa_w1': 8.0,
     'L0_attn_aaa_w2': 8.0,
     'L0_attn_ma_w1': 8.0,
     'L0_attn_ma_w2': 8.0,
     'L0_attn_mk_w1': 8.0,
     'L0_attn_mk_w2': 8.0,
     'L0_attn_time_decay': 4.428,
     'L0_attn_time_faaaa': 189.739,
     'L0_attn_time_aaaaa': 64.0,
     'L0_attn_time_misc_a': 64.0,
     'L0_attn_time_misc_k': 39.024}
    for name, (base, spread) in spreads.items():
        noise = np.random.default_rng([zlib.crc32(name.encode()), seed]).standard_normal(out[name].shape)
        drawn = base * np.exp(spread * noise) if base else spread * noise
        out[name] = jnp.asarray(drawn.astype(out[name].dtype))
    for name, factor in factors.items():
        out[name] = (out[name] * factor).astype(out[name].dtype)
    return out
```

```python
from contextlib import ExitStack

import numpy as np

import concourse.bass as bass
from concourse import mybir

F32 = mybir.dt.float32
ALU = mybir.AluOpType
ACT = mybir.ActivationFunctionType
AX_X = mybir.AxisListType.X

P = 128
B, N, E = 32, 256, 256
KC = E // P
STRIDE = 4
T = N // STRIDE
TOK = B * T
TILES = TOK // P
LN_EPS = 1e-5
BANK = 512


def wait(eng, sem, count):
    if isinstance(count, int) and count <= 0:
        return
    eng.wait_ge(sem, count)


class Chain:

    def __init__(self, eng, sem):
        self.eng, self.sem, self.done, self.turns = eng, sem, 0, 0

    def __call__(self, ins):
        self.done += 1
        ins.then_inc(self.sem, 1)
        self.eng.wait_ge(self.sem, self.turns + self.done)

    def enter(self, turn, per_turn):
        self.before, self.per_turn = self.done, per_turn
        self.turns = turn * per_turn

    def leave(self, turns):
        assert self.done - self.before == self.per_turn, (self.done - self.before, self.per_turn)
        self.turns = 0
        self.done = self.before + turns * self.per_turn


def inverse_sqrt(dve, chain, y, t, v):
    i32 = mybir.dt.int32
    chain(dve.tensor_scalar(t.bitcast(i32), v.bitcast(i32), 1, None, ALU.logical_shift_right))
    chain(dve.tensor_scalar(y.bitcast(i32), t.bitcast(i32), -1.0, float(0x5F3759DF), ALU.mult, ALU.add))
    for _ in range(3):
        chain(dve.tensor_tensor(t, y, y, ALU.mult))
        chain(dve.tensor_tensor(t, t, v, ALU.mult))
        chain(dve.tensor_scalar(t, t, -0.5, 1.5, ALU.mult, ALU.add))
        chain(dve.tensor_tensor(y, y, t, ALU.mult))


RSQRT_LINKS = 14


def touch(dve, tile):
    dve.memset(tile[:, 0:1], 0.0)


def tok_stage(nc, d, c):
    with ExitStack() as ctx:
        sb = lambda name, shape: ctx.enter_context(nc.sbuf_tensor("tok_" + name, shape, F32))
        sem = lambda name: ctx.enter_context(nc.semaphore(name))
        wq_t = sb("wq_t", [P, KC, E])
        wk_t = sb("wk_t", [P, KC, E])
        wv = sb("wv", [P, KC, E])
        wqk = sb("wqk", [P, KC, E])
        gamma = sb("gamma", [P, E])
        beta = sb("beta", [P, E])
        x_in = sb("x_in", [P, 2, KC, E])
        xT_in = sb("xT_in", [P, 2, KC, N])
        g_sb = sb("g_sb", [P, 2, KC, N])
        probs = sb("probs", [P, 2, 2, N])
        pool_w = sb("pool_w", [P, P // STRIDE])
        pool_r = sb("pool_r", [P, 2, 2, P // STRIDE])
        pooled = sb("pooled", [P, 2, 2, T])
        px_sb = sb("px_sb", [P, KC, 2, T])
        mx = sb("mx", [P, 2, 2])
        neg_mx = sb("neg_mx", [P, 2, 2])
        row_sum = sb("row_sum", [P, 2, 2])
        row_inv = sb("row_inv", [P, 2, 2])
        stats = sb("stats", [P, 6])
        mean_var = sb("mean_var", [P, 2, 2])
        var_eps = sb("var_eps", [P, 2])
        rstd = sb("rstd", [P, 2])
        nwt = sb("nwt", [P, 1])
        attn_n = sb("attn_n", [P, E])
        h_tmp = sb("h_tmp", [P, E])
        xn = sb("xn", [P, E])
        ps = ctx.enter_context(nc.psum_tensor("ps_tok", [P, 8, BANK], F32))
        ps_g = [ps[:, b, :].rearrange("p (c n) -> p c n", c=KC) for b in (0, 1)]
        ps_s = [ps[:, 2 + b, :].rearrange("p (c n) -> p c n", c=2) for b in (0, 1)]
        ps_pool = ps[:, 4, 0:2 * T].rearrange("p (c t) -> p c t", c=2)
        ps_px = ps[:, 5, 0:KC * T].rearrange("p (c t) -> p c t", c=KC)
        ps_attn = ps[:, 6, 0:E]
        ps_tr = ps[:, 7, 0:KC * P].rearrange("p (c t) -> p c t", c=KC)

        w_in = sem("tok_wq_wk_in")
        wv_in = sem("tok_wv_gamma_beta_in")
        xT_loaded = [sem("xT_loaded0"), sem("xT_loaded1")]
        x_loaded = [sem("x_loaded0"), sem("x_loaded1")]
        pw_set = sem("pool_w_set")
        wqk_done = sem("wqk_done")
        wqk_copied = sem("wqk_copied")
        g_done = sem("g_done")
        g_copied = sem("g_copied")
        s_done = sem("s_done")
        nb_ready = sem("neg_max_ready")
        exp_done = sem("exp_done")
        er_ready = sem("pool_r_ready")
        pool_done = sem("pool_done")
        pool_copied = sem("pool_copied")
        px_done = sem("px_done")
        px_copied = sem("px_copied")
        attn_done = sem("attn_done")
        attn_read = sem("attn_read")
        xn_ready = sem("xn_ready")
        tr_done = sem("tr_done")
        tr_copied = sem("tr_copied")
        dve_link = sem("tok_dve_link")
        id_set = sem("ident_set")
        block = ctx.enter_context(nc.Block())

        HALF = B // 2 - 2

        def steps(eng, step, chain=None, links=0):
            for n in range(3):
                step(n, n // 2, n % 2)
            with eng.Fori(0, HALF) as i:
                if chain:
                    chain.enter(i, links)
                step(2 * i + 3, i + 1, 1, inner=True)
                step(2 * i + 4, i + 2, 0, inner=True)
                if chain:
                    chain.leave(HALF)
            for n in range(B - 1, B + 3):
                step(n, n // 2, n % 2)

        @block.sync
        def _(sp):
            sp.dma_start(wq_t[:], d["wqT"].rearrange("(c p) e -> p c e", p=P)).then_inc(w_in, 16)
            sp.dma_start(wk_t[:], d["wkT"].rearrange("(c p) e -> p c e", p=P)).then_inc(w_in, 16)

            def load_xT(n, par):
                wait(sp, s_done, n - 1)
                sp.dma_start(xT_in[:, par, :, :], d["xT"][bass.ds(n, 1)].rearrange("o (c p) n -> p (o c) n", p=P)
                             ).then_inc(xT_loaded[par], 16)

            def load_x(n, par):
                wait(sp, px_done, n - 1)
                sp.dma_start(x_in[:, par, :, :], d["x"][bass.ds(n, 1)].rearrange("o (c p) e -> p (o c) e", p=P)
                             ).then_inc(x_loaded[par], 16)

            load_xT(0, 0)
            load_xT(1, 1)
            load_x(0, 0)
            sp.dma_start(wv[:], d["wv"].rearrange("(c p) e -> p c e", p=P)).then_inc(wv_in, 16)
            sp.dma_start(gamma[:], d["gamma"].partition_broadcast(P)).then_inc(wv_in, 16)
            sp.dma_start(beta[:], d["beta"].partition_broadcast(P)).then_inc(wv_in, 16)
            with sp.Fori(0, B // 2 - 1) as i:
                load_xT(2 * i + 2, 0)
                load_x(2 * i + 1, 1)
                load_xT(2 * i + 3, 1)
                load_x(2 * i + 2, 0)
            load_x(B - 1, 1)

        @block.gpsimd
        def _(pool):
            pool.memset(pool_w[:], 1.0 / STRIDE).then_inc(pw_set, 1)
            pool.wait_ge(pw_set, 1)
            pool.affine_select(out=pool_w[:], in_=pool_w[:], compare_op=ALU.is_ge, fill=0.0, base=0,
                               pattern=[[-STRIDE, P // STRIDE]], channel_multiplier=1).then_inc(pw_set, 1)
            pool.wait_ge(pw_set, 2)
            pool.affine_select(out=pool_w[:], in_=pool_w[:], compare_op=ALU.is_ge, fill=0.0, base=STRIDE - 1,
                               pattern=[[STRIDE, P // STRIDE]], channel_multiplier=-1).then_inc(pw_set, 1)
            pool.memset(c.ident[:], 0.0).then_inc(id_set, 1)
            pool.wait_ge(id_set, 1)
            pool.affine_select(out=c.ident[:], in_=c.ident[:], compare_op=ALU.not_equal, fill=1.0, base=0,
                               pattern=[[-1, P]], channel_multiplier=1).then_inc(id_set, 1)

        @block.tensor
        def _(pe):
            pe.wait_ge(w_in, 32)
            for ec in range(KC):
                for k in range(KC):
                    last = pe.matmul(ps_s[0][:, ec, :], wq_t[:, k, ec * P:(ec + 1) * P], wk_t[:, k, :],
                                     start=(k == 0), stop=(k == KC - 1))
            last.then_inc(wqk_done, 1)

            def g_mm(n, half, par):
                pe.wait_ge(xT_loaded[par], 16 * (half + 1))
                wait(pe, g_copied, n - 1)
                for ec in range(KC):
                    for k in range(KC):
                        last = pe.matmul(ps_g[par][:, ec, :], wqk[:, k, ec * P:(ec + 1) * P],
                                         xT_in[:, par, k, :], start=(k == 0), stop=(k == KC - 1))
                last.then_inc(g_done, 1)

            def s_mm(n, par):
                pe.wait_ge(g_copied, n + 1)
                wait(pe, exp_done, n - 1)
                for qc in range(2):
                    for k in range(KC):
                        last = pe.matmul(ps_s[par][:, qc, :], g_sb[:, par, k, qc * P:(qc + 1) * P],
                                         xT_in[:, par, k, :], start=(k == 0), stop=(k == KC - 1))
                last.then_inc(s_done, 1)

            def pool_mm(n, par):
                pe.wait_ge(er_ready, n + 1)
                wait(pe, pool_copied, n)
                half_t = T // 2
                for kc in range(2):
                    for qc in range(2):
                        last = pe.matmul(ps_pool[:, kc, qc * half_t:(qc + 1) * half_t],
                                         probs[:, par, qc, kc * P:(kc + 1) * P], pool_r[:, par, qc, :],
                                         start=True, stop=True)
                last.then_inc(pool_done, 1)

            def px_mm(n, half, par):
                pe.wait_ge(x_loaded[par], 16 * (half + 1))
                pe.wait_ge(pool_copied, n + 1)
                wait(pe, px_copied, n)
                for ec in range(KC):
                    for k in range(2):
                        last = pe.matmul(ps_px[:, ec, :], x_in[:, par, k, ec * P:(ec + 1) * P],
                                         pooled[:, par, k, :], start=(k == 0), stop=(k == 1))
                last.then_inc(px_done, 1)

            def attn_mm(p):
                pe.wait_ge(px_copied, 2 * p + 2)
                wait(pe, attn_read, p)
                for k in range(KC):
                    last = pe.matmul(ps_attn, px_sb[:, k, :, :].rearrange("p b t -> p (b t)"), wv[:, k, :],
                                     start=(k == 0), stop=(k == KC - 1))
                last.then_inc(attn_done, 1)

            def tr_mm(p):
                pe.wait_ge(xn_ready, p + 1)
                wait(pe, tr_copied, p)
                for k in range(KC):
                    last = pe.transpose(ps_tr[:, k, :], xn[:, k * P:(k + 1) * P], c.ident[:])
                last.then_inc(tr_done, 1)

            pe.wait_ge(wqk_copied, 1)
            g_mm(0, 0, 0)
            pe.wait_ge(wv_in, 48)
            pe.wait_ge(id_set, 2)

            def step(n, half, par, inner=False):
                if inner or n < B:
                    s_mm(n, par)
                if inner or 1 <= n <= B:
                    pool_mm(n - 1, 1 - par)
                if inner or n + 1 < B:
                    g_mm(n + 1, half + par, 1 - par)
                if inner or 1 <= n <= B:
                    px_mm(n - 1, half + par - 1, 1 - par)
                if par == 0 and (inner or 2 <= n <= B):
                    attn_mm(half - 1)
                if par == 0 and (inner or n >= 4):
                    tr_mm(half - 2)

            steps(pe, step)

        @block.scalar
        def _(act):
            def copy_g(n, par):
                act.wait_ge(g_done, n + 1)
                wait(act, s_done, n - 1)
                act.copy(g_sb[:, par, :, :], ps_g[par]).then_inc(g_copied, 1)

            def exps(n, par):
                act.wait_ge(nb_ready, n + 1)
                wait(act, pool_done, n - 1)
                act.activation(probs[:, par, 0, :], ps_s[par][:, 0, :], ACT.Exp, bias=neg_mx[:, par, 0:1],
                               scale=float(E) ** -0.5, accum_out=row_sum[:, par, 0:1])
                act.activation(probs[:, par, 1, :], ps_s[par][:, 1, :], ACT.Exp, bias=neg_mx[:, par, 1:2],
                               scale=float(E) ** -0.5, accum_out=row_sum[:, par, 1:2]).then_inc(exp_done, 1)

            def step(n, half, par, inner=False):
                if inner or n < B:
                    exps(n, par)
                if inner or n + 1 < B:
                    copy_g(n + 1, 1 - par)
                if inner or 1 <= n <= B:
                    act.wait_ge(px_done, n)
                    if par == 1:
                        wait(act, attn_done, half)
                    act.copy(px_sb[:, :, 1 - par, :], ps_px).then_inc(px_copied, 1)

            act.wait_ge(g_done, 1)
            act.copy(g_sb[:, 0, :, :], ps_g[0]).then_inc(g_copied, 1)
            steps(act, step)

        @block.vector
        def _(dve):
            chain = Chain(dve, dve_link)
            dve.wait_ge(wqk_done, 1)
            dve.tensor_copy(wqk[:], ps_s[0]).then_inc(wqk_copied, 1)
            dve.wait_ge(pw_set, 3)
            dve.wait_ge(wv_in, 48)

            def row_max(n, par):
                dve.wait_ge(s_done, n + 1)
                chain(dve.tensor_reduce(mx[:, par, :], ps_s[par], AX_X, ALU.max))
                dve.tensor_scalar(neg_mx[:, par, :], mx[:, par, :], -float(E) ** -0.5, None,
                                  ALU.mult).then_inc(nb_ready, 1)

            def pool_weights(n, par):
                dve.wait_ge(exp_done, n + 1)
                wait(dve, pool_done, n - 1)
                chain(dve.reciprocal(row_inv[:, par, :], row_sum[:, par, :]))
                dve.tensor_scalar(pool_r[:, par, 0, :], pool_w[:], row_inv[:, par, 0:1], None, ALU.mult)
                dve.tensor_scalar(pool_r[:, par, 1, :], pool_w[:], row_inv[:, par, 1:2], None,
                                  ALU.mult).then_inc(er_ready, 1)

            def copy_pooled(n, par):
                dve.wait_ge(pool_done, n + 1)
                wait(dve, px_done, n - 1)
                dve.tensor_copy(pooled[:, par, :, :], ps_pool).then_inc(pool_copied, 1)

            def moments(w, src):
                chain(dve.bn_stats(stats[:], src))
                touch(dve, nwt)
                chain(dve.bn_aggr(mean_var[:, w, :], stats[:]))
                chain(dve.tensor_scalar(var_eps[:, w:w + 1], mean_var[:, w, 1:2], LN_EPS, None, ALU.add))

            def norm_1(p):
                inverse_sqrt(dve, chain, rstd[:, 0:1], nwt[:], var_eps[:, 0:1])
                ins = dve.tensor_scalar(attn_n[:], ps_attn, mean_var[:, 0, 0:1], rstd[:, 0:1], ALU.subtract, ALU.mult)
                ins.then_inc(attn_read, 1)
                dve.wait_ge(attn_read, p + 1)
                chain(dve.tensor_tensor(h_tmp[:], attn_n[:], gamma[:], ALU.mult))
                chain(dve.tensor_tensor(xn[:], h_tmp[:], beta[:], ALU.add))
                moments(1, xn[:])
                dve.tensor_tensor(c.h[:, bass.ds(p, 1), :].rearrange("p o e -> p (o e)"), h_tmp[:], beta[:], ALU.add)

            def norm_2(p):
                inverse_sqrt(dve, chain, rstd[:, 1:2], nwt[:], var_eps[:, 1:2])
                dve.tensor_scalar(xn[:], xn[:], mean_var[:, 1, 0:1], rstd[:, 1:2], ALU.subtract,
                                  ALU.mult).then_inc(xn_ready, 1)

            def copy_xnT(p):
                dve.wait_ge(tr_done, p + 1)
                dve.tensor_scalar(c.xnT[:, :, bass.ds(p * P, P)], ps_tr, 1.0, None, ALU.mult).then_inc(tr_copied, 1)

            def step(n, half, par, inner=False):
                if inner or n < B:
                    row_max(n, par)
                if inner or 1 <= n <= B:
                    copy_pooled(n - 1, 1 - par)
                if par == 1 and (inner or n >= 3):
                    norm_1(half - 1)
                if inner or n < B:
                    pool_weights(n, par)
                if par == 0 and (inner or 2 <= n <= B):
                    dve.wait_ge(attn_done, half)
                    moments(0, ps_attn)
                if par == 1 and (inner or n >= 3):
                    norm_2(half - 1)
                if par == 0 and (inner or n >= 4):
                    copy_xnT(half - 2)

            steps(dve, step, chain, 2 + 2 + 2 * (3 + RSQRT_LINKS) + 2)


SL = 256
SLICES = TOK // SL
ST = SL // P
SB = SL // T
HEADS, HS = 16, 16
LOW_D, LOW = 64, 16
ARRAYS = 5
SCAN_Q, SCAN_A, SCAN_B, SCAN_K, SCAN_V = ROW_Q, ROW_A, ROW_B, ROW_K, ROW_V = range(ARRAYS)
TINY = 1e-24


def mix_stage(nc, d, c):
    with ExitStack() as ctx:
        sb = lambda name, shape: ctx.enter_context(nc.sbuf_tensor("mix_" + name, shape, F32))
        sem = lambda name: ctx.enter_context(nc.semaphore("mix_" + name))
        maa = sb("maa", [P, KC, 5])
        maa_w1 = sb("maa_w1", [P, KC, P])
        maa_w2 = sb("maa_w2", [P, E])
        w_r, w_k, w_v = (sb(n, [P, KC, E]) for n in ("w_r", "w_k", "w_v"))
        w_a1 = sb("w_a1", [P, KC, P])
        w_a2 = sb("w_a2", [P, 3 * E])
        a_bias = sb("a_bias", [P, 2])
        w_b1 = sb("w_b1", [P, KC, 64])
        w_b2 = sb("w_b2", [64, 2 * E])
        w_g1 = sb("w_g1", [P, KC, P])
        w_g2 = sb("w_g2", [P, E])
        faaaa = sb("faaaa", [P, E])

        xx = sb("xx", [P, KC, SL])
        mix = sb("mix", [P, KC, SL])
        lo1 = sb("lo1", [P, SL])
        xm = sb("xm", [P, 4, KC, SL])
        xm_tmp = sb("xm_tmp", [P, 2, SL])
        hid_a = sb("hid_a", [P, SL])
        hid_g = sb("hid_g", [P, SL])
        hid_b = sb("hid_b", [64, SL])

        scan = sb("scan", [P, 2, ST, ARRAYS, E])
        cum = sb("cum", [P, 3, ST, E])
        tri = sb("tri", [P, 2, P])
        k_raw = sb("k_raw", [P, 2, ST, E])
        kk = sb("kk", [P, 2, ST, E])
        zd = sb("zd", [P, 2, ST, E])
        a_sig = sb("a_sig", [P, 2, ST, E])
        mam_k = sb("mam_k", [P, 2, ST, 2, E])
        t0 = sb("t0", [P, ST, E])
        t1 = sb("t1", [P, ST, E])
        az = sb("az", [P, ST, E])
        mn = sb("mn", [P, ST, E])
        k2 = sb("k2", [P, ST, E])
        ls = sb("ls", [P, ST, E])
        b_raw = sb("b_raw", [P, ST, E])
        k3 = sb("k3", [P, ST, E])
        rf = sb("rf", [P, ST, E])
        wl = sb("wl", [P, ST, E])
        wm = sb("wm", [P, ST, E])
        ss = sb("ss", [P, ST * HEADS])
        rn = sb("rn", [P, ST * HEADS])
        rt = sb("rt", [P, ST * HEADS])
        rk = sb("rk", [P, ST * HEADS])

        ps = ctx.enter_context(nc.psum_tensor("ps_mix", [P, 8, BANK], F32))
        ps_rg, ps_kv, ps_kkk, ps_za, ps_mm = (ps[:, b, :] for b in range(5))
        pc = [ps[:, b, :].rearrange("p (c n) -> p c n", c=KC) for b in (5, 6, 7)]
        ps_lo1, ps_hb = pc[0], pc[0]
        ps_lo2 = [pc[1], pc[2], pc[0], pc[1]]
        ps_hag = pc[2]

        w_in = sem("w_in")
        mix_ready, lo1_done, lo1_act, lo2_done, xm_ready = (sem(n) for n in ("mix_ready", "lo1_done", "lo1_act", "lo2_done", "xm_ready"))
        hag_done, hag_act, hb_done, hb_act = (sem(n) for n in ("hag_done", "hag_act", "hb_done", "hb_act"))
        rg_done, kv_done, kkk_done, z_done = (sem(n) for n in ("rg_done", "kv_done", "kkk_done", "z_done"))
        rg_read, kv_read, z_read, kk_ready = (sem(n) for n in ("rg_read", "kv_read", "z_read", "kk_ready"))
        az_ready, ls_ready, wm_ready, wide_done = (sem(n) for n in ("az_ready", "ls_ready", "wm_ready", "wide_done"))
        scan_out = [sem("scan_out0"), sem("scan_out1")]
        dve_link, act_link = sem("dve_link"), sem("act_link")
        zeros = sb("zeros", [1, (ARRAYS - 1) * E])
        zero_set, tail_out, tri_set = sem("zero_set"), sem("tail_out"), sem("tri_set")
        e1_ready, cum_done, cum_read = sem("e1_ready"), sem("cum_done"), sem("cum_read")
        ps_cum = [ps[:, b, :].rearrange("p (t e) -> p t e", t=ST) for b in (6, 7)]
        STORE = 16 * 2
        block = ctx.enter_context(nc.Block())
        LOOP = SLICES // 2 - 1

        def slices(eng, first, turn, last, chain=None, links=0):
            first()
            turn(0, 0, 0, has_prev=False)
            with eng.Fori(0, LOOP) as i:
                if chain:
                    chain.enter(i, links)
                turn(2 * i + 1, i, 1)
                turn(2 * i + 2, i + 1, 0)
                if chain:
                    chain.leave(LOOP)
            turn(SLICES - 1, SLICES // 2 - 1, 1, has_next=False)
            last()

        @block.sync
        def _(sp):
            for dst, src in ((maa, "maa"), (maa_w1, "maa_w1T"), (w_a1, "w_a1T"), (w_b1, "w_b1T"), (w_g1, "w_g1T"),
                             (w_r, "w_rT"), (w_k, "w_kT"), (w_v, "w_vT")):
                sp.dma_start(dst[:], d[src].rearrange("(c p) e -> p c e", p=P)).then_inc(w_in, 16)
            for dst, src in ((maa_w2, "maa_w2"), (w_a2, "w_a2"), (a_bias, "a_bias"), (w_b2, "w_b2"), (w_g2, "w_g2")):
                sp.dma_start(dst[:], d[src]).then_inc(w_in, 16)
            sp.dma_start(faaaa[:], d["faaaa"].partition_broadcast(P)).then_inc(w_in, 16)

            sp.wait_ge(zero_set, 1)
            sp.dma_start(d["scan"][TOK:TOK + 1, ROW_A:, :].rearrange("o m e -> o (m e)"), zeros[:]).then_inc(tail_out, 16)

            def store(s, par):
                sp.wait_ge(wide_done, s + 1)
                rows = lambda first, a, b: d["scan"][first:first + TOK, a:b, :].rearrange(
                    "(s t p) m e -> s p t (m e)", p=P, t=ST)[bass.ds(s, 1)].rearrange("o p t f -> (o p) t f")
                sp.dma_start(rows(1, ROW_Q, ROW_Q + 1), scan[:, par, :, SCAN_Q, :]).then_inc(scan_out[par], 16)
                sp.dma_start(rows(0, ROW_A, ROW_V + 1), scan[:, par, :, SCAN_A:, :].rearrange("p t m e -> p t (m e)")
                             ).then_inc(scan_out[par], 16)

            with sp.Fori(0, SLICES // 2) as i:
                store(2 * i, 0)
                store(2 * i + 1, 1)
            for q in scan_out:
                sp.wait_ge(q, STORE * (SLICES // 2))
            sp.wait_ge(tail_out, 16)

        @block.gpsimd
        def _(pool):
            pool.memset(zeros[:], 0.0).then_inc(zero_set, 1)
            pool.memset(tri[:], 1.0).then_inc(tri_set, 1)
            pool.wait_ge(tri_set, 1)
            for w in range(2):
                pool.affine_select(out=tri[:, w, :], in_=tri[:, w, :], compare_op=ALU.is_ge, fill=0.0, base=-w,
                                   pattern=[[1, P]], channel_multiplier=-1).then_inc(tri_set, 1)
            pool.wait_ge(tri_set, 3)
            for w in range(2):
                pool.memset(tri[0:T, w, T:P], 0.0).then_inc(tri_set, 1)

        @block.tensor
        def _(pe):
            def cumulate(s):
                pe.wait_ge(e1_ready, s + 1)
                for w in range(2):
                    for t in range(ST):
                        last = pe.matmul(ps_cum[w][:, t, :], tri[:, w, :], wl[:, t, :], start=True, stop=True)
                last.then_inc(cum_done, 1)

            def chan(s, half, par):
                pe.wait_ge(mix_ready, s + 1)
                wait(pe, hb_act, s)
                for k in range(KC):
                    last = pe.matmul(ps_lo1[:, 0, :], maa_w1[:, k, :], mix[:, k, :], start=(k == 0), stop=(k == KC - 1))
                last.then_inc(lo1_done, 1)
                pe.wait_ge(lo1_act, s + 1)
                for g, (free, count) in enumerate(((xm_ready, 4 * s), (hag_act, s), (None, 0), (xm_ready, 4 * s + 1))):
                    if g < 2:
                        wait(pe, cum_read, s - 1)
                    if free is not None:
                        wait(pe, free, count)
                    for k in range(KC):
                        last = pe.matmul(ps_lo2[g][:, k, :], maa_w2[32 * g:32 * g + 32, k * P:(k + 1) * P],
                                         lo1[32 * g:32 * g + 32, :], start=True, stop=True)
                    last.then_inc(lo2_done, 1)
                pe.wait_ge(xm_ready, 4 * s + 2)
                for k in range(KC):
                    pe.matmul(ps_hag[:, 0, :], w_a1[:, k, :], xm[:, 1, k, :], start=(k == 0), stop=(k == KC - 1))
                for k in range(KC):
                    last = pe.matmul(ps_hag[:, 1, :], w_g1[:, k, :], xm[:, 0, k, :], start=(k == 0), stop=(k == KC - 1))
                last.then_inc(hag_done, 1)
                pe.wait_ge(xm_ready, 4 * s + 3)
                for k in range(KC):
                    last = pe.matmul(ps_hb[0:64, 0, :], w_b1[:, k, :], xm[:, 2, k, :], start=(k == 0), stop=(k == KC - 1))
                last.then_inc(hb_done, 1)

            def tiles(s):
                for t in range(ST):
                    j = ST * s + t
                    tok = slice(t * P, (t + 1) * P)
                    if t == 0:
                        pe.wait_ge(hag_act, s + 1)
                    wait(pe, rg_read, j)
                    for k in range(KC):
                        pe.matmul(ps_rg[:, 0:E], xm[:, 0, k, tok], w_r[:, k, :], start=(k == 0), stop=(k == KC - 1))
                    pe.matmul(ps_rg[:, E:2 * E], hid_g[:, tok], w_g2[:], start=True, stop=True).then_inc(rg_done, 1)
                    if t == 0:
                        pe.wait_ge(xm_ready, 4 * s + 4)
                    wait(pe, kv_read, j)
                    for k in range(KC):
                        pe.matmul(ps_kv[:, 0:E], xm[:, 2, k, tok], w_k[:, k, :], start=(k == 0), stop=(k == KC - 1))
                    for k in range(KC):
                        last = pe.matmul(ps_kv[:, E:2 * E], xm[:, 3, k, tok], w_v[:, k, :], start=(k == 0), stop=(k == KC - 1))
                    last.then_inc(kv_done, 1)
                    if t == 0:
                        pe.wait_ge(hb_act, s + 1)
                    wait(pe, kk_ready, j)
                    pe.matmul(ps_kkk[:, 0:E], hid_b[0:64, tok], w_b2[0:64, 0:E], start=True, stop=True).then_inc(kkk_done, 1)
                    wait(pe, z_read, j)
                    pe.matmul(ps_za[:, :], hid_a[:, tok], w_a2[:, 0:2 * E], start=True, stop=True)
                    pe.matmul(ps_mm[:, 0:E], hid_a[:, tok], w_a2[:, 2 * E:3 * E], start=True, stop=True)
                    pe.matmul(ps_mm[:, E:2 * E], hid_b[0:64, tok], w_b2[0:64, E:2 * E], start=True, stop=True).then_inc(z_done, 1)

            def turn(s, half, par, has_prev=True, has_next=True):
                tiles(s)
                if has_prev:
                    cumulate(s - 1)
                if has_next:
                    chan(s + 1, half + par, 1 - par)

            pe.wait_ge(w_in, 16 * 14)
            pe.wait_ge(tri_set, 5)
            slices(pe, lambda: chan(0, 0, 0), turn, lambda: cumulate(SLICES - 1))

        @block.scalar
        def _(act):
            chain = Chain(act, act_link)

            def chan(s):
                act.wait_ge(lo1_done, s + 1)
                act.activation(lo1[:], ps_lo1[:, 0, :], ACT.Tanh, bias=0.0).then_inc(lo1_act, 1)
                act.wait_ge(hag_done, s + 1)
                act.activation(hid_a[0:64, :], ps_hag[0:64, 0, :], ACT.Tanh, bias=0.0)
                act.activation(hid_a[64:128, :], ps_hag[64:128, 0, :], ACT.Identity, bias=a_bias[64:128, 0:1])
                act.activation(hid_g[:], ps_hag[:, 1, :], ACT.Tanh, bias=0.0).then_inc(hag_act, 1)
                act.wait_ge(hb_done, s + 1)
                act.activation(hid_b[0:32, :], ps_hb[0:32, 0, :], ACT.Tanh, bias=0.0)
                act.activation(hid_b[32:64, :], ps_hb[32:64, 0, :], ACT.Identity, bias=a_bias[32:64, 1:2]).then_inc(hb_act, 1)

            def tiles(s, half, par):
                wait(act, wide_done, s - 1)
                wait(act, scan_out[par], STORE * half)
                for t in range(ST):
                    j = ST * s + t
                    act.wait_ge(rg_done, j + 1)
                    act.copy(scan[:, par, t, SCAN_Q, :], ps_rg[:, 0:E])
                    act.copy(c.gate[:, bass.ds(j, 1), :].rearrange("p o e -> p (o e)"), ps_rg[:, E:2 * E]).then_inc(rg_read, 1)
                    act.wait_ge(kv_done, j + 1)
                    act.copy(k_raw[:, par, t, :], ps_kv[:, 0:E])
                    act.copy(scan[:, par, t, SCAN_V, :], ps_kv[:, E:2 * E]).then_inc(kv_read, 1)
                    act.wait_ge(z_done, j + 1)
                    act.copy(zd[:, par, t, :], ps_za[:, 0:E])
                    act.activation(a_sig[:, par, t, :], ps_za[:, E:2 * E], ACT.Sigmoid, bias=0.0)
                    act.activation(mam_k[:, par, t].rearrange("p m e -> p (m e)"), ps_mm, ACT.Sigmoid, bias=0.0).then_inc(z_read, 1)

            def sig_az(s):
                act.wait_ge(az_ready, s + 1)
                act.activation(az[:], az[:], ACT.Sigmoid, bias=0.0).then_inc(act_link, 1)

            def wide(s, par):
                chain.done += 1
                act.wait_ge(act_link, chain.turns + chain.done)
                act.activation(ls[:], az[:], ACT.Ln, bias=0.0).then_inc(ls_ready, 1)
                act.wait_ge(wm_ready, s + 1)
                act.activation(wl[:], wl[:], ACT.Exp, bias=0.0).then_inc(e1_ready, 1)
                act.activation(wm[:], wm[:], ACT.Exp, bias=0.0)
                act.wait_ge(cum_done, s + 1)
                act.activation(cum[:, 0], ps_cum[0], ACT.Exp, scale=-1.0, bias=0.0)
                act.activation(cum[:, 1], ps_cum[0], ACT.Exp, bias=0.0)
                act.activation(cum[:, 2], ps_cum[1], ACT.Exp, scale=-1.0, bias=0.0).then_inc(cum_read, 1)

            def turn(s, half, par, has_prev=True, has_next=True):
                if has_prev:
                    sig_az(s - 1)
                tiles(s, half, par)
                if has_prev:
                    wide(s - 1, 1 - par)
                if has_next:
                    chan(s + 1)

            def last():
                sig_az(SLICES - 1)
                wide(SLICES - 1, 1)

            act.wait_ge(w_in, 16 * 14)
            slices(act, lambda: chan(0), turn, last, chain, 2)

        @block.vector
        def _(dve):
            chain = Chain(dve, dve_link)
            heads = lambda ap: ap.rearrange("p t (h j) -> p t h j", j=HS)
            per_head = lambda ap: ap[:].rearrange("p (t h) -> p t h", t=ST)

            def chan(s):
                x = c.xnT[:, :, bass.ds(s * SL, SL)]
                xb = x.rearrange("p c (b t) -> p c b t", t=T)
                xxb = xx[:].rearrange("p c (b t) -> p c b t", t=T)
                for k in range(KC):
                    dve.tensor_tensor(xxb[:, k, :, 1:T], xb[:, k, :, 0:T - 1], xb[:, k, :, 1:T], ALU.subtract)
                for k in range(KC):
                    chain(dve.tensor_scalar(xxb[:, k, :, 0:1], xb[:, k, :, 0:1], -1.0, None, ALU.mult))
                wait(dve, lo1_done, s)
                for k in range(KC):
                    last = dve.scalar_tensor_tensor(out=mix[:, k, :], in0=xx[:, k, :], scalar=maa[:, k, 4:5],
                                                    in1=x[:, k, :], op0=ALU.mult, op1=ALU.add)
                last.then_inc(mix_ready, 1)
                for g in range(4):
                    dve.wait_ge(lo2_done, 4 * s + g + 1)
                    wait(dve, xm_ready, 4 * s + g)
                    for k in range(KC):
                        last = dve.scalar_tensor_tensor(out=xm_tmp[:, k, :], in0=ps_lo2[g][:, k, :], scalar=maa[:, k, g:g + 1],
                                                        in1=xx[:, k, :], op0=ALU.add, op1=ALU.mult)
                    chain(last)
                    dve.tensor_tensor(xm[:, g, :, :], xm_tmp[:], x, ALU.add).then_inc(xm_ready, 1)

            def tiles(s, par):
                for t in range(ST):
                    j = ST * s + t
                    dve.wait_ge(kkk_done, j + 1)
                    dve.wait_ge(kv_read, j + 1)
                    dve.tensor_tensor(kk[:, par, t, :], ps_kkk[:, 0:E], k_raw[:, par, t, :], ALU.add).then_inc(kk_ready, 1)

            def wide_1(s, par):
                a, ma = a_sig[:, par], mam_k[:, par, :, 0, :]
                dve.wait_ge(z_read, ST * (s + 1))
                dve.wait_ge(kk_ready, ST * (s + 1))
                dve.scalar_tensor_tensor(out=az[:], in0=zd[:, par], scalar=-1.0, in1=zd[:, par],
                                         op0=ALU.mult, op1=ALU.max).then_inc(az_ready, 1)
                dve.tensor_scalar(mn[:], zd[:, par], 0.0, None, ALU.min)
                chain(dve.tensor_tensor(t0[:], kk[:, par], kk[:, par], ALU.mult))
                chain(dve.tensor_reduce(per_head(ss), heads(t0[:]), AX_X, ALU.add))
                chain(dve.tensor_scalar(ss[:], ss[:], TINY, None, ALU.max))
                inverse_sqrt(dve, chain, rn[:], rt[:], ss[:])
                chain(dve.tensor_tensor(heads(kk[:, par]), heads(kk[:, par]),
                                        per_head(rn).unsqueeze(3).to_broadcast([P, ST, HEADS, HS]), ALU.mult))
                dve.scalar_tensor_tensor(out=b_raw[:], in0=kk[:, par], scalar=-1.0,
                                         in1=a, op0=ALU.mult, op1=ALU.mult)
                chain(dve.scalar_tensor_tensor(out=t1[:], in0=ma, scalar=1.0, in1=a, op0=ALU.subtract, op1=ALU.mult))
                chain(dve.tensor_tensor(t1[:], ma, t1[:], ALU.subtract))
                chain(dve.tensor_tensor(k2[:], k_raw[:, par], t1[:], ALU.mult))

            def wide_2(s, par):
                dve.wait_ge(ls_ready, s + 1)
                chain(dve.scalar_tensor_tensor(out=wl[:], in0=ls[:], scalar=-0.5, in1=mn[:], op0=ALU.add, op1=ALU.add))
                dve.tensor_tensor(wm[:], wl[:], mam_k[:, par, :, 1, :], ALU.mult).then_inc(wm_ready, 1)
                chain(dve.tensor_tensor(rf[:], scan[:, par, :, SCAN_Q, :],
                                        faaaa[:].unsqueeze(1).to_broadcast([P, ST, E]), ALU.mult))

            def wide_3(s, par):
                dve.wait_ge(cum_read, s + 1)
                chain(dve.tensor_tensor(k3[:], k2[:], wm[:], ALU.mult))
                chain(dve.tensor_tensor(rf[:], rf[:], k3[:], ALU.mult))
                chain(dve.tensor_reduce(per_head(rk), heads(rf[:]), AX_X, ALU.add))
                dve.tensor_tensor(scan[:, par, :, SCAN_Q, :], scan[:, par, :, SCAN_Q, :], cum[:, 0], ALU.mult)
                dve.tensor_tensor(scan[:, par, :, SCAN_K, :], k3[:], cum[:, 1], ALU.mult)
                dve.tensor_tensor(scan[:, par, :, SCAN_B, :], b_raw[:], cum[:, 1], ALU.mult)
                dve.tensor_tensor(scan[:, par, :, SCAN_A, :], kk[:, par], cum[:, 2], ALU.mult)
                dve.tensor_tensor(c.bonus[:, bass.ds(ST * s, ST), :].rearrange("p t (h j) -> p t h j", j=HS),
                                  heads(scan[:, par, :, SCAN_V, :]),
                                  per_head(rk).unsqueeze(3).to_broadcast([P, ST, HEADS, HS]), ALU.mult).then_inc(wide_done, 1)

            def turn(s, half, par, has_prev=True, has_next=True):
                if has_prev:
                    wide_1(s - 1, 1 - par)
                tiles(s, par)
                if has_prev:
                    wide_2(s - 1, 1 - par)
                if has_next:
                    chan(s + 1)
                if has_prev:
                    wide_3(s - 1, 1 - par)

            def last():
                wide_1(SLICES - 1, 1)
                wide_2(SLICES - 1, 1)
                wide_3(SLICES - 1, 1)

            dve.wait_ge(w_in, 16 * 14)
            slices(dve, lambda: chan(0), turn, last, chain,
                   2 * (2 + 4 + 3 + RSQRT_LINKS + 1 + 3 + 2 + 3))


CHUNK = 8
CHUNKS = T // CHUNK
HG = 4
GH = HEADS // HG
GC = GH * HS
HALF_I = HS // 2
LOADS = 16 * HG


def scan_stage(nc, d, c):
    with ExitStack() as ctx:
        sb = lambda name, shape: ctx.enter_context(nc.sbuf_tensor("scan_" + name, shape, F32))
        sem = lambda name: ctx.enter_context(nc.semaphore("scan_" + name))
        vec = sb("vec", [P, 2, CHUNK, ARRAYS, GC])
        prod = sb("prod", [P, 2, 2, 2, HALF_I * GC])
        outer = sb("outer", [P, 2, HALF_I * GC])
        kv = sb("kv", [P, 2, HS * GC])
        sa = sb("sa", [P, HS * GH])
        y = sb("y", [P, 2, CHUNK, GC])
        part = sb("part", [P, 3, 2, HALF_I * GH, HS // 2])
        first = sb("first", [P, 2, GC])
        ps = ctx.enter_context(nc.psum_tensor("ps_scan", [P, 2, BANK], F32))
        loaded = [sem("loaded0"), sem("loaded1")]
        stored = [sem("stored0"), sem("stored1")]
        added, o_ready, prod_ready = ([sem(f"{n}{h}") for h in range(2)] for n in ("added", "outer_ready", "prod_ready"))
        kv_ready, y_done, sa_link, outer_zero = sem("kv_ready"), sem("y_done"), sem("sa_link"), sem("outer_zero")
        blank = sb("blank", [P, NT // P * E])
        blank_set, cleared = sem("blank_set"), sem("cleared")
        first_in, part_link = sem("first_in"), sem("part_link")
        block = ctx.enter_context(nc.Block())
        TURNS = CHUNKS // 2

        rows = lambda ap, g: ap[g * B:(g + 1) * B]

        def steps(eng, step):
            with eng.Fori(0, TURNS) as i:
                for par in range(2):
                    for tau in range(CHUNK):
                        step(i * 2 * CHUNK + par * CHUNK + tau, 2 * i + par, i, par, tau)

        @block.sync
        def _(sp):
            src = d["scan"][1:TOK + 1].rearrange("(b n t) m (g e) -> n g b t m e", t=CHUNK, n=CHUNKS, g=HG)

            def load(chunk, par):
                if not isinstance(chunk, int):
                    sp.wait_ge(o_ready[1], CHUNK * (chunk - 1) + 1)
                    sp.wait_ge(kv_ready, CHUNK * (chunk - 1) + 1)
                for g in range(HG):
                    sp.dma_start(rows(vec, g)[:, par].rearrange("b t m e -> b t m e"),
                                 src[bass.ds(chunk, 1), g].rearrange("o b t m e -> (o b) t m e")).then_inc(loaded[par], 16)

            heads_0 = d["scan"][0:TOK].rearrange("(b t) m (g e) -> t g b m e", t=T, g=HG)
            for g in range(HG):
                sp.dma_start(rows(first, g), heads_0[0, g, :, ROW_K:ROW_V + 1, :]).then_inc(first_in, 16)
            load(0, 0)
            load(1, 1)
            with sp.Fori(1, TURNS) as i:
                load(2 * i, 0)
                load(2 * i + 1, 1)

        @block.scalar
        def _(act):
            act.wait_ge(blank_set, 1)
            for j in range(TURNS_X):
                act.dma_start(d["x_slots"][j * NT:(j + 1) * NT].rearrange("(t p) e -> p (t e)", t=1, p=P) if False else d["x_slots"][j * NT:(j + 1) * NT].rearrange("(p t) e -> p (t e)", p=P), blank[:]).then_inc(cleared, 16)
            dst = d["y"].rearrange("(b n t) (g e) -> n g b t e", t=CHUNK, n=CHUNKS, g=HG)
            with act.Fori(0, TURNS) as i:
                for par in range(2):
                    act.wait_ge(y_done, CHUNK * (2 * i + par + 1) + 1)
                    for g in range(HG):
                        act.dma_start(dst[bass.ds(2 * i + par, 1), g].rearrange("o b t e -> (o b) t e"),
                                      rows(y, g)[:, par]).then_inc(stored[par], 16)
            for q in stored:
                act.wait_ge(q, LOADS * TURNS)
            act.wait_ge(cleared, 16 * TURNS_X)

        @block.gpsimd
        def _(pool):
            pool.memset(outer[:], 0.0).then_inc(outer_zero, 1)
            pool.memset(blank[:], 0.0).then_inc(blank_set, 1)
            pool.memset(y[:], 0.0).then_inc(y_done, 1)

            def v_outer_k(slot, k, v):
                v = v.rearrange("p (h i) -> p i h", i=HS).unsqueeze(3).to_broadcast([P, HS, GH, HS])
                k = k.rearrange("p (h j) -> p h j", j=HS).unsqueeze(1).to_broadcast([P, HS, GH, HS])
                pool.tensor_tensor(kv[:, slot, :].rearrange("p (i h j) -> p i h j", i=HS, h=GH), v, k,
                                   ALU.mult).then_inc(kv_ready, 1)

            def sum_y(t, half, par, tau):
                pool.wait_ge(prod_ready[1], t + 1)
                if tau == 0:
                    wait(pool, stored[par], LOADS * half)
                src = prod[:, tau % 2, :, 0, :].rearrange("p s (r j) -> p s r j", j=HS)
                n = HS // 2
                for level in range(3):
                    dst = part[:, level, :, :, 0:n]
                    pool.tensor_tensor(dst, src[:, :, :, 0:n], src[:, :, :, n:2 * n], ALU.add).then_inc(part_link, 1)
                    pool.wait_ge(part_link, 3 * t + level + 1)
                    src, n = dst, n // 2
                terms = src.rearrange("p s (i h) j -> p (s i) h j", h=GH)
                pool.tensor_tensor(y[:, par, tau, :].rearrange("p (h i) -> p i h", i=HS), terms[:, :, :, 0],
                                   terms[:, :, :, 1], ALU.add).then_inc(y_done, 1)

            def step(t, chunk, half, par, tau):
                if tau == 0:
                    pool.wait_ge(loaded[par], LOADS * (half + 1))
                pool.wait_ge(added[1], t + 1)
                v_outer_k((tau + 1) % 2, vec[:, par, tau, ROW_K, :], vec[:, par, tau, ROW_V, :])
                sum_y(t, half, par, tau)

            pool.wait_ge(first_in, LOADS)
            v_outer_k(0, first[:, 0, :], first[:, 1, :])
            steps(pool, step)

        @block.tensor
        def _(pe):
            pe.wait_ge(outer_zero, 1)
            for h in range(2):
                pe.matmul(ps[:, h, :], c.ident[:], outer[:, h, :], start=True, stop=True).then_inc(added[h], 1)

            def step(t, chunk, half, par, tau):
                pe.wait_ge(kv_ready, t + 1)
                for h in range(2):
                    wait(pe, prod_ready[h], t)
                    pe.matmul(ps[:, h, :], c.ident[:], kv[:, tau % 2, h * BANK:(h + 1) * BANK], start=False, stop=False,
                              skip_group_check=True)
                    pe.wait_ge(o_ready[h], t + 1)
                    pe.matmul(ps[:, h, :], c.ident[:], outer[:, h, :], start=False, stop=True,
                              skip_group_check=True).then_inc(added[h], 1)

            steps(pe, step)

        @block.vector
        def _(dve):
            def outer_u_b(h, vec_b):
                shape = [P, HALF_I, GH, HS]
                u = sa[:, h * HALF_I * GH:(h + 1) * HALF_I * GH].rearrange("p (i h) -> p i h", h=GH)
                b = vec_b.rearrange("p (h j) -> p h j", j=HS)
                dve.tensor_tensor(outer[:, h, :].rearrange("p (i h j) -> p i h j", h=GH, j=HS),
                                  u.unsqueeze(3).to_broadcast(shape), b.unsqueeze(1).to_broadcast(shape),
                                  ALU.mult).then_inc(o_ready[h], 1)

            for h in range(2):
                dve.wait_ge(outer_zero, 1)
                dve.wait_ge(added[h], 1)
                dve.memset(outer[:, h, :], 0.0).then_inc(o_ready[h], 1)

            def step(t, chunk, half, par, tau):
                for h in range(2):
                    dve.wait_ge(added[h], t + 2)
                    if tau == 0 and h == 0:
                        dve.wait_ge(loaded[par], LOADS * (half + 1))
                    dve.wait_ge(y_done, t)
                    pr = prod[:, tau % 2, h, :, :]
                    vecs = vec[:, par, tau, ROW_Q:ROW_A + 1, :].unsqueeze(2).to_broadcast([P, 2, HALF_I, GC])
                    state = ps[:, h, :].rearrange("p (i e) -> p i e", e=GC).unsqueeze(1).to_broadcast([P, 2, HALF_I, GC])
                    dve.tensor_tensor(pr.rearrange("p m (i e) -> p m i e", e=GC), state, vecs, ALU.mult).then_inc(prod_ready[h], 1)
                    dve.wait_ge(prod_ready[h], t + 1)
                    dve.tensor_reduce(sa[:, h * HALF_I * GH:(h + 1) * HALF_I * GH],
                                      pr[:, 1, :].rearrange("p (r j) -> p r j", j=HS), AX_X, ALU.add).then_inc(sa_link, 1)
                    dve.wait_ge(sa_link, 2 * t + h + 1)
                    outer_u_b(h, vec[:, par, tau, ROW_B, :])

            steps(dve, step)


GROUP = 2
GROUPS = TILES // GROUP
GN_EPS = 0.00064
EXPERTS, FF = 8, 1024
FC = FF // P
JITTER = 0.01
NT = 256
TURNS_X = (2 * TOK - EXPERTS) // NT + EXPERTS
U32 = mybir.dt.uint32
I32 = mybir.dt.int32


def out_stage(nc, d, c):
    with ExitStack() as ctx:
        sb = lambda name, shape, dt=F32: ctx.enter_context(nc.sbuf_tensor("out_" + name, shape, dt))
        sem = lambda name: ctx.enter_context(nc.semaphore("out_" + name))
        y = sb("y", [P, TILES, E])
        sq = sb("sq", [P, GROUP, E])
        h_new = sb("h_new", [P, GROUP, E])
        gated = sb("gated", [P, GROUP, E])
        ln_w, ln_b = sb("ln_w", [P, E]), sb("ln_b", [P, E])
        w_o = sb("w_o", [P, KC, E])
        gate_w = sb("gate_w", [P, KC, EXPERTS])
        NG = GROUP * HEADS
        g_sum, g_mean, g_var, g_rstd, g_tmp = (sb(n, [P, NG]) for n in ("g_sum", "g_mean", "g_var", "g_rstd", "g_tmp"))
        ygT = sb("ygT", [P, GROUP, KC, P])
        xn = sb("xn", [P, GROUP, E])
        xT = sb("xT", [P, GROUP, KC, P])
        stats = sb("stats", [P, GROUP, 6])
        mean_var = sb("mean_var", [P, GROUP, 2])
        var_eps, rstd, nwt = (sb(n, [P, GROUP]) for n in ("var_eps", "rstd", "nwt"))
        logits = sb("logits", [P, TILES, EXPERTS])
        top = sb("top", [P, TILES, 8])
        top_i = sb("top_i", [P, TILES, 8], mybir.dt.uint32)
        top_f = sb("top_f", [P, TILES, 2])
        expert_no = sb("expert_no", [P, EXPERTS])
        expert_ni = sb("expert_ni", [P, EXPERTS], mybir.dt.int32)
        hot = [sb("hot0", [P, TILES, EXPERTS]), sb("hot1", [P, TILES, EXPERTS])]
        absl, dif, fac, keep, ex = (sb(n, [P, TILES, EXPERTS]) for n in ("absl", "dif", "fac", "keep", "ex"))
        den = sb("den", [P, TILES])
        chosen, rank = sb("chosen", [P, TILES, EXPERTS]), sb("rank", [P, TILES, EXPERTS])
        before = [sb("before0", [P, TILES, EXPERTS]), sb("before1", [P, TILES, EXPERTS])]
        n_i = sb("n_i", [P, EXPERTS], I32)
        turns_of, start, base = (sb(n, [P, EXPERTS]) for n in ("turns_of", "start", "base"))
        le = sb("le", [P, TURNS_X, EXPERTS])
        te, turn_no = sb("te", [P, TURNS_X]), sb("turn_no", [P, TURNS_X])
        turn_ni = sb("turn_ni", [P, TURNS_X], I32)
        tri = sb("tri", [P, P])
        ones = sb("ones", [P, P])
        ps = ctx.enter_context(nc.psum_tensor("ps_out", [P, 5, BANK], F32))
        ps_t = ps[:, 0, :].rearrange("p (t k n) -> p t k n", t=GROUP, k=KC)
        ps_o = ps[:, 1, :].rearrange("p (t e) -> p t e", t=GROUP)
        ps_x = ps[:, 2, :].rearrange("p (t k n) -> p t k n", t=GROUP, k=KC)
        ps_l = ps[:, 3, 0:TILES * EXPERTS].rearrange("p (t x) -> p t x", t=TILES)
        ps_rank, ps_count = (ps[:, 4, w * TILES * EXPERTS:(w + 1) * TILES * EXPERTS].rearrange("p (t x) -> p t x", t=TILES)
                             for w in range(2))
        chosen_ready, ranks_done, tri_set = sem("chosen_ready"), sem("ranks_done"), sem("tri_set")
        w_in, y_in = sem("w_in"), sem("y_in")
        yg_ready, t_done, t_copied, o_done, o_read = (sem(n) for n in ("yg_ready", "t_done", "t_copied", "o_done", "o_read"))
        xn_ready, x_done, x_copied, l_done, no_set = (sem(n) for n in ("xn_ready", "x_done", "x_copied", "l_done", "no_set"))
        dve_link, e_asked, e_ready = sem("dve_link"), sem("exp_asked"), sem("exp_ready")
        block = ctx.enter_context(nc.Block())

        @block.sync
        def _(sp):
            sp.dma_start(y[:], d["y"].rearrange("(t p) e -> p t e", p=P)).then_inc(y_in, 16)
            sp.dma_start(ln_w[:], d["ln_w"].partition_broadcast(P)).then_inc(w_in, 16)
            sp.dma_start(ln_b[:], d["ln_b"].partition_broadcast(P)).then_inc(w_in, 16)
            sp.dma_start(w_o[:], d["w_oT"].rearrange("(c p) e -> p c e", p=P)).then_inc(w_in, 16)
            sp.dma_start(gate_w[:], d["gate_w"].rearrange("(c p) e -> p c e", p=P)).then_inc(w_in, 16)

        @block.gpsimd
        def _(pool):
            pool.iota(expert_ni[:], pattern=[[1, EXPERTS]], base=0, channel_multiplier=0).then_inc(no_set, 1)
            pool.wait_ge(no_set, 1)
            pool.tensor_copy(expert_no[:], expert_ni[:]).then_inc(no_set, 1)
            pool.iota(turn_ni[:], pattern=[[1, TURNS_X]], base=0, channel_multiplier=0).then_inc(no_set, 1)
            pool.wait_ge(no_set, 3)
            pool.tensor_copy(turn_no[:], turn_ni[:]).then_inc(no_set, 1)
            pool.memset(ones[:], 1.0).then_inc(tri_set, 1)
            pool.memset(tri[:], 1.0).then_inc(tri_set, 1)
            pool.wait_ge(tri_set, 2)
            pool.affine_select(out=tri[:], in_=tri[:], compare_op=ALU.is_ge, fill=0.0, base=-1,
                               pattern=[[1, P]], channel_multiplier=-1).then_inc(tri_set, 1)

        @block.tensor
        def _(pe):
            def project(g):
                pe.wait_ge(yg_ready, g + 1)
                wait(pe, t_copied, g)
                for t in range(GROUP):
                    for k in range(KC):
                        last = pe.transpose(ps_t[:, t, k, :], gated[:, t, k * P:(k + 1) * P], c.ident[:])
                last.then_inc(t_done, 1)
                pe.wait_ge(t_copied, g + 1)
                wait(pe, o_read, g)
                for t in range(GROUP):
                    for k in range(KC):
                        last = pe.matmul(ps_o[:, t, :], ygT[:, t, k, :], w_o[:, k, :], start=(k == 0), stop=(k == KC - 1))
                last.then_inc(o_done, 1)

            def gate(g):
                pe.wait_ge(xn_ready, g + 1)
                wait(pe, x_copied, g)
                for t in range(GROUP):
                    for k in range(KC):
                        last = pe.transpose(ps_x[:, t, k, :], xn[:, t, k * P:(k + 1) * P], c.ident[:])
                last.then_inc(x_done, 1)
                pe.wait_ge(x_copied, g + 1)
                for t in range(GROUP):
                    for k in range(KC):
                        last = pe.matmul(ps_l[:, bass.ds(g * GROUP + t, 1), :].rearrange("p o x -> p (o x)"),
                                         xT[:, t, k, :], gate_w[:, k, :], start=(k == 0), stop=(k == KC - 1))
                last.then_inc(l_done, 1)

            pe.wait_ge(w_in, 64)
            project(0)
            with pe.Fori(0, GROUPS - 1) as i:
                project(i + 1)
                gate(i)
            gate(GROUPS - 1)
            pe.wait_ge(tri_set, 3)
            pe.wait_ge(chosen_ready, 1)
            flat = chosen[:].rearrange("p t x -> p (t x)")
            pe.matmul(ps_rank.rearrange("p t x -> p (t x)"), tri[:], flat, start=True, stop=True)
            pe.matmul(ps_count.rearrange("p t x -> p (t x)"), ones[:], flat, start=True, stop=True).then_inc(ranks_done, 1)

        @block.scalar
        def _(act):
            def copy_t(g):
                act.wait_ge(t_done, g + 1)
                wait(act, o_done, g)
                act.copy(ygT[:], ps_t).then_inc(t_copied, 1)

            def copy_x(g):
                act.wait_ge(x_done, g + 1)
                wait(act, l_done, g)
                act.copy(xT[:], ps_x).then_inc(x_copied, 1)

            copy_t(0)
            with act.Fori(0, GROUPS - 1) as i:
                copy_t(i + 1)
                copy_x(i)
            copy_x(GROUPS - 1)
            for w in range(2):
                act.wait_ge(e_asked, w + 1)
                act.activation(ex[:], ex[:], ACT.Exp, bias=0.0).then_inc(e_ready, 1)

        @block.vector
        def _(dve):
            chain = Chain(dve, dve_link)
            heads = lambda ap: ap.rearrange("p t (h j) -> p t h j", j=HS)
            per_head = lambda ap: ap[:].rearrange("p (t h) -> p t h", t=GROUP)
            spread = lambda ap: per_head(ap).unsqueeze(3).to_broadcast([P, GROUP, HEADS, HS])
            tiled = lambda ap: ap[:].unsqueeze(1).to_broadcast([P, GROUP, E])

            def norm_y(g):
                at = bass.ds(g * GROUP, GROUP)
                yg = y[:, at, :]
                chain(dve.tensor_reduce(per_head(g_sum), heads(yg), AX_X, ALU.add))
                chain(dve.tensor_scalar(g_mean[:], g_sum[:], 1.0 / HS, None, ALU.mult))
                chain(dve.tensor_tensor(heads(yg), heads(yg), spread(g_mean), ALU.subtract))
                chain(dve.tensor_tensor(sq[:], yg, yg, ALU.mult))
                chain(dve.tensor_reduce(per_head(g_var), heads(sq[:]), AX_X, ALU.add))
                chain(dve.tensor_scalar(g_var[:], g_var[:], 1.0 / HS, GN_EPS, ALU.mult, ALU.add))
                inverse_sqrt(dve, chain, g_rstd[:], g_tmp[:], g_var[:])
                chain(dve.tensor_tensor(heads(yg), heads(yg), spread(g_rstd), ALU.mult))
                chain(dve.tensor_tensor(yg, yg, tiled(ln_w), ALU.mult))
                chain(dve.tensor_tensor(yg, yg, tiled(ln_b), ALU.add))
                chain(dve.tensor_tensor(yg, yg, c.bonus[:, at, :], ALU.add))
                wait(dve, t_done, g)
                dve.tensor_tensor(gated[:], yg, c.gate[:, at, :], ALU.mult).then_inc(yg_ready, 1)

            def add_norm(g):
                h = c.h[:, bass.ds(g * GROUP, GROUP), :]
                dve.wait_ge(o_done, g + 1)
                chain(dve.tensor_tensor(h_new[:], h, ps_o, ALU.add))
                dve.tensor_tensor(h, h, ps_o, ALU.add).then_inc(o_read, 1)
                for t in range(GROUP):
                    last = dve.bn_stats(stats[:, t, :], h_new[:, t, :])
                chain(last)
                touch(dve, nwt)
                for t in range(GROUP):
                    last = dve.bn_aggr(mean_var[:, t, :], stats[:, t, :])
                chain(last)
                chain(dve.tensor_scalar(var_eps[:], mean_var[:, :, 1], LN_EPS, None, ALU.add))
                inverse_sqrt(dve, chain, rstd[:], nwt[:], var_eps[:])
                wait(dve, x_done, g)
                for t in range(GROUP):
                    last = dve.tensor_scalar(xn[:, t, :], h_new[:, t, :], mean_var[:, t, 0:1], rstd[:, t:t + 1],
                                             ALU.subtract, ALU.mult)
                last.then_inc(xn_ready, 1)
                for t in range(GROUP):
                    dve.tensor_scalar(c.xn[:, bass.ds(g * GROUP + t, 1), :].rearrange("p o e -> p (o e)"), h_new[:, t, :],
                                      mean_var[:, t, 0:1], rstd[:, t:t + 1], ALU.subtract, ALU.mult)
                chain(dve.memset(nwt[:], 0.0))

            dve.wait_ge(w_in, 64)
            dve.wait_ge(y_in, 16)
            norm_y(0)
            links = 6 + RSQRT_LINKS + 4 + 5 + RSQRT_LINKS
            with dve.Fori(0, GROUPS - 1) as i:
                chain.enter(i, links)
                norm_y(i + 1)
                add_norm(i)
                chain.leave(GROUPS - 1)
            add_norm(GROUPS - 1)

            dve.wait_ge(l_done, GROUPS)
            chain(dve.tensor_copy(logits[:], ps_l))
            for t in range(TILES):
                last = dve.max(top[:, t, :], logits[:, t, :])
            chain(last)
            for t in range(TILES):
                last = dve.max_index(top_i[:, t, :], top[:, t, :], logits[:, t, :])
            chain(last)
            dve.wait_ge(no_set, 4)
            chain(dve.tensor_copy(top_f[:], top_i[:, :, 0:2]))
            all_x = lambda ap: ap.to_broadcast([P, TILES, EXPERTS])
            for w in range(2):
                chain(dve.tensor_tensor(hot[w][:], expert_no[:].unsqueeze(1).to_broadcast([P, TILES, EXPERTS]),
                                        all_x(top_f[:, :, w:w + 1]), ALU.is_equal))
            chain(dve.scalar_tensor_tensor(out=absl[:], in0=logits[:], scalar=-1.0, in1=logits[:], op0=ALU.mult, op1=ALU.max))
            for w in range(2):
                thr = all_x(top[:, :, w:w + 1])
                chain(dve.tensor_tensor(dif[:], logits[:], thr, ALU.subtract))
                dve.tensor_scalar(ex[:], dif[:], 0.0, None, ALU.min).then_inc(e_asked, 1)
                chain(dve.tensor_tensor(fac[:], absl[:], thr, ALU.max))
                chain(dve.reciprocal(fac[:], fac[:]))
                chain(dve.tensor_tensor(keep[:], dif[:], fac[:], ALU.mult))
                chain(dve.tensor_scalar(keep[:], keep[:], -2.0 * JITTER, None, ALU.is_lt))
                chain(dve.tensor_scalar(keep[:], keep[:], -1.0, 1.0, ALU.mult, ALU.add))
                if w == 1:
                    chain(dve.tensor_scalar(dif[:], hot[0][:], -1.0, 1.0, ALU.mult, ALU.add))
                    chain(dve.tensor_tensor(keep[:], keep[:], dif[:], ALU.mult))
                dve.wait_ge(e_ready, w + 1)
                chain(dve.tensor_tensor(keep[:], keep[:], ex[:], ALU.mult))
                chain(dve.tensor_reduce(den[:], keep[:], AX_X, ALU.add))
                chain(dve.reciprocal(c.weight[:, w, :], den[:]))

            chain(dve.tensor_tensor(chosen[:], hot[0][:], hot[1][:], ALU.add))
            dve.tensor_copy(absl[:], chosen[:]).then_inc(chosen_ready, 1)
            dve.wait_ge(ranks_done, 1)
            chain(dve.tensor_copy(rank[:], ps_rank))
            chain(dve.tensor_copy(before[0][:], ps_count))
            src = 0
            for step in (1, 2, 4, 8):
                a, b = before[src], before[1 - src]
                dve.tensor_copy(b[:, 0:step, :], a[:, 0:step, :])
                chain(dve.tensor_tensor(b[:, step:, :], a[:, step:, :], a[:, 0:TILES - step, :], ALU.add))
                src = 1 - src
            total = before[src]
            chain(dve.tensor_tensor(rank[:, 1:, :], rank[:, 1:, :], total[:, 0:TILES - 1, :], ALU.add))
            chain(dve.tensor_scalar(n_i[:], total[:, TILES - 1, :], float(NT - 1), None, ALU.add))
            chain(dve.tensor_scalar(n_i[:], n_i[:], NT.bit_length() - 1, None, ALU.logical_shift_right))
            chain(dve.tensor_copy(turns_of[:], n_i[:]))
            chain(dve.memset(start[:, 0:1], 0.0))
            for x in range(1, EXPERTS):
                chain(dve.tensor_tensor(start[:, x:x + 1], start[:, x - 1:x], turns_of[:, x - 1:x], ALU.add))
            chain(dve.tensor_scalar(base[:], start[:], float(NT), None, ALU.mult))
            chain(dve.tensor_tensor(rank[:], rank[:], base[:].unsqueeze(1).to_broadcast([P, TILES, EXPERTS]), ALU.add))
            for w in range(2):
                chain(dve.tensor_tensor(keep[:], rank[:], hot[w][:], ALU.mult))
                chain(dve.tensor_reduce(den[:], keep[:], AX_X, ALU.add))
                chain(dve.tensor_copy(c.slot[:, w, :], den[:]))
            chain(dve.tensor_tensor(le[:], start[:].unsqueeze(1).to_broadcast([P, TURNS_X, EXPERTS]),
                                    turn_no[:].unsqueeze(2).to_broadcast([P, TURNS_X, EXPERTS]), ALU.is_le))
            chain(dve.tensor_reduce(te[:], le[:], AX_X, ALU.add))
            chain(dve.tensor_scalar(te[:], te[:], -1.0, None, ALU.add))
            chain(dve.tensor_copy(c.turn_expert[:], te[:]))


def ffn_stage(nc, d, c, out):
    with ExitStack() as ctx:
        sb = lambda name, shape, dt=F32: ctx.enter_context(nc.sbuf_tensor("ffn_" + name, shape, dt))
        sem = lambda name: ctx.enter_context(nc.semaphore("ffn_" + name))
        w1, w3 = sb("w1", [P, 2, KC, FF]), sb("w3", [P, 2, KC, FF])
        w2 = sb("w2", [P, 2, FC, E])
        TT = NT // P
        x_in = sb("x_in", [P, 2, TT, E])
        xT = sb("xT", [P, 2, KC, NT])
        silu = sb("silu", [P, 2, NT])
        hid = sb("hid", [P, FC, NT])
        y_out = sb("y_out", [P, 2, TT, E])
        RING = 4
        got = sb("got", [P, RING, 2, E])
        R = 4
        ps = ctx.enter_context(nc.psum_tensor("ps_ffn", [P, R + 2, BANK], F32))
        ps_y = ps[:, R, :].rearrange("p (t e) -> p t e", t=TT)
        ps_t = ps[:, R + 1, :].rearrange("p (k n) -> p k n", k=KC)
        w_in = [sem("w_in0"), sem("w_in1")]
        x_loaded = [sem("x_loaded0"), sem("x_loaded1")]
        y_stored = [sem("y_stored0"), sem("y_stored1")]
        gathered = [sem(f"gathered{r}") for r in range(RING)]
        scattered, xt_done, xt_copied, up_done, silu_done, hid_ready, down_done, y_ready, summed, stored = (sem(n) for n in (
            "scattered", "xt_done", "xt_copied", "up_done", "silu_done", "hid_ready", "down_done", "y_ready", "summed", "stored"))
        dve_link = sem("dve_link")
        block = ctx.enter_context(nc.Block())
        xs, ys = d["x_slots"], d["y_slots"]
        EVEN = TURNS_X // 2

        def turns(eng, step):
            with eng.Fori(0, EVEN) as i:
                step(2 * i, i, 0)
                step(2 * i + 1, i, 1)
            for j in range(2 * EVEN, TURNS_X):
                step(j, j // 2, j % 2)

        @block.sync
        def _(sp):
            def weights(j, par):
                wait(sp, down_done, j - 1)
                x = sp.value_load(c.turn_expert[0:1, bass.ds(j, 1)], min_val=0, max_val=EXPERTS - 1)
                at = bass.ds(x, 1)
                sp.dma_start(w1[:, par], d["w1"][at].rearrange("o (k p) f -> p (o k) f", p=P)).then_inc(w_in[par], 16)
                sp.dma_start(w3[:, par], d["w3"][at].rearrange("o (k p) f -> p (o k) f", p=P)).then_inc(w_in[par], 16)
                sp.dma_start(w2[:, par], d["w2"][at].rearrange("o (k p) f -> p (o k) f", p=P)).then_inc(w_in[par], 16)

            def rows(j, par):
                wait(sp, xt_done, j - 1)
                sp.dma_start(x_in[:, par], xs[bass.ds(j * NT, NT)].rearrange("(t p) e -> p t e", p=P)).then_inc(x_loaded[par], 16)

            for j in range(2):
                weights(j, j)
            sp.wait_ge(scattered, 16 * 2 * TILES)
            for j in range(2):
                rows(j, j)
            with sp.Fori(1, EVEN) as i:
                for par in range(2):
                    rows(2 * i + par, par)
                    weights(2 * i + par, par)
            for j in range(2 * EVEN, TURNS_X):
                rows(j, j % 2)
                weights(j, j % 2)
            for t in range(TILES):
                sp.wait_ge(summed, t + 1)
                sp.dma_start(out[:, t, :], c.h[:, t, :]).then_inc(stored, 16)
            sp.wait_ge(stored, 16 * TILES)

        @block.gpsimd
        def _(pool):
            for t in range(TILES):
                for w in range(2):
                    pool.indirect_dma_start(xs, bass.IndirectOffsetOnAxis(ap=c.slot[:, w, t:t + 1], axis=0),
                                            c.xn[:, t, :], None).then_inc(scattered, 16)
            for par in range(2):
                pool.wait_ge(y_stored[par], 16 * ((TURNS_X + 1 - par) // 2))
            for t in range(TILES):
                if t >= RING:
                    pool.wait_ge(summed, t - RING + 1)
                for w in range(2):
                    pool.indirect_dma_start(got[:, t % RING, w, :], None, ys,
                                            bass.IndirectOffsetOnAxis(ap=c.slot[:, w, t:t + 1], axis=0)
                                            ).then_inc(gathered[t % RING], 16)

        @block.tensor
        def _(pe):
            def transposes(j, half, par):
                pe.wait_ge(x_loaded[par], 16 * (half + 1))
                wait(pe, xt_copied, j)
                for k in range(KC):
                    for t in range(TT):
                        last = pe.transpose(ps_t[:, k, t * P:(t + 1) * P], x_in[:, par, t, k * P:(k + 1) * P], c.ident[:])
                last.then_inc(xt_done, 1)

            def step(j, half, par, last_turn=False):
                pe.wait_ge(w_in[par], 48 * (half + 1))
                pe.wait_ge(xt_copied, j + 1)
                for f in range(FC):
                    if f >= R:
                        pe.wait_ge(hid_ready, j * FC + f - R + 1)
                    for m, w in enumerate((w1, w3)):
                        for k in range(KC):
                            last = pe.matmul(ps[:, f % R, m * NT:(m + 1) * NT], w[:, par, k, f * P:(f + 1) * P],
                                             xT[:, par, k, :], start=(k == 0), stop=(k == KC - 1))
                    last.then_inc(up_done, 1)
                if not (isinstance(j, int) and j == TURNS_X - 1):
                    transposes(j + 1, half + par, 1 - par)
                pe.wait_ge(hid_ready, (j + 1) * FC)
                wait(pe, y_ready, j)
                for t in range(TT):
                    for f in range(FC):
                        last = pe.matmul(ps_y[:, t, :], hid[:, f, t * P:(t + 1) * P], w2[:, par, f, :],
                                         start=(f == 0), stop=(f == FC - 1))
                last.then_inc(down_done, 1)

            transposes(0, 0, 0)
            turns(pe, step)

        @block.scalar
        def _(act):
            def copy_x(j, par):
                act.wait_ge(xt_done, j + 1)
                wait(act, up_done, (j - 1) * FC)
                act.copy(xT[:, par], ps_t).then_inc(xt_copied, 1)

            def step(j, half, par):
                for f in range(FC):
                    act.wait_ge(up_done, j * FC + f + 1)
                    wait(act, hid_ready, j * FC + f - 1 if isinstance(j, int) or f >= 2 else j * FC)
                    act.activation(silu[:, f % 2, :], ps[:, f % R, 0:NT], ACT.Silu, bias=0.0).then_inc(silu_done, 1)
                if not (isinstance(j, int) and j == TURNS_X - 1):
                    copy_x(j + 1, 1 - par)
                act.wait_ge(y_ready, j + 1)
                act.dma_start(ys[bass.ds(j * NT, NT)].rearrange("(t p) e -> p t e", p=P), y_out[:, par]).then_inc(y_stored[par], 16)

            copy_x(0, 0)
            turns(act, step)

        @block.vector
        def _(dve):
            def step(j, half, par):
                for f in range(FC):
                    dve.wait_ge(silu_done, j * FC + f + 1)
                    if f == 0:
                        wait(dve, down_done, j)
                    dve.tensor_tensor(hid[:, f, :], ps[:, f % R, NT:2 * NT], silu[:, f % 2, :], ALU.mult).then_inc(hid_ready, 1)
                dve.wait_ge(down_done, j + 1)
                wait(dve, y_stored[par], 16 * half)
                dve.tensor_copy(y_out[:, par], ps_y).then_inc(y_ready, 1)

            turns(dve, step)
            chain = Chain(dve, dve_link)
            for t in range(TILES):
                dve.wait_ge(gathered[t % RING], 32 * (t // RING + 1))
                for w in range(2):
                    ins = dve.scalar_tensor_tensor(out=c.h[:, t, :], in0=got[:, t % RING, w, :], scalar=c.weight[:, w, t:t + 1],
                                                   in1=c.h[:, t, :], op0=ALU.mult, op1=ALU.add)
                    if w == 0:
                        chain(ins)
                ins.then_inc(summed, 1)


class Kept:
    pass


def audio_tower(nc, d):
    with ExitStack() as ctx:
        c = Kept()
        c.ident = ctx.enter_context(nc.sbuf_tensor("ident", [P, P], F32))
        c.h = ctx.enter_context(nc.sbuf_tensor("h", [P, TILES, E], F32))
        c.xnT = ctx.enter_context(nc.sbuf_tensor("xnT", [P, KC, TOK], F32))
        tok_stage(nc, d, c)
        d["scan"] = nc.dram_tensor("scan_rows", [TOK + 1, ARRAYS, E], F32, kind="Internal").ap()
        d["y"] = nc.dram_tensor("y_rows", [TOK, E], F32, kind="Internal").ap()
        c.gate = ctx.enter_context(nc.sbuf_tensor("gate", [P, TILES, E], F32))
        c.bonus = ctx.enter_context(nc.sbuf_tensor("bonus", [P, TILES, E], F32))
        d["x_slots"] = nc.dram_tensor("x_slots", [TURNS_X * NT, E], F32, kind="Internal").ap()
        d["y_slots"] = nc.dram_tensor("y_slots", [TURNS_X * NT, E], F32, kind="Internal").ap()
        mix_stage(nc, d, c)
        scan_stage(nc, d, c)
        c.xn = ctx.enter_context(nc.sbuf_tensor("xn", [P, TILES, E], F32))
        c.weight = ctx.enter_context(nc.sbuf_tensor("weight", [P, 2, TILES], F32))
        c.slot = ctx.enter_context(nc.sbuf_tensor("slot", [P, 2, TILES], U32))
        c.turn_expert = ctx.enter_context(nc.sbuf_tensor("turn_expert", [P, TURNS_X], I32))
        out_stage(nc, d, c)
        ffn_stage(nc, d, c, d["out"].rearrange("(s b) t e -> (b t) s e", b=2))


def layout(i):
    g = lambda n: np.asarray(i[n])
    t = lambda a: np.ascontiguousarray(np.swapaxes(a, -1, -2))
    z = lambda *s: np.zeros(s, np.float32)
    tok, att, ffn = "L0_tok_", "L0_attn_", "L0_ffn_"
    a = lambda n: g(att + n)
    w_a1T = np.concatenate([t(a("decay_w1")), t(a("aaa_w1")), z(256, 16), t(a("ma_w1")), z(256, 16)], 1)
    w_a2 = np.concatenate([
        np.concatenate([a("decay_w2"), z(64, 512)], 1),
        np.concatenate([z(16, 256), a("aaa_w2"), z(16, 256)], 1), z(16, 768),
        np.concatenate([z(16, 512), a("ma_w2")], 1),
        np.concatenate([a("time_decay"), a("time_aaaaa"), a("time_misc_a")])[None], z(15, 768)], 0)
    w_b1T = np.concatenate([t(a("kkk_w1")), z(256, 16), t(a("mk_w1")), z(256, 16)], 1)
    w_b2 = np.concatenate([
        np.concatenate([a("kkk_w2"), z(16, 256)], 1), z(16, 512),
        np.concatenate([z(16, 256), a("mk_w2")], 1),
        np.concatenate([z(256), a("time_misc_k")])[None], z(15, 512)], 0)
    ones = z(128, 2)
    ones[112, 0] = 1.0
    ones[48, 1] = 1.0
    maa = np.concatenate([t(a("time_maa").reshape(4, 256)), a("time_maa_x")[:, None]], 1)
    c = np.ascontiguousarray
    return {
        "x": g("x"), "xT": t(g("x")), "wqT": t(g(tok + "Wq")), "wkT": t(g(tok + "Wk")), "wv": g(tok + "Wv"),
        "gamma": g(tok + "gamma"), "beta": g(tok + "beta"),
        "maa": c(maa), "maa_w1T": t(a("maa_w1")), "maa_w2": a("maa_w2").reshape(128, 256),
        "w_rT": t(a("Wr")), "w_kT": t(a("Wk")), "w_vT": t(a("Wv")), "w_oT": t(a("Wo")),
        "w_a1T": c(w_a1T), "w_a2": c(w_a2), "w_b1T": c(w_b1T), "w_b2": c(w_b2), "a_bias": ones,
        "w_g1T": t(a("gate_w1")), "w_g2": a("gate_w2"), "faaaa": a("time_faaaa"),
        "ln_w": a("ln_w"), "ln_b": a("ln_b"),
        "gate_w": g(ffn + "gate_w"), "w1": g(ffn + "w1"), "w2": g(ffn + "w2"), "w3": g(ffn + "w3"),
    }


def kernel(**inputs):
    from concourse import bacc
    from concourse.bass_utils import run_bass_kernel_spmd

    nc = bacc.Bacc("TRN2", target_bir_lowering=False, num_devices=1)
    arrays = layout(inputs)
    d = {name: nc.dram_tensor(f"in_{name}", a.shape, mybir.dt.from_np(a.dtype), kind="ExternalInput").ap()
         for name, a in arrays.items()}
    d["out"] = nc.dram_tensor("out_0", (B, T, E), F32, kind="ExternalOutput").ap()
    audio_tower(nc, d)
    ran = run_bass_kernel_spmd(nc, [{f"in_{name}": a for name, a in arrays.items()}], core_ids=[0])
    return ran.results[0]["out_0"]
```

```python
from contextlib import ExitStack

import numpy as np

import concourse.bass as bass
from concourse import mybir

F32 = mybir.dt.float32
ALU = mybir.AluOpType
ACT = mybir.ActivationFunctionType
AX_X = mybir.AxisListType.X

P = 128
B, N, E = 32, 256, 256
KC = E // P
STRIDE = 4
T = N // STRIDE
TOK = B * T
TILES = TOK // P
LN_EPS = 1e-5
BANK = 512


def wait(eng, sem, count):
    if isinstance(count, int) and count <= 0:
        return
    eng.wait_ge(sem, count)


class Chain:

    def __init__(self, eng, sem):
        self.eng, self.sem, self.done, self.turns = eng, sem, 0, 0

    def __call__(self, ins):
        self.done += 1
        ins.then_inc(self.sem, 1)
        self.eng.wait_ge(self.sem, self.turns + self.done)

    def enter(self, turn, per_turn):
        self.before, self.per_turn = self.done, per_turn
        self.turns = turn * per_turn

    def leave(self, turns):
        assert self.done - self.before == self.per_turn, (self.done - self.before, self.per_turn)
        self.turns = 0
        self.done = self.before + turns * self.per_turn


def inverse_sqrt(dve, chain, y, t, v):
    i32 = mybir.dt.int32
    chain(dve.tensor_scalar(t.bitcast(i32), v.bitcast(i32), 1, None, ALU.logical_shift_right))
    chain(dve.tensor_scalar(y.bitcast(i32), t.bitcast(i32), -1.0, float(0x5F3759DF), ALU.mult, ALU.add))
    for _ in range(3):
        chain(dve.tensor_tensor(t, y, y, ALU.mult))
        chain(dve.tensor_tensor(t, t, v, ALU.mult))
        chain(dve.tensor_scalar(t, t, -0.5, 1.5, ALU.mult, ALU.add))
        chain(dve.tensor_tensor(y, y, t, ALU.mult))


RSQRT_LINKS = 14


def touch(dve, tile):
    dve.memset(tile[:, 0:1], 0.0)


def tok_stage(nc, d, c):
    with ExitStack() as ctx:
        sb = lambda name, shape: ctx.enter_context(nc.sbuf_tensor("tok_" + name, shape, F32))
        sem = lambda name: ctx.enter_context(nc.semaphore(name))
        wq_t = sb("wq_t", [P, KC, E])
        wk_t = sb("wk_t", [P, KC, E])
        wv = sb("wv", [P, KC, E])
        wqk = sb("wqk", [P, KC, E])
        gamma = sb("gamma", [P, E])
        beta = sb("beta", [P, E])
        x_in = sb("x_in", [P, 2, KC, E])
        xT_in = sb("xT_in", [P, 2, KC, N])
        g_sb = sb("g_sb", [P, 2, KC, N])
        probs = sb("probs", [P, 2, 2, N])
        pool_w = sb("pool_w", [P, P // STRIDE])
        pool_r = sb("pool_r", [P, 2, 2, P // STRIDE])
        pooled = sb("pooled", [P, 2, 2, T])
        px_sb = sb("px_sb", [P, KC, 2, T])
        mx = sb("mx", [P, 2, 2])
        neg_mx = sb("neg_mx", [P, 2, 2])
        row_sum = sb("row_sum", [P, 2, 2])
        row_inv = sb("row_inv", [P, 2, 2])
        stats = sb("stats", [P, 6])
        mean_var = sb("mean_var", [P, 2, 2])
        var_eps = sb("var_eps", [P, 2])
        rstd = sb("rstd", [P, 2])
        nwt = sb("nwt", [P, 2])
        z = sb("z", [P, E])
        attn_n = sb("attn_n", [P, E])
        h_tmp = sb("h_tmp", [P, E])
        xn = sb("xn", [P, E])
        ps = ctx.enter_context(nc.psum_tensor("ps_tok", [P, 8, BANK], F32))
        ps_g = [ps[:, b, :].rearrange("p (c n) -> p c n", c=KC) for b in (0, 1)]
        ps_s = [ps[:, 2 + b, :].rearrange("p (c n) -> p c n", c=2) for b in (0, 1)]
        ps_pool = ps[:, 4, 0:2 * T].rearrange("p (c t) -> p c t", c=2)
        ps_px = ps[:, 5, 0:KC * T].rearrange("p (c t) -> p c t", c=KC)
        ps_attn = ps[:, 6, 0:E]
        ps_tr = ps[:, 7, 0:KC * P].rearrange("p (c t) -> p c t", c=KC)

        w_in = sem("tok_wq_wk_in")
        wv_in = sem("tok_wv_gamma_beta_in")
        xT_loaded = [sem("xT_loaded0"), sem("xT_loaded1")]
        x_loaded = [sem("x_loaded0"), sem("x_loaded1")]
        pw_set = sem("pool_w_set")
        wqk_done = sem("wqk_done")
        wqk_copied = sem("wqk_copied")
        g_done = sem("g_done")
        g_copied = sem("g_copied")
        s_done = sem("s_done")
        nb_ready = sem("neg_max_ready")
        exp_done = sem("exp_done")
        er_ready = sem("pool_r_ready")
        pool_done = sem("pool_done")
        pool_copied = sem("pool_copied")
        px_done = sem("px_done")
        px_copied = sem("px_copied")
        attn_done = sem("attn_done")
        attn_read = sem("attn_read")
        xn_ready = sem("xn_ready")
        tr_done = sem("tr_done")
        tr_copied = sem("tr_copied")
        dve_link = sem("tok_dve_link")
        id_set = sem("ident_set")
        block = ctx.enter_context(nc.Block())

        FIRST, LAST = 5, B + 5
        HALF = (B - 1 - FIRST) // 2

        def steps(eng, step, chain=None, links=0):
            for n in range(FIRST):
                step(n, n // 2, n % 2)
            with eng.Fori(0, HALF) as i:
                if chain:
                    chain.enter(i, links)
                step(2 * i + FIRST, i + FIRST // 2, 1, inner=True)
                step(2 * i + FIRST + 1, i + FIRST // 2 + 1, 0, inner=True)
                if chain:
                    chain.leave(HALF)
            for n in range(B - 1, LAST):
                step(n, n // 2, n % 2)

        @block.sync
        def _(sp):
            sp.dma_start(wq_t[:], d["wqT"].rearrange("(c p) e -> p c e", p=P)).then_inc(w_in, 16)
            sp.dma_start(wk_t[:], d["wkT"].rearrange("(c p) e -> p c e", p=P)).then_inc(w_in, 16)

            def load_xT(n, par):
                wait(sp, s_done, n - 1)
                sp.dma_start(xT_in[:, par, :, :], d["xT"][bass.ds(n, 1)].rearrange("o (c p) n -> p (o c) n", p=P)
                             ).then_inc(xT_loaded[par], 16)

            def load_x(n, par):
                if not isinstance(n, int):
                    sp.wait_ge(px_done, n - 1)
                sp.dma_start(x_in[:, par, :, :], d["x"][bass.ds(n, 1)].rearrange("o (c p) e -> p (o c) e", p=P)
                             ).then_inc(x_loaded[par], 16)

            load_xT(0, 0)
            load_xT(1, 1)
            load_x(0, 0)
            sp.dma_start(wv[:], d["wv"].rearrange("(c p) e -> p c e", p=P)).then_inc(wv_in, 16)
            sp.dma_start(gamma[:], d["gamma"].partition_broadcast(P)).then_inc(wv_in, 16)
            sp.dma_start(beta[:], d["beta"].partition_broadcast(P)).then_inc(wv_in, 16)
            load_x(1, 1)
            with sp.Fori(1, B // 2) as i:
                for load in (load_xT, load_x):
                    for par in range(2):
                        load(2 * i + par, par)
            for name, src, shape in MIX_WEIGHTS:
                of = d[src]
                if src == "faaaa":
                    of = of.partition_broadcast(P)
                elif len(shape) == 3:
                    of = of.rearrange("(c p) e -> p c e", p=P)
                sp.dma_start(c.mix_w[name][:], of).then_inc(c.mix_w_in, 16)

        @block.gpsimd
        def _(pool):
            pool.memset(pool_w[:], 1.0 / STRIDE).then_inc(pw_set, 1)
            pool.wait_ge(pw_set, 1)
            pool.affine_select(out=pool_w[:], in_=pool_w[:], compare_op=ALU.is_ge, fill=0.0, base=0,
                               pattern=[[-STRIDE, P // STRIDE]], channel_multiplier=1).then_inc(pw_set, 1)
            pool.wait_ge(pw_set, 2)
            pool.affine_select(out=pool_w[:], in_=pool_w[:], compare_op=ALU.is_ge, fill=0.0, base=STRIDE - 1,
                               pattern=[[STRIDE, P // STRIDE]], channel_multiplier=-1).then_inc(pw_set, 1)
            pool.memset(c.ident[:], 0.0).then_inc(id_set, 1)
            pool.wait_ge(id_set, 1)
            pool.affine_select(out=c.ident[:], in_=c.ident[:], compare_op=ALU.not_equal, fill=1.0, base=0,
                               pattern=[[-1, P]], channel_multiplier=1).then_inc(id_set, 1)

        @block.tensor
        def _(pe):
            pe.wait_ge(w_in, 32)
            for ec in range(KC):
                for k in range(KC):
                    last = pe.matmul(ps_s[0][:, ec, :], wq_t[:, k, ec * P:(ec + 1) * P], wk_t[:, k, :],
                                     start=(k == 0), stop=(k == KC - 1))
            last.then_inc(wqk_done, 1)

            def g_mm(n, half, par):
                pe.wait_ge(xT_loaded[par], 16 * (half + 1))
                wait(pe, g_copied, n - 1)
                for ec in range(KC):
                    for k in range(KC):
                        last = pe.matmul(ps_g[par][:, ec, :], wqk[:, k, ec * P:(ec + 1) * P],
                                         xT_in[:, par, k, :], start=(k == 0), stop=(k == KC - 1))
                last.then_inc(g_done, 1)

            def s_mm(n, par):
                pe.wait_ge(g_copied, n + 1)
                wait(pe, exp_done, n - 1)
                for qc in range(2):
                    for k in range(KC):
                        last = pe.matmul(ps_s[par][:, qc, :], g_sb[:, par, k, qc * P:(qc + 1) * P],
                                         xT_in[:, par, k, :], start=(k == 0), stop=(k == KC - 1))
                last.then_inc(s_done, 1)

            def pool_mm(n, par):
                pe.wait_ge(er_ready, n + 1)
                wait(pe, pool_copied, n)
                half_t = T // 2
                for kc in range(2):
                    for qc in range(2):
                        last = pe.matmul(ps_pool[:, kc, qc * half_t:(qc + 1) * half_t],
                                         probs[:, par, qc, kc * P:(kc + 1) * P], pool_r[:, par, qc, :],
                                         start=True, stop=True)
                last.then_inc(pool_done, 1)

            def px_mm(n, half, par):
                pe.wait_ge(x_loaded[par], 16 * (half + 1))
                pe.wait_ge(pool_copied, n + 1)
                wait(pe, px_copied, n)
                for ec in range(KC):
                    for k in range(2):
                        last = pe.matmul(ps_px[:, ec, :], x_in[:, par, k, ec * P:(ec + 1) * P],
                                         pooled[:, par, k, :], start=(k == 0), stop=(k == 1))
                last.then_inc(px_done, 1)

            def attn_mm(p):
                pe.wait_ge(px_copied, 2 * p + 2)
                wait(pe, attn_read, p)
                for k in range(KC):
                    last = pe.matmul(ps_attn, px_sb[:, k, :, :].rearrange("p b t -> p (b t)"), wv[:, k, :],
                                     start=(k == 0), stop=(k == KC - 1))
                last.then_inc(attn_done, 1)

            def tr_mm(p):
                pe.wait_ge(xn_ready, p + 1)
                for k in range(KC):
                    last = pe.transpose(ps_tr[:, k, :], xn[:, k * P:(k + 1) * P], c.ident[:])
                last.then_inc(tr_done, 1)

            pe.wait_ge(wqk_copied, 1)
            g_mm(0, 0, 0)
            pe.wait_ge(wv_in, 48)
            pe.wait_ge(id_set, 2)

            def step(n, half, par, inner=False):
                if inner or n < B:
                    s_mm(n, par)
                if par == 0 and (inner or n >= 6):
                    tr_mm(half - 3)
                if inner or 1 <= n <= B:
                    pool_mm(n - 1, 1 - par)
                if inner or n + 1 < B:
                    g_mm(n + 1, half + par, 1 - par)
                if inner or 1 <= n <= B:
                    px_mm(n - 1, half + par - 1, 1 - par)
                if par == 0 and (inner or 2 <= n <= B):
                    attn_mm(half - 1)

            steps(pe, step)

        @block.scalar
        def _(act):
            def copy_g(n, par):
                act.wait_ge(g_done, n + 1)
                wait(act, s_done, n - 1)
                act.copy(g_sb[:, par, :, :], ps_g[par]).then_inc(g_copied, 1)

            def exps(n, par):
                act.wait_ge(nb_ready, n + 1)
                wait(act, pool_done, n - 1)
                act.activation(probs[:, par, 0, :], ps_s[par][:, 0, :], ACT.Exp, bias=neg_mx[:, par, 0:1],
                               scale=float(E) ** -0.5, accum_out=row_sum[:, par, 0:1])
                act.activation(probs[:, par, 1, :], ps_s[par][:, 1, :], ACT.Exp, bias=neg_mx[:, par, 1:2],
                               scale=float(E) ** -0.5, accum_out=row_sum[:, par, 1:2]).then_inc(exp_done, 1)

            def step(n, half, par, inner=False):
                if inner or n < B:
                    exps(n, par)
                if inner or n + 1 < B:
                    copy_g(n + 1, 1 - par)
                if inner or 1 <= n <= B:
                    act.wait_ge(px_done, n)
                    if par == 1:
                        wait(act, attn_done, half)
                    act.copy(px_sb[:, :, 1 - par, :], ps_px).then_inc(px_copied, 1)

            act.wait_ge(g_done, 1)
            act.copy(g_sb[:, 0, :, :], ps_g[0]).then_inc(g_copied, 1)
            steps(act, step)

        @block.vector
        def _(dve):
            chain = Chain(dve, dve_link)
            dve.wait_ge(wqk_done, 1)
            dve.tensor_copy(wqk[:], ps_s[0]).then_inc(wqk_copied, 1)
            chain(dve.memset(var_eps[:], 1.0))
            dve.wait_ge(pw_set, 3)
            dve.wait_ge(wv_in, 48)

            def row_max(n, par):
                dve.wait_ge(s_done, n + 1)
                chain(dve.tensor_reduce(mx[:, par, :], ps_s[par], AX_X, ALU.max))
                dve.tensor_scalar(neg_mx[:, par, :], mx[:, par, :], -float(E) ** -0.5, None,
                                  ALU.mult).then_inc(nb_ready, 1)

            def pool_weights(n, par):
                dve.wait_ge(exp_done, n + 1)
                wait(dve, pool_done, n - 1)
                chain(dve.reciprocal(row_inv[:, par, :], row_sum[:, par, :]))
                dve.tensor_scalar(pool_r[:, par, 0, :], pool_w[:], row_inv[:, par, 0:1], None, ALU.mult)
                dve.tensor_scalar(pool_r[:, par, 1, :], pool_w[:], row_inv[:, par, 1:2], None,
                                  ALU.mult).then_inc(er_ready, 1)

            def copy_pooled(n, par):
                dve.wait_ge(pool_done, n + 1)
                wait(dve, px_done, n - 1)
                dve.tensor_copy(pooled[:, par, :, :], ps_pool).then_inc(pool_copied, 1)

            def moments(w, src):
                chain(dve.bn_stats(stats[:], src))
                touch(dve, nwt)
                chain(dve.bn_aggr(mean_var[:, w, :], stats[:]))
                chain(dve.tensor_scalar(var_eps[:, w:w + 1], mean_var[:, w, 1:2], LN_EPS, None, ALU.add))

            def norms(p, first=True, second=True):
                inverse_sqrt(dve, chain, rstd[:], nwt[:], var_eps[:])
                if first:
                    dve.tensor_scalar(attn_n[:], ps_attn, mean_var[:, 0, 0:1], rstd[:, 0:1], ALU.subtract,
                                      ALU.mult).then_inc(attn_read, 1)
                if second:
                    dve.tensor_scalar(xn[:], z[:], mean_var[:, 1, 0:1], rstd[:, 1:2], ALU.subtract,
                                      ALU.mult).then_inc(xn_ready, 1)

            def affine(p):
                dve.wait_ge(attn_read, p + 1)
                chain(dve.tensor_tensor(h_tmp[:], attn_n[:], gamma[:], ALU.mult))
                chain(dve.tensor_tensor(z[:], h_tmp[:], beta[:], ALU.add))
                moments(1, z[:])
                dve.tensor_tensor(c.h[:, bass.ds(p, 1), :].rearrange("p o e -> p (o e)"), h_tmp[:], beta[:], ALU.add)

            def copy_xnT(p):
                dve.wait_ge(tr_done, p + 1)
                dve.tensor_scalar(c.xnT[:, :, bass.ds(p * P, P)], ps_tr, 1.0, None, ALU.mult).then_inc(tr_copied, 1)

            def step(n, half, par, inner=False):
                if inner or n < B:
                    row_max(n, par)
                if inner or 1 <= n <= B:
                    copy_pooled(n - 1, 1 - par)
                if inner or n < B:
                    pool_weights(n, par)
                if par == 1 and (inner or n >= 3):
                    norms(half - 1, first=inner or n <= B + 1, second=inner or n >= 5)
                if par == 0 and (inner or n >= 6):
                    copy_xnT(half - 3)
                if par == 0 and (inner or 4 <= n <= B + 2):
                    affine(half - 2)
                if par == 0 and (inner or 2 <= n <= B):
                    dve.wait_ge(attn_done, half)
                    moments(0, ps_attn)

            steps(dve, step, chain, 2 + 2 + RSQRT_LINKS + 2 + 2 * 3)


SL = 256
SLICES = TOK // SL
ST = SL // P
SB = SL // T
HEADS, HS = 16, 16
LOW_D, LOW = 64, 16
ARRAYS = 5
SCAN_Q, SCAN_A, SCAN_B, SCAN_K, SCAN_V = ROW_Q, ROW_A, ROW_B, ROW_K, ROW_V = range(ARRAYS)
TINY = 1e-24


RATE = float(np.exp(-0.5))
MIX_WEIGHTS = [("maa", "maa", [P, KC, 5]), ("maa_w1", "maa_w1T", [P, KC, P]), ("w_a1", "w_a1T", [P, KC, P]),
               ("w_b1", "w_b1T", [P, KC, 64]), ("w_g1", "w_g1T", [P, KC, P]), ("w_r", "w_rT", [P, KC, E]),
               ("w_k", "w_kT", [P, KC, E]), ("w_v", "w_vT", [P, KC, E]), ("maa_w2", "maa_w2", [P, E]),
               ("w_a2", "w_a2", [P, 3 * E]), ("a_bias", "a_bias", [P, 2]), ("w_b2", "w_b2", [64, 2 * E]),
               ("w_g2", "w_g2", [P, E]), ("faaaa", "faaaa", [P, E])]


def mix_stage(nc, d, c):
    with ExitStack() as ctx:
        sb = lambda name, shape: ctx.enter_context(nc.sbuf_tensor("mix_" + name, shape, F32))
        sem = lambda name: ctx.enter_context(nc.semaphore("mix_" + name))
        maa, maa_w1, w_a1, w_b1, w_g1, w_r, w_k, w_v, maa_w2, w_a2, a_bias, w_b2, w_g2, faaaa = (
            c.mix_w[n] for n, _, _ in MIX_WEIGHTS)
        xx = sb("xx", [P, KC, SL])
        mix = sb("mix", [P, KC, SL])
        lo1 = sb("lo1", [P, SL])
        xm = sb("xm", [P, 4, KC, SL])
        xm_tmp = sb("xm_tmp", [P, 2, SL])
        hid_a = sb("hid_a", [P, SL])
        hid_g = sb("hid_g", [P, SL])
        hid_b = sb("hid_b", [64, SL])

        scan = sb("scan", [P, 2, ST, ARRAYS - 1, E])
        q_raw = sb("q_raw", [P, 2, ST, E])
        v_raw = sb("v_raw", [P, 2, ST, E])
        sums = sb("sums", [P, 2, ST, E])
        cum = sb("cum", [P, 3, ST, E])
        tri = sb("tri", [P, 2, P])
        k_raw = sb("k_raw", [P, 2, ST, E])
        kk = sb("kk", [P, 2, ST, E])
        zd = sb("zd", [P, 2, ST, E])
        za_sig = sb("za_sig", [P, 2, ST, 2, E])
        mam_k = sb("mam_k", [P, 2, ST, 2, E])
        t0 = sb("t0", [P, ST, E])
        t1 = sb("t1", [P, ST, E])
        az = sb("az", [P, ST, E])
        mn = sb("mn", [P, ST, E])
        k2 = sb("k2", [P, ST, E])
        ls = sb("ls", [P, ST, E])
        b_raw = sb("b_raw", [P, ST, E])
        wm = sb("wm", [P, ST, E])
        ss = sb("ss", [P, ST * HEADS])
        rn = sb("rn", [P, ST * HEADS])
        rt = sb("rt", [P, ST * HEADS])
        rk = sb("rk", [P, ST * HEADS])

        ps = ctx.enter_context(nc.psum_tensor("ps_mix", [P, 8, BANK], F32))
        ps_rg, ps_kv, ps_kkk, ps_za, ps_mm = (ps[:, b, :] for b in range(5))
        pc = [ps[:, b, :].rearrange("p (c n) -> p c n", c=KC) for b in (5, 6, 7)]
        ps_lo1, ps_hb = pc[0], pc[0]
        ps_lo2 = [pc[1], pc[2], pc[0], pc[1]]
        ps_hag = pc[2]

        w_in = c.mix_w_in
        mix_ready, lo1_done, lo1_act, lo2_done, xm_ready = (sem(n) for n in ("mix_ready", "lo1_done", "lo1_act", "lo2_done", "xm_ready"))
        hag_done, hag_act, hb_done, hb_act = (sem(n) for n in ("hag_done", "hag_act", "hb_done", "hb_act"))
        rg_done, kv_done, kkk_done, z_done = (sem(n) for n in ("rg_done", "kv_done", "kkk_done", "z_done"))
        rg_read, kv_read, z_read, kk_ready = (sem(n) for n in ("rg_read", "kv_read", "z_read", "kk_ready"))
        az_ready, ls_ready, wm_ready, wide_done = (sem(n) for n in ("az_ready", "ls_ready", "wm_ready", "wide_done"))
        scan_out = [sem("scan_out0"), sem("scan_out1")]
        dve_link, act_link = sem("dve_link"), sem("act_link")
        zeros = sb("zeros", [ARRAYS - 1, E])
        zero_set, tail_out, tri_set = sem("zero_set"), sem("tail_out"), sem("tri_set")
        cum_done, cum_read, decay_ready = sem("cum_done"), sem("cum_read"), sem("decay_ready")
        k3_ready, scan_ready, v_out = sem("k3_ready"), sem("scan_ready"), [sem("v_out0"), sem("v_out1")]
        ps_cum = [ps[:, b, :].rearrange("p (t e) -> p t e", t=ST) for b in (6, 7)]
        STORE = 16 * 2
        block = ctx.enter_context(nc.Block())
        LOOP = SLICES // 2 - 2

        def slices(eng, first, turn, last, chain=None, links=0):
            first()
            turn(0, 0, 0, has_prev=False)
            turn(1, 0, 1)
            with eng.Fori(1, LOOP + 1) as i:
                if chain:
                    chain.enter(i - 1, links)
                turn(2 * i, i, 0)
                turn(2 * i + 1, i, 1)
                if chain:
                    chain.leave(LOOP)
            turn(SLICES - 2, SLICES // 2 - 1, 0)
            turn(SLICES - 1, SLICES // 2 - 1, 1, has_next=False)
            last()

        @block.sync
        def _(sp):
            sp.wait_ge(zero_set, 1)
            sp.dma_start(d["scan"][TOK:TOK + 1, ROW_A:, :].rearrange("o m e -> (o m) e"), zeros[:]).then_inc(tail_out, 16)

            rows = lambda first, a, b, s: d["scan"][first:first + TOK, a:b, :].rearrange(
                "(s t p) m e -> s p t (m e)", p=P, t=ST)[bass.ds(s, 1)].rearrange("o p t f -> (o p) t f")

            def store_v(s, par):
                sp.wait_ge(kv_read, ST * (s + 1))
                sp.dma_start(rows(0, ROW_V, ROW_V + 1, s), v_raw[:, par]).then_inc(v_out[par], 16)

            def store(s, par):
                sp.wait_ge(scan_ready, s + 1)
                sp.dma_start(rows(1, ROW_Q, ROW_Q + 1, s), scan[:, par, :, SCAN_Q, :]).then_inc(scan_out[par], 16)
                sp.dma_start(rows(0, ROW_A, ROW_K + 1, s), scan[:, par, :, SCAN_A:, :].rearrange("p t m e -> p t (m e)")
                             ).then_inc(scan_out[par], 16)

            store_v(0, 0)
            store_v(1, 1)
            store(0, 0)
            with sp.Fori(1, SLICES // 2) as i:
                store_v(2 * i, 0)
                store(2 * i - 1, 1)
                store_v(2 * i + 1, 1)
                store(2 * i, 0)
            store(SLICES - 1, 1)
            for q in scan_out:
                sp.wait_ge(q, STORE * (SLICES // 2))
            for q in v_out:
                sp.wait_ge(q, 16 * (SLICES // 2))
            sp.wait_ge(tail_out, 16)

        @block.gpsimd
        def _(pool):
            pool.memset(zeros[:], 0.0).then_inc(zero_set, 1)
            pool.memset(tri[:], 1.0).then_inc(tri_set, 1)
            pool.wait_ge(tri_set, 1)
            for w in range(2):
                pool.affine_select(out=tri[:, w, :], in_=tri[:, w, :], compare_op=ALU.is_ge, fill=0.0, base=-w,
                                   pattern=[[1, P]], channel_multiplier=-1).then_inc(tri_set, 1)
            pool.wait_ge(tri_set, 3)
            for w in range(2):
                pool.memset(tri[0:T, w, T:P], 0.0).then_inc(tri_set, 1)

            def products(s, half, par):
                pool.wait_ge(k3_ready, s + 1)
                wait(pool, scan_out[par], STORE * half)
                pool.tensor_tensor(scan[:, par, :, SCAN_Q, :], q_raw[:, par], cum[:, 0], ALU.mult)
                pool.tensor_tensor(scan[:, par, :, SCAN_K, :], k2[:], cum[:, 1], ALU.mult)
                pool.tensor_tensor(scan[:, par, :, SCAN_B, :], b_raw[:], cum[:, 1], ALU.mult)
                pool.tensor_tensor(scan[:, par, :, SCAN_A, :], kk[:, par], cum[:, 2], ALU.mult).then_inc(scan_ready, 1)

            for s in range(2):
                products(s, 0, s)
            with pool.Fori(1, SLICES // 2) as i:
                for par in range(2):
                    products(2 * i + par, i, par)

        @block.tensor
        def _(pe):
            def cumulate(s, par):
                pe.wait_ge(z_read, ST * (s + 1))
                for w in range(2):
                    for t in range(ST):
                        last = pe.matmul(ps_cum[w][:, t, :], tri[:, w, :], za_sig[:, par, t, 0, :], start=True, stop=True)
                last.then_inc(cum_done, 1)

            def chan(s, half, par):
                pe.wait_ge(mix_ready, s + 1)
                wait(pe, hb_act, s)
                for k in range(KC):
                    last = pe.matmul(ps_lo1[:, 0, :], maa_w1[:, k, :], mix[:, k, :], start=(k == 0), stop=(k == KC - 1))
                last.then_inc(lo1_done, 1)
                pe.wait_ge(lo1_act, s + 1)
                for g, (free, count) in enumerate(((xm_ready, 4 * s), (hag_act, s), (None, 0), (xm_ready, 4 * s + 1))):
                    if g < 2:
                        wait(pe, cum_read, s - 1)
                    if free is not None:
                        wait(pe, free, count)
                    for k in range(KC):
                        last = pe.matmul(ps_lo2[g][:, k, :], maa_w2[32 * g:32 * g + 32, k * P:(k + 1) * P],
                                         lo1[32 * g:32 * g + 32, :], start=True, stop=True)
                    last.then_inc(lo2_done, 1)
                pe.wait_ge(xm_ready, 4 * s + 2)
                for k in range(KC):
                    pe.matmul(ps_hag[:, 0, :], w_a1[:, k, :], xm[:, 1, k, :], start=(k == 0), stop=(k == KC - 1))
                for k in range(KC):
                    last = pe.matmul(ps_hag[:, 1, :], w_g1[:, k, :], xm[:, 0, k, :], start=(k == 0), stop=(k == KC - 1))
                last.then_inc(hag_done, 1)
                pe.wait_ge(xm_ready, 4 * s + 3)
                for k in range(KC):
                    last = pe.matmul(ps_hb[0:64, 0, :], w_b1[:, k, :], xm[:, 2, k, :], start=(k == 0), stop=(k == KC - 1))
                last.then_inc(hb_done, 1)

            def tiles(s):
                for t in range(ST):
                    j = ST * s + t
                    tok = slice(t * P, (t + 1) * P)
                    if t == 0:
                        pe.wait_ge(hag_act, s + 1)
                    wait(pe, rg_read, j)
                    for k in range(KC):
                        pe.matmul(ps_rg[:, 0:E], xm[:, 0, k, tok], w_r[:, k, :], start=(k == 0), stop=(k == KC - 1))
                    pe.matmul(ps_rg[:, E:2 * E], hid_g[:, tok], w_g2[:], start=True, stop=True).then_inc(rg_done, 1)
                    if t == 0:
                        pe.wait_ge(xm_ready, 4 * s + 4)
                    wait(pe, kv_read, j)
                    for k in range(KC):
                        pe.matmul(ps_kv[:, 0:E], xm[:, 2, k, tok], w_k[:, k, :], start=(k == 0), stop=(k == KC - 1))
                    for k in range(KC):
                        last = pe.matmul(ps_kv[:, E:2 * E], xm[:, 3, k, tok], w_v[:, k, :], start=(k == 0), stop=(k == KC - 1))
                    last.then_inc(kv_done, 1)
                    if t == 0:
                        pe.wait_ge(hb_act, s + 1)
                    if t == 0:
                        wait(pe, kk_ready, s)
                    pe.matmul(ps_kkk[:, t * E:(t + 1) * E], hid_b[0:64, tok], w_b2[0:64, 0:E], start=True, stop=True).then_inc(kkk_done, 1)
                    wait(pe, z_read, j)
                    pe.matmul(ps_za[:, :], hid_a[:, tok], w_a2[:, 0:2 * E], start=True, stop=True)
                    pe.matmul(ps_mm[:, 0:E], hid_a[:, tok], w_a2[:, 2 * E:3 * E], start=True, stop=True)
                    pe.matmul(ps_mm[:, E:2 * E], hid_b[0:64, tok], w_b2[0:64, E:2 * E], start=True, stop=True).then_inc(z_done, 1)

            def turn(s, half, par, has_prev=True, has_next=True):
                tiles(s)
                if has_prev:
                    cumulate(s - 1, 1 - par)
                if has_next:
                    chan(s + 1, half + par, 1 - par)

            pe.wait_ge(w_in, 16 * len(MIX_WEIGHTS))
            pe.wait_ge(tri_set, 5)
            def last():
                pe.wait_ge(cum_read, SLICES - 1)
                cumulate(SLICES - 1, 1)

            slices(pe, lambda: chan(0, 0, 0), turn, last)

        @block.scalar
        def _(act):
            chain = Chain(act, act_link)

            def lows(s):
                act.wait_ge(lo1_done, s + 1)
                act.activation(lo1[:], ps_lo1[:, 0, :], ACT.Tanh, bias=0.0).then_inc(lo1_act, 1)

            def hiddens(s):
                act.wait_ge(hag_done, s + 1)
                act.activation(hid_a[0:64, :], ps_hag[0:64, 0, :], ACT.Tanh, bias=0.0)
                act.activation(hid_a[64:128, :], ps_hag[64:128, 0, :], ACT.Identity, bias=a_bias[64:128, 0:1])
                act.activation(hid_g[:], ps_hag[:, 1, :], ACT.Tanh, bias=0.0).then_inc(hag_act, 1)
                act.wait_ge(hb_done, s + 1)
                act.activation(hid_b[0:32, :], ps_hb[0:32, 0, :], ACT.Tanh, bias=0.0)
                act.activation(hid_b[32:64, :], ps_hb[32:64, 0, :], ACT.Identity, bias=a_bias[32:64, 1:2]).then_inc(hb_act, 1)

            def tiles(s, half, par):
                wait(act, wide_done, s - 1)
                wait(act, scan_ready, s - 1)
                wait(act, v_out[par], 16 * half)
                for t in range(ST):
                    j = ST * s + t
                    act.wait_ge(rg_done, j + 1)
                    act.copy(q_raw[:, par, t, :], ps_rg[:, 0:E])
                    act.copy(c.gate[:, bass.ds(j, 1), :].rearrange("p o e -> p (o e)"), ps_rg[:, E:2 * E]).then_inc(rg_read, 1)
                    act.wait_ge(kv_done, j + 1)
                    act.copy(k_raw[:, par, t, :], ps_kv[:, 0:E])
                    act.copy(v_raw[:, par, t, :], ps_kv[:, E:2 * E]).then_inc(kv_read, 1)
                    act.wait_ge(z_done, j + 1)
                    act.copy(zd[:, par, t, :], ps_za[:, 0:E])
                    act.activation(za_sig[:, par, t].rearrange("p m e -> p (m e)"), ps_za, ACT.Sigmoid, bias=0.0)
                    act.activation(mam_k[:, par, t].rearrange("p m e -> p (m e)"), ps_mm, ACT.Sigmoid, bias=0.0).then_inc(z_read, 1)

            def sig_az(s):
                act.wait_ge(az_ready, s + 1)
                act.activation(az[:], az[:], ACT.Sigmoid, bias=0.0).then_inc(act_link, 1)

            def copy_sums(s):
                act.wait_ge(cum_done, s + 1)
                for w in range(2):
                    last = act.copy(sums[:, w], ps_cum[w])
                last.then_inc(cum_read, 1)

            def wide(s):
                chain.done += 1
                act.wait_ge(act_link, chain.turns + chain.done)
                act.activation(ls[:], az[:], ACT.Ln, bias=0.0).then_inc(ls_ready, 1)
                act.wait_ge(cum_read, s + 1)
                wait(act, scan_ready, s)
                act.activation(cum[:, 0], sums[:, 0], ACT.Exp, scale=-RATE, bias=0.0)
                act.activation(cum[:, 1], sums[:, 0], ACT.Exp, scale=RATE, bias=0.0)
                act.activation(cum[:, 2], sums[:, 1], ACT.Exp, scale=-RATE, bias=0.0)
                act.wait_ge(wm_ready, s + 1)
                act.activation(wm[:], wm[:], ACT.Exp, bias=0.0).then_inc(decay_ready, 1)

            def turn(s, half, par, has_prev=True, has_next=True):
                if has_prev:
                    sig_az(s - 1)
                tiles(s, half, par)
                if has_prev:
                    copy_sums(s - 1)
                if has_next:
                    lows(s + 1)
                if has_prev:
                    wide(s - 1)
                if has_next:
                    hiddens(s + 1)

            def first():
                lows(0)
                hiddens(0)

            def last():
                sig_az(SLICES - 1)
                copy_sums(SLICES - 1)
                wide(SLICES - 1)

            act.wait_ge(w_in, 16 * len(MIX_WEIGHTS))
            slices(act, first, turn, last, chain, 2)

        @block.vector
        def _(dve):
            chain = Chain(dve, dve_link)
            heads = lambda ap: ap.rearrange("p t (h j) -> p t h j", j=HS)
            per_head = lambda ap: ap[:].rearrange("p (t h) -> p t h", t=ST)

            def shift(s):
                x = c.xnT[:, :, bass.ds(s * SL, SL)]
                xb = x.rearrange("p c (b t) -> p c b t", t=T)
                xxb = xx[:].rearrange("p c (b t) -> p c b t", t=T)
                for k in range(KC):
                    dve.tensor_tensor(xxb[:, k, :, 1:T], xb[:, k, :, 0:T - 1], xb[:, k, :, 1:T], ALU.subtract)
                for k in range(KC):
                    chain(dve.tensor_scalar(xxb[:, k, :, 0:1], xb[:, k, :, 0:1], -1.0, None, ALU.mult))
                wait(dve, lo1_done, s)
                for k in range(KC):
                    last = dve.scalar_tensor_tensor(out=mix[:, k, :], in0=xx[:, k, :], scalar=maa[:, k, 4:5],
                                                    in1=x[:, k, :], op0=ALU.mult, op1=ALU.add)
                last.then_inc(mix_ready, 1)

            def mixes(s, which):
                x = c.xnT[:, :, bass.ds(s * SL, SL)]
                for g in which:
                    dve.wait_ge(lo2_done, 4 * s + g + 1)
                    wait(dve, xm_ready, 4 * s + g)
                    for k in range(KC):
                        last = dve.scalar_tensor_tensor(out=xm_tmp[:, k, :], in0=ps_lo2[g][:, k, :], scalar=maa[:, k, g:g + 1],
                                                        in1=xx[:, k, :], op0=ALU.add, op1=ALU.mult)
                    chain(last)
                    dve.tensor_tensor(xm[:, g, :, :], xm_tmp[:], x, ALU.add).then_inc(xm_ready, 1)

            def tiles(s, par):
                dve.wait_ge(kkk_done, ST * (s + 1))
                dve.wait_ge(kv_read, ST * (s + 1))
                wait(dve, scan_ready, s - 1)
                dve.tensor_tensor(kk[:, par], ps_kkk.rearrange("p (t e) -> p t e", t=ST), k_raw[:, par], ALU.add).then_inc(kk_ready, 1)

            def log_sigmoid(s, par):
                dve.wait_ge(z_read, ST * (s + 1))
                dve.scalar_tensor_tensor(out=az[:], in0=zd[:, par], scalar=-1.0, in1=zd[:, par],
                                         op0=ALU.mult, op1=ALU.max).then_inc(az_ready, 1)
                dve.tensor_scalar(mn[:], zd[:, par], 0.0, None, ALU.min)

            def wide_1(s, par):
                a, ma = za_sig[:, par, :, 1, :], mam_k[:, par, :, 0, :]
                dve.wait_ge(kk_ready, s + 1)
                chain(dve.tensor_tensor(t0[:], kk[:, par], kk[:, par], ALU.mult))
                chain(dve.tensor_reduce(per_head(ss), heads(t0[:]), AX_X, ALU.add))
                chain(dve.tensor_scalar(ss[:], ss[:], TINY, None, ALU.max))
                inverse_sqrt(dve, chain, rn[:], rt[:], ss[:])
                chain(dve.tensor_tensor(heads(kk[:, par]), heads(kk[:, par]),
                                        per_head(rn).unsqueeze(3).to_broadcast([P, ST, HEADS, HS]), ALU.mult))
                wait(dve, scan_ready, s)
                dve.scalar_tensor_tensor(out=b_raw[:], in0=kk[:, par], scalar=-1.0,
                                         in1=a, op0=ALU.mult, op1=ALU.mult)
                chain(dve.scalar_tensor_tensor(out=t1[:], in0=ma, scalar=1.0, in1=a, op0=ALU.subtract, op1=ALU.mult))
                chain(dve.tensor_tensor(t1[:], ma, t1[:], ALU.subtract))
                chain(dve.tensor_tensor(k2[:], k_raw[:, par], t1[:], ALU.mult))

            def wide_2(s, par):
                dve.wait_ge(ls_ready, s + 1)
                chain(dve.scalar_tensor_tensor(out=ls[:], in0=ls[:], scalar=-0.5, in1=mn[:], op0=ALU.add, op1=ALU.add))
                dve.tensor_tensor(wm[:], ls[:], mam_k[:, par, :, 1, :], ALU.mult).then_inc(wm_ready, 1)
                chain(dve.tensor_tensor(t0[:], q_raw[:, par],
                                        faaaa[:].unsqueeze(1).to_broadcast([P, ST, E]), ALU.mult))

            def wide_3(s, par):
                dve.wait_ge(decay_ready, s + 1)
                dve.tensor_tensor(k2[:], k2[:], wm[:], ALU.mult).then_inc(k3_ready, 1)
                dve.wait_ge(k3_ready, s + 1)
                chain(dve.tensor_tensor(t0[:], t0[:], k2[:], ALU.mult))
                chain(dve.tensor_reduce(per_head(rk), heads(t0[:]), AX_X, ALU.add))
                dve.tensor_tensor(c.bonus[:, bass.ds(ST * s, ST), :].rearrange("p t (h j) -> p t h j", j=HS),
                                  heads(v_raw[:, par]),
                                  per_head(rk).unsqueeze(3).to_broadcast([P, ST, HEADS, HS]), ALU.mult).then_inc(wide_done, 1)

            def turn(s, half, par, has_prev=True, has_next=True):
                if has_prev:
                    log_sigmoid(s - 1, 1 - par)
                if has_next:
                    shift(s + 1)
                if has_prev:
                    wide_1(s - 1, 1 - par)
                tiles(s, par)
                if has_next:
                    mixes(s + 1, (0,))
                if has_prev:
                    wide_2(s - 1, 1 - par)
                if has_next:
                    mixes(s + 1, (1, 2, 3))
                if has_prev:
                    wide_3(s - 1, 1 - par)

            def first():
                shift(0)
                mixes(0, range(4))

            def last():
                log_sigmoid(SLICES - 1, 1)
                wide_1(SLICES - 1, 1)
                wide_2(SLICES - 1, 1)
                wide_3(SLICES - 1, 1)

            dve.wait_ge(w_in, 16 * len(MIX_WEIGHTS))
            slices(dve, first, turn, last, chain, 2 * (1 + 4 + 3 + RSQRT_LINKS + 1 + 3 + 2 + 3))


CHUNK = 8
CHUNKS = T // CHUNK
HG = 4
GH = HEADS // HG
GC = GH * HS
HALF_I = HS // 2
LOADS = 16 * HG


def scan_stage(nc, d, c):
    with ExitStack() as ctx:
        sb = lambda name, shape: ctx.enter_context(nc.sbuf_tensor("scan_" + name, shape, F32))
        sem = lambda name: ctx.enter_context(nc.semaphore("scan_" + name))
        vec = sb("vec", [P, 2, CHUNK, ARRAYS, GC])
        prod = sb("prod", [P, 2, 2, 2, HALF_I * GC])
        outer = sb("outer", [P, 2, HALF_I * GC])
        kv = sb("kv", [P, 2, HS * GC])
        sa = sb("sa", [P, HS * GH])
        y = sb("y", [P, 2, CHUNK, GC])
        part = sb("part", [P, 3, 2, HALF_I * GH, HS // 2])
        first = sb("first", [P, 2, GC])
        ps = ctx.enter_context(nc.psum_tensor("ps_scan", [P, 2, BANK], F32))
        loaded = [sem("loaded0"), sem("loaded1")]
        stored = [sem("stored0"), sem("stored1")]
        added, o_ready, prod_ready = ([sem(f"{n}{h}") for h in range(2)] for n in ("added", "outer_ready", "prod_ready"))
        kv_ready, y_done, sa_link, outer_zero = sem("kv_ready"), sem("y_done"), sem("sa_link"), sem("outer_zero")
        first_in, part_link = sem("first_in"), sem("part_link")
        block = ctx.enter_context(nc.Block())
        TURNS = CHUNKS // 2

        rows = lambda ap, g: ap[g * B:(g + 1) * B]

        def steps(eng, step):
            with eng.Fori(0, TURNS) as i:
                for par in range(2):
                    for tau in range(CHUNK):
                        step(i * 2 * CHUNK + par * CHUNK + tau, 2 * i + par, i, par, tau)

        @block.sync
        def _(sp):
            src = d["scan"][1:TOK + 1].rearrange("(b n t) m (g e) -> n g b t m e", t=CHUNK, n=CHUNKS, g=HG)

            def load(chunk, par):
                if not isinstance(chunk, int):
                    sp.wait_ge(o_ready[1], CHUNK * (chunk - 1) + 1)
                    sp.wait_ge(kv_ready, CHUNK * (chunk - 1) + 1)
                for g in range(HG):
                    sp.dma_start(rows(vec, g)[:, par].rearrange("b t m e -> b t m e"),
                                 src[bass.ds(chunk, 1), g].rearrange("o b t m e -> (o b) t m e")).then_inc(loaded[par], 16)

            heads_0 = d["scan"][0:TOK].rearrange("(b t) m (g e) -> t g b m e", t=T, g=HG)
            for g in range(HG):
                sp.dma_start(rows(first, g), heads_0[0, g, :, ROW_K:ROW_V + 1, :]).then_inc(first_in, 16)
            load(0, 0)
            load(1, 1)
            with sp.Fori(1, TURNS) as i:
                load(2 * i, 0)
                load(2 * i + 1, 1)

        @block.scalar
        def _(act):
            dst = d["y"].rearrange("(b n t) (g e) -> n g b t e", t=CHUNK, n=CHUNKS, g=HG)
            with act.Fori(0, TURNS) as i:
                for par in range(2):
                    act.wait_ge(y_done, CHUNK * (2 * i + par + 1) + 1)
                    for g in range(HG):
                        act.dma_start(dst[bass.ds(2 * i + par, 1), g].rearrange("o b t e -> (o b) t e"),
                                      rows(y, g)[:, par]).then_inc(stored[par], 16)
            for q in stored:
                act.wait_ge(q, LOADS * TURNS)

        @block.gpsimd
        def _(pool):
            pool.memset(outer[:], 0.0).then_inc(outer_zero, 1)
            pool.memset(y[:], 0.0).then_inc(y_done, 1)

            def v_outer_k(slot, k, v):
                v = v.rearrange("p (h i) -> p i h", i=HS).unsqueeze(3).to_broadcast([P, HS, GH, HS])
                k = k.rearrange("p (h j) -> p h j", j=HS).unsqueeze(1).to_broadcast([P, HS, GH, HS])
                pool.tensor_tensor(kv[:, slot, :].rearrange("p (i h j) -> p i h j", i=HS, h=GH), v, k,
                                   ALU.mult).then_inc(kv_ready, 1)

            def sum_y(t, half, par, tau):
                pool.wait_ge(prod_ready[1], t + 1)
                if tau == 0:
                    wait(pool, stored[par], LOADS * half)
                src = prod[:, tau % 2, :, 0, :].rearrange("p s (r j) -> p s r j", j=HS)
                n = HS // 2
                for level in range(3):
                    dst = part[:, level, :, :, 0:n]
                    pool.tensor_tensor(dst, src[:, :, :, 0:n], src[:, :, :, n:2 * n], ALU.add).then_inc(part_link, 1)
                    pool.wait_ge(part_link, 3 * t + level + 1)
                    src, n = dst, n // 2
                terms = src.rearrange("p s (i h) j -> p (s i) h j", h=GH)
                pool.tensor_tensor(y[:, par, tau, :].rearrange("p (h i) -> p i h", i=HS), terms[:, :, :, 0],
                                   terms[:, :, :, 1], ALU.add).then_inc(y_done, 1)

            def step(t, chunk, half, par, tau):
                if tau == 0:
                    pool.wait_ge(loaded[par], LOADS * (half + 1))
                pool.wait_ge(added[1], t + 1)
                v_outer_k((tau + 1) % 2, vec[:, par, tau, ROW_K, :], vec[:, par, tau, ROW_V, :])
                sum_y(t, half, par, tau)

            pool.wait_ge(first_in, LOADS)
            v_outer_k(0, first[:, 0, :], first[:, 1, :])
            steps(pool, step)

        @block.tensor
        def _(pe):
            pe.wait_ge(outer_zero, 1)
            for h in range(2):
                pe.matmul(ps[:, h, :], c.ident[:], outer[:, h, :], start=True, stop=True).then_inc(added[h], 1)

            def step(t, chunk, half, par, tau):
                pe.wait_ge(kv_ready, t + 1)
                for h in range(2):
                    wait(pe, prod_ready[h], t)
                    pe.matmul(ps[:, h, :], c.ident[:], kv[:, tau % 2, h * BANK:(h + 1) * BANK], start=False, stop=False,
                              skip_group_check=True)
                    pe.wait_ge(o_ready[h], t + 1)
                    pe.matmul(ps[:, h, :], c.ident[:], outer[:, h, :], start=False, stop=True,
                              skip_group_check=True).then_inc(added[h], 1)

            steps(pe, step)

        @block.vector
        def _(dve):
            def outer_u_b(h, vec_b):
                shape = [P, HALF_I, GH, HS]
                u = sa[:, h * HALF_I * GH:(h + 1) * HALF_I * GH].rearrange("p (i h) -> p i h", h=GH)
                b = vec_b.rearrange("p (h j) -> p h j", j=HS)
                dve.tensor_tensor(outer[:, h, :].rearrange("p (i h j) -> p i h j", h=GH, j=HS),
                                  u.unsqueeze(3).to_broadcast(shape), b.unsqueeze(1).to_broadcast(shape),
                                  ALU.mult).then_inc(o_ready[h], 1)

            for h in range(2):
                dve.wait_ge(outer_zero, 1)
                dve.wait_ge(added[h], 1)
                dve.memset(outer[:, h, :], 0.0).then_inc(o_ready[h], 1)

            def step(t, chunk, half, par, tau):
                for h in range(2):
                    dve.wait_ge(added[h], t + 2)
                    if tau == 0 and h == 0:
                        dve.wait_ge(loaded[par], LOADS * (half + 1))
                    dve.wait_ge(y_done, t)
                    pr = prod[:, tau % 2, h, :, :]
                    vecs = vec[:, par, tau, ROW_Q:ROW_A + 1, :].unsqueeze(2).to_broadcast([P, 2, HALF_I, GC])
                    state = ps[:, h, :].rearrange("p (i e) -> p i e", e=GC).unsqueeze(1).to_broadcast([P, 2, HALF_I, GC])
                    dve.tensor_tensor(pr.rearrange("p m (i e) -> p m i e", e=GC), state, vecs, ALU.mult).then_inc(prod_ready[h], 1)
                    dve.wait_ge(prod_ready[h], t + 1)
                    dve.tensor_reduce(sa[:, h * HALF_I * GH:(h + 1) * HALF_I * GH],
                                      pr[:, 1, :].rearrange("p (r j) -> p r j", j=HS), AX_X, ALU.add).then_inc(sa_link, 1)
                    dve.wait_ge(sa_link, 2 * t + h + 1)
                    outer_u_b(h, vec[:, par, tau, ROW_B, :])

            steps(dve, step)


GROUP = 2
GROUPS = TILES // GROUP
GN_EPS = 0.00064
EXPERTS, FF = 8, 1024
FC = FF // P
JITTER = 0.01
NT = 256
TURNS_X = (2 * TOK - EXPERTS) // NT + EXPERTS
TT = NT // P
SLOT_TILES = TURNS_X * TT
F32R = mybir.dt.float32r
HL, HI, LO = 2, 0, 1
GF = 2
G = FC // GF
ROWS = TOK + NT
U32 = mybir.dt.uint32
I32 = mybir.dt.int32


def load_expert(sp, d, c, j, split=None):
    x = sp.value_load(c.turn_expert[0:1, bass.ds(j, 1)], min_val=0, max_val=EXPERTS - 1)
    for n, name in enumerate(("w1", "w3", "w2")):
        if split:
            sp.wait_ge(split[n], j)
        sp.dma_start(c.raw[n][:], d[name][bass.ds(x, 1)].rearrange("o (k p) f -> p (o k) f", p=P)).then_inc(c.raw_in[n], 16)


def out_stage(nc, d, c):
    with ExitStack() as ctx:
        sb = lambda name, shape, dt=F32: ctx.enter_context(nc.sbuf_tensor("out_" + name, shape, dt))
        sem = lambda name: ctx.enter_context(nc.semaphore("out_" + name))
        y = sb("y", [P, TILES, E])
        sq = sb("sq", [P, GROUP, E])
        h_new = sb("h_new", [P, GROUP, E])
        gated = sb("gated", [P, GROUP, E])
        ln_w, ln_b = sb("ln_w", [P, E]), sb("ln_b", [P, E])
        w_o = sb("w_o", [P, KC, E])
        gate_w = sb("gate_w", [P, KC, EXPERTS])
        NG = GROUP * HEADS
        g_sum, g_mean, g_var, g_rstd, g_tmp = (sb(n, [P, NG]) for n in ("g_sum", "g_mean", "g_var", "g_rstd", "g_tmp"))
        ygT = sb("ygT", [P, GROUP, KC, P])
        xn = sb("xn", [P, GROUP, E])
        xT = sb("xT", [P, GROUP, KC, P])
        stats = sb("stats", [P, GROUP, 6])
        mean_var = sb("mean_var", [P, GROUP, 2])
        var_eps, rstd, nwt = (sb(n, [P, GROUP]) for n in ("var_eps", "rstd", "nwt"))
        logits = sb("logits", [P, TILES, EXPERTS])
        top = sb("top", [P, TILES, 8])
        top_i = sb("top_i", [P, TILES, 8], mybir.dt.uint32)
        top_f = sb("top_f", [P, TILES, 2])
        expert_no = sb("expert_no", [P, EXPERTS])
        expert_ni = sb("expert_ni", [P, EXPERTS], mybir.dt.int32)
        hot = [sb("hot0", [P, TILES, EXPERTS]), sb("hot1", [P, TILES, EXPERTS])]
        absl, dif, fac, keep, ex = (sb(n, [P, TILES, EXPERTS]) for n in ("absl", "dif", "fac", "keep", "ex"))
        den = sb("den", [P, TILES])
        chosen, rank = sb("chosen", [P, TILES, EXPERTS]), sb("rank", [P, TILES, EXPERTS])
        before = [sb("before0", [P, TILES, EXPERTS]), sb("before1", [P, TILES, EXPERTS])]
        n_i = sb("n_i", [P, EXPERTS], I32)
        turns_of, start, base = (sb(n, [P, EXPERTS]) for n in ("turns_of", "start", "base"))
        le = sb("le", [P, TURNS_X, EXPERTS])
        te, turn_no = sb("te", [P, TURNS_X]), sb("turn_no", [P, TURNS_X])
        turn_ni = sb("turn_ni", [P, TURNS_X], I32)
        weight = sb("weight", [P, 2, TILES])
        slot_f, slot_i = sb("slot_f", [P, 2, TILES]), sb("slot_i", [P, 2, TILES], I32)
        place_i, tile_i = sb("place_i", [P, 2, TILES], I32), sb("tile_i", [P, 2, TILES], I32)
        place, tile = sb("place", [P, 2, TILES]), sb("tile", [P, 2, TILES])
        at_place = sb("at_place", [P, 2, TILES, P])
        at_tile = sb("at_tile", [P, 2, TILES, 2, SLOT_TILES])
        place_no, tile_no, row_no = sb("place_no", [P, P]), sb("tile_no", [P, SLOT_TILES]), sb("row_no", [P, TILES])
        empty_row, taken = sb("empty_row", [P, SLOT_TILES]), sb("taken", [P, SLOT_TILES])
        numbers = sb("numbers", [P, P + SLOT_TILES + TILES + SLOT_TILES], I32)
        zeros = sb("zeros", [P, E])
        tri = sb("tri", [P, P])
        ones = sb("ones", [P, P])
        ps = ctx.enter_context(nc.psum_tensor("ps_out", [P, 6, BANK], F32))
        ps_t = ps[:, 0, :].rearrange("p (t k n) -> p t k n", t=GROUP, k=KC)
        ps_o = ps[:, 1, :].rearrange("p (t e) -> p t e", t=GROUP)
        ps_x = ps[:, 2, :].rearrange("p (t k n) -> p t k n", t=GROUP, k=KC)
        ps_l = ps[:, 3, 0:TILES * EXPERTS].rearrange("p (t x) -> p t x", t=TILES)
        ps_rank, ps_count = (ps[:, 4, w * TILES * EXPERTS:(w + 1) * TILES * EXPERTS].rearrange("p (t x) -> p t x", t=TILES)
                             for w in range(2))
        ps_slots = ps[:, 5, 0:2 * SLOT_TILES].rearrange("p (v a) -> p v a", v=2)
        places_ready, slots_done, tiles_in = sem("places_ready"), sem("slots_done"), sem("y_rest_in")
        stored, zero_set, zero_stored, experts_ready = sem("stored"), sem("zero_set"), sem("zero_stored"), sem("experts_ready")
        chosen_ready, ranks_done, tri_set = sem("chosen_ready"), sem("ranks_done"), sem("tri_set")
        w_in, y_in = sem("w_in"), sem("y_in")
        yg_ready, t_done, t_copied, o_done, o_read = (sem(n) for n in ("yg_ready", "t_done", "t_copied", "o_done", "o_read"))
        xn_ready, x_done, x_copied, l_done, no_set = (sem(n) for n in ("xn_ready", "x_done", "x_copied", "l_done", "no_set"))
        dve_link, e_asked, e_ready = sem("dve_link"), sem("exp_asked"), sem("exp_ready")
        block = ctx.enter_context(nc.Block())

        @block.sync
        def _(sp):
            rows = d["y"].rearrange("(t p) e -> p t e", p=P)
            sp.dma_start(y[:, 0:GROUP], rows[:, 0:GROUP]).then_inc(y_in, 16)
            sp.dma_start(ln_w[:], d["ln_w"].partition_broadcast(P)).then_inc(w_in, 16)
            sp.dma_start(ln_b[:], d["ln_b"].partition_broadcast(P)).then_inc(w_in, 16)
            sp.dma_start(w_o[:], d["w_oT"].rearrange("(c p) e -> p c e", p=P)).then_inc(w_in, 16)
            sp.dma_start(gate_w[:], d["gate_w"].rearrange("(c p) e -> p c e", p=P)).then_inc(w_in, 16)
            sp.dma_start(y[:, GROUP:], rows[:, GROUP:]).then_inc(tiles_in, 16)
            sp.wait_ge(zero_set, 1)
            for name in ("xn_rows", "sum_rows"):
                for t in range(TT):
                    sp.dma_start(d[name][TOK + t * P:TOK + (t + 1) * P], zeros[:]).then_inc(zero_stored, 16)
            xn_rows, sum_rows = (d[n][0:TOK].rearrange("(t p) e -> p t e", p=P) for n in ("xn_rows", "sum_rows"))
            with sp.Fori(0, GROUPS) as g:
                at = bass.ds(g * GROUP, GROUP)
                sp.wait_ge(xn_ready, g + 1)
                sp.dma_start(xn_rows[:, at], xn[:]).then_inc(stored, 16)
                sp.dma_start(sum_rows[:, at], c.h[:, at]).then_inc(stored, 16)
            sp.wait_ge(zero_stored, 2 * TT * 16)
            sp.wait_ge(stored, GROUPS * 32)

            sp.wait_ge(experts_ready, 1)
            load_expert(sp, d, c, 0)

        @block.gpsimd
        def _(pool):
            pool.iota(expert_ni[:], pattern=[[1, EXPERTS]], base=0, channel_multiplier=0).then_inc(no_set, 1)
            pool.wait_ge(no_set, 1)
            pool.tensor_copy(expert_no[:], expert_ni[:]).then_inc(no_set, 1)
            pool.iota(turn_ni[:], pattern=[[1, TURNS_X]], base=0, channel_multiplier=0).then_inc(no_set, 1)
            pool.wait_ge(no_set, 3)
            pool.tensor_copy(turn_no[:], turn_ni[:]).then_inc(no_set, 1)
            pool.memset(zeros[:], 0.0).then_inc(zero_set, 1)
            at = 0
            for n, start, step_p, pattern in ((P, 0, 0, [[1, P]]), (SLOT_TILES, 0, 0, [[1, SLOT_TILES]]),
                                              (TILES, 1, 1, [[P, TILES]]), (SLOT_TILES, TOK + 1, 1, [[0, TURNS_X], [P, TT]])):
                last = pool.iota(numbers[:, at:at + n], pattern=pattern, base=start, channel_multiplier=step_p)
                at += n
            last.then_inc(no_set, 1)
            pool.wait_ge(no_set, 5)
            at = 0
            for to in (place_no, tile_no, row_no, empty_row):
                n = to.shape[1]
                last = pool.tensor_copy(to[:], numbers[:, at:at + n])
                at += n
            last.then_inc(no_set, 1)
            pool.memset(ones[:], 1.0).then_inc(tri_set, 1)
            pool.memset(tri[:], 1.0).then_inc(tri_set, 1)
            pool.wait_ge(tri_set, 2)
            pool.affine_select(out=tri[:], in_=tri[:], compare_op=ALU.is_ge, fill=0.0, base=-1,
                               pattern=[[1, P]], channel_multiplier=-1).then_inc(tri_set, 1)

        @block.tensor
        def _(pe):
            def project(g):
                pe.wait_ge(yg_ready, g + 1)
                wait(pe, t_copied, g)
                for t in range(GROUP):
                    for k in range(KC):
                        last = pe.transpose(ps_t[:, t, k, :], gated[:, t, k * P:(k + 1) * P], c.ident[:])
                last.then_inc(t_done, 1)
                pe.wait_ge(t_copied, g + 1)
                wait(pe, o_read, g)
                for t in range(GROUP):
                    for k in range(KC):
                        last = pe.matmul(ps_o[:, t, :], ygT[:, t, k, :], w_o[:, k, :], start=(k == 0), stop=(k == KC - 1))
                last.then_inc(o_done, 1)

            def gate(g):
                pe.wait_ge(xn_ready, g + 1)
                wait(pe, x_copied, g)
                for t in range(GROUP):
                    for k in range(KC):
                        last = pe.transpose(ps_x[:, t, k, :], xn[:, t, k * P:(k + 1) * P], c.ident[:])
                last.then_inc(x_done, 1)
                pe.wait_ge(x_copied, g + 1)
                for t in range(GROUP):
                    for k in range(KC):
                        last = pe.matmul(ps_l[:, bass.ds(g * GROUP + t, 1), :].rearrange("p o x -> p (o x)"),
                                         xT[:, t, k, :], gate_w[:, k, :], start=(k == 0), stop=(k == KC - 1))
                last.then_inc(l_done, 1)

            pe.wait_ge(w_in, 64)
            project(0)
            project(1)
            gate(0)
            with pe.Fori(1, GROUPS - 1) as i:
                project(i + 1)
                gate(i)
            gate(GROUPS - 1)
            pe.wait_ge(tri_set, 3)
            pe.wait_ge(chosen_ready, 1)
            flat = chosen[:].rearrange("p t x -> p (t x)")
            pe.matmul(ps_rank.rearrange("p t x -> p (t x)"), tri[:], flat, start=True, stop=True)
            pe.matmul(ps_count.rearrange("p t x -> p (t x)"), ones[:], flat, start=True, stop=True).then_inc(ranks_done, 1)
            pe.wait_ge(places_ready, 1)
            for w in range(2):
                for t in range(TILES):
                    last = pe.matmul(ps[:, 5, 0:2 * SLOT_TILES], at_place[:, w, t, :],
                                     at_tile[:, w, t].rearrange("p v a -> p (v a)"),
                                     start=(w == 0 and t == 0), stop=(w == 1 and t == TILES - 1))
            last.then_inc(slots_done, 1)

        @block.scalar
        def _(act):
            def copy_t(g):
                act.wait_ge(t_done, g + 1)
                wait(act, o_done, g)
                act.copy(ygT[:], ps_t).then_inc(t_copied, 1)

            def copy_x(g):
                act.wait_ge(x_done, g + 1)
                wait(act, l_done, g)
                act.copy(xT[:], ps_x).then_inc(x_copied, 1)

            copy_t(0)
            copy_t(1)
            copy_x(0)
            with act.Fori(1, GROUPS - 1) as i:
                copy_t(i + 1)
                copy_x(i)
            copy_x(GROUPS - 1)
            for w in range(2):
                act.wait_ge(e_asked, w + 1)
                act.activation(ex[:], ex[:], ACT.Exp, bias=0.0).then_inc(e_ready, 1)

        @block.vector
        def _(dve):
            chain = Chain(dve, dve_link)
            heads = lambda ap: ap.rearrange("p t (h j) -> p t h j", j=HS)
            per_head = lambda ap: ap[:].rearrange("p (t h) -> p t h", t=GROUP)
            spread = lambda ap: per_head(ap).unsqueeze(3).to_broadcast([P, GROUP, HEADS, HS])
            tiled = lambda ap: ap[:].unsqueeze(1).to_broadcast([P, GROUP, E])

            def norm_y(g):
                at = bass.ds(g * GROUP, GROUP)
                yg = y[:, at, :]
                chain(dve.tensor_reduce(per_head(g_sum), heads(yg), AX_X, ALU.add))
                chain(dve.tensor_scalar(g_mean[:], g_sum[:], 1.0 / HS, None, ALU.mult))
                chain(dve.tensor_tensor(heads(yg), heads(yg), spread(g_mean), ALU.subtract))
                chain(dve.tensor_tensor(sq[:], yg, yg, ALU.mult))
                chain(dve.tensor_reduce(per_head(g_var), heads(sq[:]), AX_X, ALU.add))
                chain(dve.tensor_scalar(g_var[:], g_var[:], 1.0 / HS, GN_EPS, ALU.mult, ALU.add))
                inverse_sqrt(dve, chain, g_rstd[:], g_tmp[:], g_var[:])
                chain(dve.tensor_tensor(heads(yg), heads(yg), spread(g_rstd), ALU.mult))
                chain(dve.tensor_tensor(yg, yg, tiled(ln_w), ALU.mult))
                chain(dve.tensor_tensor(yg, yg, tiled(ln_b), ALU.add))
                chain(dve.tensor_tensor(yg, yg, c.bonus[:, at, :], ALU.add))
                wait(dve, t_done, g)
                dve.tensor_tensor(gated[:], yg, c.gate[:, at, :], ALU.mult).then_inc(yg_ready, 1)

            def add_norm(g):
                h = c.h[:, bass.ds(g * GROUP, GROUP), :]
                dve.wait_ge(o_done, g + 1)
                chain(dve.tensor_tensor(h_new[:], h, ps_o, ALU.add))
                dve.tensor_tensor(h, h, ps_o, ALU.add).then_inc(o_read, 1)
                for t in range(GROUP):
                    last = dve.bn_stats(stats[:, t, :], h_new[:, t, :])
                chain(last)
                touch(dve, nwt)
                for t in range(GROUP):
                    last = dve.bn_aggr(mean_var[:, t, :], stats[:, t, :])
                chain(last)
                chain(dve.tensor_scalar(var_eps[:], mean_var[:, :, 1], LN_EPS, None, ALU.add))
                inverse_sqrt(dve, chain, rstd[:], nwt[:], var_eps[:])
                wait(dve, x_done, g)
                wait(dve, stored, 32 * g)
                for t in range(GROUP):
                    last = dve.tensor_scalar(xn[:, t, :], h_new[:, t, :], mean_var[:, t, 0:1], rstd[:, t:t + 1],
                                             ALU.subtract, ALU.mult)
                last.then_inc(xn_ready, 1)
                chain(dve.memset(nwt[:], 0.0))

            dve.wait_ge(w_in, 64)
            dve.wait_ge(y_in, 16)
            norm_y(0)
            dve.wait_ge(tiles_in, 16)
            norm_y(1)
            add_norm(0)
            links = 6 + RSQRT_LINKS + 4 + 5 + RSQRT_LINKS
            with dve.Fori(1, GROUPS - 1) as i:
                chain.enter(i - 1, links)
                norm_y(i + 1)
                add_norm(i)
                chain.leave(GROUPS - 2)
            add_norm(GROUPS - 1)

            dve.wait_ge(l_done, GROUPS)
            chain(dve.tensor_copy(logits[:], ps_l))
            for t in range(TILES):
                last = dve.max(top[:, t, :], logits[:, t, :])
            chain(last)
            for t in range(TILES):
                last = dve.max_index(top_i[:, t, :], top[:, t, :], logits[:, t, :])
            chain(last)
            dve.wait_ge(no_set, 6)
            chain(dve.tensor_copy(top_f[:], top_i[:, :, 0:2]))
            all_x = lambda ap: ap.to_broadcast([P, TILES, EXPERTS])
            for w in range(2):
                chain(dve.tensor_tensor(hot[w][:], expert_no[:].unsqueeze(1).to_broadcast([P, TILES, EXPERTS]),
                                        all_x(top_f[:, :, w:w + 1]), ALU.is_equal))
            chain(dve.scalar_tensor_tensor(out=absl[:], in0=logits[:], scalar=-1.0, in1=logits[:], op0=ALU.mult, op1=ALU.max))
            for w in range(2):
                thr = all_x(top[:, :, w:w + 1])
                chain(dve.tensor_tensor(dif[:], logits[:], thr, ALU.subtract))
                dve.tensor_scalar(ex[:], dif[:], 0.0, None, ALU.min).then_inc(e_asked, 1)
                chain(dve.tensor_tensor(fac[:], absl[:], thr, ALU.max))
                chain(dve.reciprocal(fac[:], fac[:]))
                chain(dve.tensor_tensor(keep[:], dif[:], fac[:], ALU.mult))
                chain(dve.tensor_scalar(keep[:], keep[:], -2.0 * JITTER, None, ALU.is_lt))
                chain(dve.tensor_scalar(keep[:], keep[:], -1.0, 1.0, ALU.mult, ALU.add))
                if w == 1:
                    chain(dve.tensor_scalar(dif[:], hot[0][:], -1.0, 1.0, ALU.mult, ALU.add))
                    chain(dve.tensor_tensor(keep[:], keep[:], dif[:], ALU.mult))
                dve.wait_ge(e_ready, w + 1)
                chain(dve.tensor_tensor(keep[:], keep[:], ex[:], ALU.mult))
                chain(dve.tensor_reduce(den[:], keep[:], AX_X, ALU.add))
                chain(dve.reciprocal(weight[:, w, :], den[:]))

            chain(dve.tensor_tensor(chosen[:], hot[0][:], hot[1][:], ALU.add))
            dve.tensor_copy(absl[:], chosen[:]).then_inc(chosen_ready, 1)
            dve.wait_ge(ranks_done, 1)
            chain(dve.tensor_copy(rank[:], ps_rank))
            chain(dve.tensor_copy(before[0][:], ps_count))
            src = 0
            for step in (1, 2, 4, 8):
                a, b = before[src], before[1 - src]
                dve.tensor_copy(b[:, 0:step, :], a[:, 0:step, :])
                chain(dve.tensor_tensor(b[:, step:, :], a[:, step:, :], a[:, 0:TILES - step, :], ALU.add))
                src = 1 - src
            total = before[src]
            chain(dve.tensor_scalar(n_i[:], total[:, TILES - 1, :], float(NT - 1), None, ALU.add))
            chain(dve.tensor_scalar(n_i[:], n_i[:], NT.bit_length() - 1, None, ALU.logical_shift_right))
            chain(dve.tensor_copy(turns_of[:], n_i[:]))
            chain(dve.memset(start[:, 0:1], 0.0))
            for x in range(1, EXPERTS):
                chain(dve.tensor_tensor(start[:, x:x + 1], start[:, x - 1:x], turns_of[:, x - 1:x], ALU.add))
            chain(dve.tensor_tensor(le[:], start[:].unsqueeze(1).to_broadcast([P, TURNS_X, EXPERTS]),
                                    turn_no[:].unsqueeze(2).to_broadcast([P, TURNS_X, EXPERTS]), ALU.is_le))
            chain(dve.tensor_reduce(te[:], le[:], AX_X, ALU.add))
            chain(dve.tensor_scalar(te[:], te[:], -1.0, None, ALU.add))
            dve.tensor_copy(c.turn_expert[:], te[:]).then_inc(experts_ready, 1)
            chain(dve.tensor_tensor(rank[:, 1:, :], rank[:, 1:, :], total[:, 0:TILES - 1, :], ALU.add))
            chain(dve.tensor_scalar(base[:], start[:], float(NT), None, ALU.mult))
            chain(dve.tensor_tensor(rank[:], rank[:], base[:].unsqueeze(1).to_broadcast([P, TILES, EXPERTS]), ALU.add))
            for w in range(2):
                chain(dve.tensor_tensor(keep[:], rank[:], hot[w][:], ALU.mult))
                chain(dve.tensor_reduce(slot_f[:, w, :], keep[:], AX_X, ALU.add))
            chain(dve.tensor_copy(slot_i[:], slot_f[:]))
            dve.tensor_scalar(place_i[:], slot_i[:], P - 1, None, ALU.bitwise_and)
            chain(dve.tensor_scalar(tile_i[:], slot_i[:], P.bit_length() - 1, None, ALU.logical_shift_right))
            dve.tensor_copy(place[:], place_i[:])
            chain(dve.tensor_copy(tile[:], tile_i[:]))
            for w in range(2):
                dve.tensor_tensor(at_place[:, w], place_no[:].unsqueeze(1).to_broadcast([P, TILES, P]),
                                  place[:, w, :].unsqueeze(2).to_broadcast([P, TILES, P]), ALU.is_equal)
                for v in range(2):
                    last = dve.tensor_tensor(at_tile[:, w, :, v, :], tile_no[:].unsqueeze(1).to_broadcast([P, TILES, SLOT_TILES]),
                                             tile[:, w, :].unsqueeze(2).to_broadcast([P, TILES, SLOT_TILES]), ALU.is_equal)
            chain(last)
            for w in range(2):
                for v, of in enumerate((row_no[:], weight[:, w, :])):
                    last = dve.tensor_tensor(at_tile[:, w, :, v, :], at_tile[:, w, :, v, :],
                                             of.unsqueeze(2).to_broadcast([P, TILES, SLOT_TILES]), ALU.mult)
            last.then_inc(places_ready, 1)
            dve.wait_ge(slots_done, 1)
            chain(dve.tensor_scalar(taken[:], ps_slots[:, 0, :], 0.5, None, ALU.is_gt))
            dve.tensor_copy(c.weight_at[:], ps_slots[:, 1, :])
            chain(dve.tensor_scalar(taken[:], taken[:], -1.0, 1.0, ALU.mult, ALU.add))
            chain(dve.tensor_tensor(taken[:], taken[:], empty_row[:], ALU.mult))
            chain(dve.tensor_tensor(taken[:], taken[:], ps_slots[:, 0, :], ALU.add))
            chain(dve.tensor_scalar(taken[:], taken[:], -1.0, None, ALU.add))
            chain(dve.tensor_copy(c.token_at[:], taken[:]))


def ffn_stage(nc, d, c, out):
    with ExitStack() as ctx:
        sb = lambda name, shape, dt=F32: ctx.enter_context(nc.sbuf_tensor("ffn_" + name, shape, dt))
        sem = lambda name: ctx.enter_context(nc.semaphore("ffn_" + name))
        raw, raw_in = c.raw, c.raw_in
        w1, w3 = sb("w1", [P, 2, HL, KC, FF], F32R), sb("w3", [P, 2, HL, KC, FF], F32R)
        w2 = sb("w2", [P, 2, HL, FC, E], F32R)
        x_in = [sb(f"x_in{i}{t}", [P, E]) for i in range(2) for t in range(TT)]
        xT = sb("xT", [P, 2, HL, KC, NT], F32R)
        silu = sb("silu", [P, 2, GF, NT])
        hid_f = sb("hid_f", [P, 2, GF, NT])
        hid = sb("hid", [P, HL, FC, NT], F32R)
        y_out = [sb(f"y_out{i}{t}", [P, E]) for i in range(2) for t in range(TT)]
        row_in, row_out = sb("row_in", [P, 2, TT], U32), sb("row_out", [P, 2, TT], U32)
        weight = sb("weight", [P, 2, TT])
        words = sb("words", [P, 2, 2])
        ps = ctx.enter_context(nc.psum_tensor("ps_ffn", [P, 6, BANK], F32))
        ps_up = ps[:, 0:4, :].rearrange("p (b f) n -> p b f n", b=2)
        ps_y = ps[:, 4, :].rearrange("p (t e) -> p t e", t=TT)
        ps_t = ps[:, 5, :].rearrange("p (k n) -> p k n", k=KC)
        hi_done = [sem("w1_hi_done"), sem("w3_hi_done"), sem("w2_hi_done")]
        lo_done = [sem("w1_lo_done"), sem("w3_lo_done"), sem("w2_lo_done")]
        gathered = [sem("gathered0"), sem("gathered1")]
        added = [sem("added0"), sem("added1")]
        row_in_set, xt_done, x_hi_done, x_lo_done = (sem(n) for n in ("row_in_set", "xt_done", "x_hi_done", "x_lo_done"))
        up_done, silu_done, hid_f_done, hid_ready = (sem(n) for n in ("up_done", "silu_done", "hid_f_done", "hid_ready"))
        down_done, y_ready, copied, link = (sem(n) for n in ("down_done", "y_ready", "copied", "dve_link"))
        block = ctx.enter_context(nc.Block())
        parts = (w1, w3, w2)
        W1, W3, W2 = range(3)

        def turns(eng, step, chain=None, links=0):
            for j in range(3):
                step(j, j // 2, j % 2)
            pairs = (TURNS_X - 5) // 2
            with eng.Fori(1, 1 + pairs) as i:
                if chain:
                    chain.enter(i - 1, links)
                step(2 * i + 1, i, 1)
                step(2 * i + 2, i + 1, 0)
                if chain:
                    chain.leave(pairs)
            for j in range(3 + 2 * pairs, TURNS_X):
                step(j, j // 2, j % 2)

        is_turn = lambda j: not isinstance(j, int) or j < TURNS_X

        @block.sync
        def _(sp):
            with sp.Fori(1, TURNS_X) as j:
                load_expert(sp, d, c, j, lo_done)
            for par in range(2):
                sp.wait_ge(added[par], 16 * TT * ((TURNS_X + 1 - par) // 2))
            PIECES = 8
            for n in range(PIECES):
                at = slice(n * TOK // PIECES, (n + 1) * TOK // PIECES)
                sp.dma_start(out[at], d["sum_rows"][at]).then_inc(copied, 16)
            sp.wait_ge(copied, 16 * PIECES)

        @block.gpsimd
        def _(pool):
            def split_lo(n, j, par):
                pool.wait_ge(hi_done[n], j + 1)
                pool.tensor_tensor(parts[n][:, par, LO], raw[n][:], parts[n][:, par, HI], ALU.subtract).then_inc(lo_done[n], 1)

            def gather(j, par):
                pool.wait_ge(row_in_set, j + 1)
                wait(pool, xt_done, j - 1)
                pool.tensor_tensor(words[:, 0, par:par + 1], c.ident[:, 0:1], c.ident[:, 0:1], ALU.mult)
                for t in range(TT):
                    pool.indirect_dma_start(x_in[par * TT + t][:], None, d["xn_rows"],
                                            bass.IndirectOffsetOnAxis(ap=row_in[:, par, t:t + 1], axis=0)
                                            ).then_inc(gathered[par], 16)

            def add(j, half, par):
                pool.wait_ge(y_ready, j + 1)
                wait(pool, added[1 - par], 16 * TT * (half + par))
                pool.tensor_tensor(words[:, 1, par:par + 1], c.ident[:, 0:1], c.ident[:, 0:1], ALU.mult)
                for t in range(TT):
                    pool.indirect_dma_start(d["sum_rows"], bass.IndirectOffsetOnAxis(ap=row_out[:, par, t:t + 1], axis=0),
                                            y_out[par * TT + t][:], None, compute_op=ALU.add).then_inc(added[par], 16)

            def step(j, half, par):
                if is_turn(j + 1):
                    split_lo(W1, j + 1, 1 - par)
                if not isinstance(j, int) or j > 0:
                    add(j - 1, half + par - 1, 1 - par)
                if is_turn(j + 2):
                    gather(j + 2, par)
                if is_turn(j + 1):
                    split_lo(W2, j + 1, 1 - par)

            for j in range(2):
                gather(j, j)
            split_lo(W1, 0, 0)
            split_lo(W2, 0, 0)
            turns(pool, step)
            add(TURNS_X - 1, (TURNS_X - 1) // 2, (TURNS_X - 1) % 2)

        @block.tensor
        def _(pe):
            PASSES = ((HI, HI), (HI, LO), (LO, HI))

            def transposes(j, half, par):
                pe.wait_ge(gathered[par], 16 * TT * (half + 1))
                for k in range(KC):
                    for t in range(TT):
                        last = pe.transpose(ps_t[:, k, t * P:(t + 1) * P], x_in[par * TT + t][:, k * P:(k + 1) * P], c.ident[:])
                last.then_inc(xt_done, 1)

            def up(j, par, g):
                n = j * G + g
                if g == 0:
                    for q in (x_lo_done, lo_done[W1], lo_done[W3]):
                        pe.wait_ge(q, j + 1)
                if not isinstance(j, int) or n >= 2:
                    pe.wait_ge(hid_f_done, n - 1)
                for f in range(g * GF, (g + 1) * GF):
                    for m, w in enumerate((w1, w3)):
                        for k in range(KC):
                            for q, (a, b) in enumerate(PASSES):
                                last = pe.matmul(ps_up[:, g % 2, f % GF, m * NT:(m + 1) * NT], w[:, par, a, k, f * P:(f + 1) * P],
                                                 xT[:, par, b, k, :], start=(k == 0 and q == 0), stop=(k == KC - 1 and q == 2))
                last.then_inc(up_done, 1)

            def down(j, par):
                pe.wait_ge(lo_done[W2], j + 1)
                pe.wait_ge(hid_ready, (j + 1) * G)
                wait(pe, y_ready, j)
                for t in range(TT):
                    for f in range(FC):
                        for q, (a, b) in enumerate(PASSES):
                            last = pe.matmul(ps_y[:, t, :], hid[:, a, f, t * P:(t + 1) * P], w2[:, par, b, f, :],
                                             start=(f == 0 and q == 0), stop=(f == FC - 1 and q == 2))
                last.then_inc(down_done, 1)

            def step(j, half, par):
                up(j, par, 0)
                if not isinstance(j, int) or j > 0:
                    down(j - 1, 1 - par)
                up(j, par, 1)
                if is_turn(j + 1):
                    transposes(j + 1, half + par, 1 - par)
                for g in range(2, G):
                    up(j, par, g)

            transposes(0, 0, 0)
            turns(pe, step)
            down(TURNS_X - 1, (TURNS_X - 1) % 2)

        @block.scalar
        def _(act):
            def split_hi(n, j, par):
                act.wait_ge(raw_in[n], 16 * (j + 1))
                if n == W2:
                    wait(act, down_done, j - 1)
                act.copy(parts[n][:, par, HI], raw[n][:]).then_inc(hi_done[n], 1)

            def x_hi(j, par):
                act.wait_ge(xt_done, j + 1)
                act.copy(xT[:, par, HI], ps_t).then_inc(x_hi_done, 1)

            def silus(j, g):
                n = j * G + g
                act.wait_ge(up_done, n + 1)
                if not isinstance(j, int) or n >= 2:
                    act.wait_ge(hid_f_done, n - 1)
                act.activation(silu[:, g % 2], ps_up[:, g % 2, :, 0:NT], ACT.Silu, bias=0.0).then_inc(silu_done, 1)

            def step(j, half, par):
                silus(j, 0)
                if is_turn(j + 1):
                    split_hi(W3, j + 1, 1 - par)
                    split_hi(W1, j + 1, 1 - par)
                silus(j, 1)
                if is_turn(j + 1):
                    x_hi(j + 1, 1 - par)
                    split_hi(W2, j + 1, 1 - par)
                silus(j, 2)
                silus(j, 3)

            split_hi(W1, 0, 0)
            split_hi(W3, 0, 0)
            x_hi(0, 0)
            split_hi(W2, 0, 0)
            turns(act, step)

        @block.vector
        def _(dve):
            chain = Chain(dve, link)

            def w3_lo(j, par):
                dve.wait_ge(hi_done[W3], j + 1)
                dve.tensor_tensor(w3[:, par, LO], raw[W3][:], w3[:, par, HI], ALU.subtract).then_inc(lo_done[W3], 1)

            def x_lo(j, par):
                dve.wait_ge(x_hi_done, j + 1)
                dve.tensor_tensor(xT[:, par, LO], ps_t, xT[:, par, HI], ALU.subtract).then_inc(x_lo_done, 1)

            def set_rows_in(j, par):
                dve.tensor_copy(row_in[:, par, :], c.token_at[:, bass.ds(j * TT, TT)]).then_inc(row_in_set, 1)

            def gate_up(j, g):
                dve.wait_ge(silu_done, j * G + g + 1)
                dve.tensor_tensor(hid_f[:, g % 2], ps_up[:, g % 2, :, NT:2 * NT], silu[:, g % 2], ALU.mult).then_inc(hid_f_done, 1)

            def split_hid(j, g):
                at = slice(g * GF, (g + 1) * GF)
                dve.wait_ge(hid_f_done, j * G + g + 1)
                chain(dve.tensor_copy(hid[:, HI, at], hid_f[:, g % 2]))
                dve.tensor_tensor(hid[:, LO, at], hid_f[:, g % 2], hid[:, HI, at], ALU.subtract).then_inc(hid_ready, 1)

            def results(j, half, par):
                dve.wait_ge(down_done, j + 1)
                wait(dve, added[par], 16 * TT * half)
                dve.tensor_copy(row_out[:, par, :], c.token_at[:, bass.ds(j * TT, TT)])
                chain(dve.tensor_copy(weight[:, par, :], c.weight_at[:, bass.ds(j * TT, TT)]))
                for t in range(TT):
                    last = dve.tensor_scalar(y_out[par * TT + t][:], ps_y[:, t, :], weight[:, par, t:t + 1], None, ALU.mult)
                last.then_inc(y_ready, 1)

            def step(j, half, par):
                gate_up(j, 0)
                if is_turn(j + 1):
                    w3_lo(j + 1, 1 - par)
                if is_turn(j + 2):
                    set_rows_in(j + 2, par)
                if not isinstance(j, int) or j > 0:
                    results(j - 1, half + par - 1, 1 - par)
                split_hid(j, 0)
                gate_up(j, 1)
                split_hid(j, 1)
                if is_turn(j + 1):
                    x_lo(j + 1, 1 - par)
                for g in (2, 3):
                    gate_up(j, g)
                    split_hid(j, g)

            for j in range(2):
                set_rows_in(j, j)
            w3_lo(0, 0)
            x_lo(0, 0)
            turns(dve, step, chain, 2 * (G + 1))
            j = TURNS_X - 1
            results(j, j // 2, j % 2)


class Kept:
    pass


def audio_tower(nc, d):
    rows = lambda name, *shape: nc.dram_tensor(name, list(shape), F32, kind="Internal").ap()
    d["scan"] = rows("scan_rows", TOK + 1, ARRAYS, E)
    d["y"] = rows("y_rows", TOK, E)
    d["xn_rows"] = rows("xn_rows", ROWS, E)
    d["sum_rows"] = rows("sum_rows", ROWS, E)
    c = Kept()
    with ExitStack() as ctx:
        sb = lambda name, shape, dt=F32: ctx.enter_context(nc.sbuf_tensor(name, shape, dt))
        c.ident = sb("ident", [P, P])
        c.turn_expert = sb("turn_expert", [P, TURNS_X], I32)
        c.token_at = sb("token_at", [P, SLOT_TILES], U32)
        c.weight_at = sb("weight_at", [P, SLOT_TILES])
        c.raw = [sb("raw1", [P, KC, FF]), sb("raw3", [P, KC, FF]), sb("raw2", [P, FC, E])]
        c.raw_in = [ctx.enter_context(nc.semaphore(n)) for n in ("raw1_in", "raw3_in", "raw2_in")]
        with ExitStack() as inner:
            keep = lambda name, shape: inner.enter_context(nc.sbuf_tensor(name, shape, F32))
            c.h = keep("h", [P, TILES, E])
            c.xnT = keep("xnT", [P, KC, TOK])
            c.mix_w = {name: keep("mix_" + name, shape) for name, _, shape in MIX_WEIGHTS}
            c.mix_w_in = inner.enter_context(nc.semaphore("mix_w_in"))
            tok_stage(nc, d, c)
            c.gate = keep("gate", [P, TILES, E])
            c.bonus = keep("bonus", [P, TILES, E])
            mix_stage(nc, d, c)
            scan_stage(nc, d, c)
            out_stage(nc, d, c)
            if "dbg_h" in d:
                dbg(nc, d, c)
        ffn_stage(nc, d, c, d["out"].rearrange("b t e -> (b t) e"))


def layout(i):
    g = lambda n: np.asarray(i[n])
    t = lambda a: np.ascontiguousarray(np.swapaxes(a, -1, -2))
    z = lambda *s: np.zeros(s, np.float32)
    tok, att, ffn = "L0_tok_", "L0_attn_", "L0_ffn_"
    a = lambda n: g(att + n)
    w_a1T = np.concatenate([t(a("decay_w1")), t(a("aaa_w1")), z(256, 16), t(a("ma_w1")), z(256, 16)], 1)
    w_a2 = np.concatenate([
        np.concatenate([a("decay_w2"), z(64, 512)], 1),
        np.concatenate([z(16, 256), a("aaa_w2"), z(16, 256)], 1), z(16, 768),
        np.concatenate([z(16, 512), a("ma_w2")], 1),
        np.concatenate([a("time_decay"), a("time_aaaaa"), a("time_misc_a")])[None], z(15, 768)], 0)
    w_b1T = np.concatenate([t(a("kkk_w1")), z(256, 16), t(a("mk_w1")), z(256, 16)], 1)
    w_b2 = np.concatenate([
        np.concatenate([a("kkk_w2"), z(16, 256)], 1), z(16, 512),
        np.concatenate([z(16, 256), a("mk_w2")], 1),
        np.concatenate([z(256), a("time_misc_k")])[None], z(15, 512)], 0)
    ones = z(128, 2)
    ones[112, 0] = 1.0
    ones[48, 1] = 1.0
    maa = np.concatenate([t(a("time_maa").reshape(4, 256)), a("time_maa_x")[:, None]], 1)
    c = np.ascontiguousarray
    return {
        "x": g("x"), "xT": t(g("x")), "wqT": t(g(tok + "Wq")), "wkT": t(g(tok + "Wk")), "wv": g(tok + "Wv"),
        "gamma": g(tok + "gamma"), "beta": g(tok + "beta"),
        "maa": c(maa), "maa_w1T": t(a("maa_w1")), "maa_w2": a("maa_w2").reshape(128, 256),
        "w_rT": t(a("Wr")), "w_kT": t(a("Wk")), "w_vT": t(a("Wv")), "w_oT": t(a("Wo")),
        "w_a1T": c(w_a1T), "w_a2": c(w_a2), "w_b1T": c(w_b1T), "w_b2": c(w_b2), "a_bias": ones,
        "w_g1T": t(a("gate_w1")), "w_g2": a("gate_w2"), "faaaa": a("time_faaaa"),
        "ln_w": a("ln_w"), "ln_b": a("ln_b"),
        "gate_w": g(ffn + "gate_w"), "w1": g(ffn + "w1"), "w2": g(ffn + "w2"), "w3": g(ffn + "w3"),
    }


def kernel(**inputs):
    from concourse import bacc
    from concourse.bass_utils import run_bass_kernel_spmd

    nc = bacc.Bacc("TRN2", target_bir_lowering=False, num_devices=1)
    arrays = layout(inputs)
    d = {name: nc.dram_tensor(f"in_{name}", a.shape, mybir.dt.from_np(a.dtype), kind="ExternalInput").ap()
         for name, a in arrays.items()}
    d["out"] = nc.dram_tensor("out_0", (B, T, E), F32, kind="ExternalOutput").ap()
    audio_tower(nc, d)
    ran = run_bass_kernel_spmd(nc, [{f"in_{name}": a for name, a in arrays.items()}], core_ids=[0])
    return ran.results[0]["out_0"]
```

```python
from contextlib import ExitStack

import numpy as np

import concourse.bass as bass
from concourse import mybir

F32 = mybir.dt.float32
F32R = mybir.dt.float32r
ALU = mybir.AluOpType
ACT = mybir.ActivationFunctionType
AX_X = mybir.AxisListType.X

P = 128
B, N, E = 32, 256, 256
KC = E // P
STRIDE = 4
T = N // STRIDE
TOK = B * T
TILES = TOK // P
LN_EPS = 1e-5
BANK = 512


def wait(eng, sem, count):
    if isinstance(count, int) and count <= 0:
        return
    eng.wait_ge(sem, count)


class Chain:

    def __init__(self, eng, sem):
        self.eng, self.sem, self.done, self.turns = eng, sem, 0, 0

    def __call__(self, ins):
        self.done += 1
        ins.then_inc(self.sem, 1)
        self.eng.wait_ge(self.sem, self.turns + self.done)

    def enter(self, turn, per_turn):
        self.before, self.per_turn = self.done, per_turn
        self.turns = turn * per_turn

    def leave(self, turns):
        assert self.done - self.before == self.per_turn, (self.done - self.before, self.per_turn)
        self.turns = 0
        self.done = self.before + turns * self.per_turn


def newton(dve, chain, y, t, v):
    chain(dve.tensor_tensor(t, y, y, ALU.mult))
    chain(dve.tensor_tensor(t, t, v, ALU.mult))
    chain(dve.tensor_scalar(t, t, -0.5, 1.5, ALU.mult, ALU.add))
    chain(dve.tensor_tensor(y, y, t, ALU.mult))


def inverse_sqrt(dve, chain, y, t, v):
    i32 = mybir.dt.int32
    chain(dve.tensor_scalar(t.bitcast(i32), v.bitcast(i32), 1, None, ALU.logical_shift_right))
    chain(dve.tensor_scalar(y.bitcast(i32), t.bitcast(i32), -1.0, float(0x5F3759DF), ALU.mult, ALU.add))
    for _ in range(3):
        newton(dve, chain, y, t, v)


RSQRT_LINKS = 14


def touch(dve, tile):
    return dve.memset(tile[:, 0:1], 0.0)


def tok_stage(nc, d, c):
    with ExitStack() as ctx:
        sb = lambda name, shape: ctx.enter_context(nc.sbuf_tensor("tok_" + name, shape, F32))
        sem = lambda name: ctx.enter_context(nc.semaphore(name))
        wq_t = sb("wq_t", [P, KC, E])
        wk_t = sb("wk_t", [P, KC, E])
        wv = sb("wv", [P, KC, E])
        wqk = sb("wqk", [P, KC, E])
        gamma = sb("gamma", [P, E])
        beta = sb("beta", [P, E])
        x_in = sb("x_in", [P, 2, KC, E])
        xT_in = sb("xT_in", [P, 2, KC, N])
        g_sb = sb("g_sb", [P, 2, KC, N])
        probs = sb("probs", [P, 2, 2, N])
        pool_w = sb("pool_w", [P, P // STRIDE])
        pool_r = sb("pool_r", [P, 2, 2, P // STRIDE])
        pooled = sb("pooled", [P, 2, 2, T])
        px_sb = sb("px_sb", [P, KC, 2, T])
        mx = sb("mx", [P, 2, 2])
        neg_mx = sb("neg_mx", [P, 2, 2])
        row_sum = sb("row_sum", [P, 2, 2])
        row_inv = sb("row_inv", [P, 2, 2])
        stats = sb("stats", [P, 6])
        mean_var = sb("mean_var", [P, 2, 2])
        var_eps = sb("var_eps", [P, 2])
        rstd = sb("rstd", [P, 2])
        nwt = sb("nwt", [P, 2])
        z = sb("z", [P, E])
        attn_n = sb("attn_n", [P, E])
        h_tmp = sb("h_tmp", [P, E])
        xn = sb("xn", [P, E])
        ps = ctx.enter_context(nc.psum_tensor("ps_tok", [P, 8, BANK], F32))
        ps_g = [ps[:, b, :].rearrange("p (c n) -> p c n", c=KC) for b in (0, 1)]
        ps_s = [ps[:, 2 + b, :].rearrange("p (c n) -> p c n", c=2) for b in (0, 1)]
        ps_pool = ps[:, 4, 0:2 * T].rearrange("p (c t) -> p c t", c=2)
        ps_px = ps[:, 5, 0:KC * T].rearrange("p (c t) -> p c t", c=KC)
        ps_attn = ps[:, 6, 0:E]
        ps_tr = ps[:, 7, 0:KC * P].rearrange("p (c t) -> p c t", c=KC)

        w_in = sem("tok_wq_wk_in")
        wv_in = sem("tok_wv_gamma_beta_in")
        xT_loaded = [sem("xT_loaded0"), sem("xT_loaded1")]
        x_loaded = [sem("x_loaded0"), sem("x_loaded1")]
        pw_set = sem("pool_w_set")
        wqk_done = sem("wqk_done")
        wqk_copied = sem("wqk_copied")
        g_done = sem("g_done")
        g_copied = sem("g_copied")
        s_done = sem("s_done")
        nb_ready = sem("neg_max_ready")
        exp_done = sem("exp_done")
        er_ready = sem("pool_r_ready")
        pool_done = sem("pool_done")
        pool_copied = sem("pool_copied")
        px_done = sem("px_done")
        px_copied = sem("px_copied")
        attn_done = sem("attn_done")
        attn_read = sem("attn_read")
        xn_ready = sem("xn_ready")
        tr_done = sem("tr_done")
        tr_copied = sem("tr_copied")
        dve_link = sem("tok_dve_link")
        id_set = sem("ident_set")
        block = ctx.enter_context(nc.Block())

        FIRST, LAST = 5, B + 5
        HALF = (B - 1 - FIRST) // 2

        def steps(eng, step, chain=None, links=0):
            for n in range(FIRST):
                step(n, n // 2, n % 2)
            with eng.Fori(0, HALF) as i:
                if chain:
                    chain.enter(i, links)
                step(2 * i + FIRST, i + FIRST // 2, 1, inner=True)
                step(2 * i + FIRST + 1, i + FIRST // 2 + 1, 0, inner=True)
                if chain:
                    chain.leave(HALF)
            for n in range(B - 1, LAST):
                step(n, n // 2, n % 2)

        @block.sync
        def _(sp):
            sp.dma_start(wq_t[:], d["wqT"].rearrange("(c p) e -> p c e", p=P)).then_inc(w_in, 16)
            sp.dma_start(wk_t[:], d["wkT"].rearrange("(c p) e -> p c e", p=P)).then_inc(w_in, 16)

            def load_xT(n, par):
                wait(sp, s_done, n - 1)
                sp.dma_start(xT_in[:, par, :, :], d["xT"][bass.ds(n, 1)].rearrange("o (c p) n -> p (o c) n", p=P)
                             ).then_inc(xT_loaded[par], 16)

            def load_x(n, par):
                if not isinstance(n, int):
                    sp.wait_ge(px_done, n - 1)
                sp.dma_start(x_in[:, par, :, :], d["x"][bass.ds(n, 1)].rearrange("o (c p) e -> p (o c) e", p=P)
                             ).then_inc(x_loaded[par], 16)

            load_xT(0, 0)
            load_xT(1, 1)
            load_x(0, 0)
            sp.dma_start(wv[:], d["wv"].rearrange("(c p) e -> p c e", p=P)).then_inc(wv_in, 16)
            sp.dma_start(gamma[:], d["gamma"].partition_broadcast(P)).then_inc(wv_in, 16)
            sp.dma_start(beta[:], d["beta"].partition_broadcast(P)).then_inc(wv_in, 16)
            load_x(1, 1)
            with sp.Fori(1, B // 2) as i:
                for load in (load_xT, load_x):
                    for par in range(2):
                        load(2 * i + par, par)
            for name, src, shape in MIX_WEIGHTS:
                of = d[src]
                if src == "faaaa":
                    of = of.partition_broadcast(P)
                elif len(shape) == 3:
                    of = of.rearrange("(c p) e -> p c e", p=P)
                sp.dma_start(c.mix_w[name][:], of).then_inc(c.mix_w_in, 16)

        @block.gpsimd
        def _(pool):
            pool.memset(pool_w[:], 1.0 / STRIDE).then_inc(pw_set, 1)
            pool.wait_ge(pw_set, 1)
            pool.affine_select(out=pool_w[:], in_=pool_w[:], compare_op=ALU.is_ge, fill=0.0, base=0,
                               pattern=[[-STRIDE, P // STRIDE]], channel_multiplier=1).then_inc(pw_set, 1)
            pool.wait_ge(pw_set, 2)
            pool.affine_select(out=pool_w[:], in_=pool_w[:], compare_op=ALU.is_ge, fill=0.0, base=STRIDE - 1,
                               pattern=[[STRIDE, P // STRIDE]], channel_multiplier=-1).then_inc(pw_set, 1)
            pool.memset(c.ident[:], 0.0).then_inc(id_set, 1)
            pool.wait_ge(id_set, 1)
            pool.affine_select(out=c.ident[:], in_=c.ident[:], compare_op=ALU.not_equal, fill=1.0, base=0,
                               pattern=[[-1, P]], channel_multiplier=1).then_inc(id_set, 1)

        @block.tensor
        def _(pe):
            pe.wait_ge(w_in, 32)
            for ec in range(KC):
                for k in range(KC):
                    last = pe.matmul(ps_s[0][:, ec, :], wq_t[:, k, ec * P:(ec + 1) * P], wk_t[:, k, :],
                                     start=(k == 0), stop=(k == KC - 1))
            last.then_inc(wqk_done, 1)

            def g_mm(n, half, par):
                pe.wait_ge(xT_loaded[par], 16 * (half + 1))
                wait(pe, g_copied, n - 1)
                for ec in range(KC):
                    for k in range(KC):
                        last = pe.matmul(ps_g[par][:, ec, :], wqk[:, k, ec * P:(ec + 1) * P],
                                         xT_in[:, par, k, :], start=(k == 0), stop=(k == KC - 1))
                last.then_inc(g_done, 1)

            def s_mm(n, par):
                pe.wait_ge(g_copied, n + 1)
                wait(pe, exp_done, n - 1)
                for qc in range(2):
                    for k in range(KC):
                        last = pe.matmul(ps_s[par][:, qc, :], g_sb[:, par, k, qc * P:(qc + 1) * P],
                                         xT_in[:, par, k, :], start=(k == 0), stop=(k == KC - 1))
                last.then_inc(s_done, 1)

            def pool_mm(n, par):
                pe.wait_ge(er_ready, n + 1)
                wait(pe, pool_copied, n)
                half_t = T // 2
                for kc in range(2):
                    for qc in range(2):
                        last = pe.matmul(ps_pool[:, kc, qc * half_t:(qc + 1) * half_t],
                                         probs[:, par, qc, kc * P:(kc + 1) * P], pool_r[:, par, qc, :],
                                         start=True, stop=True)
                last.then_inc(pool_done, 1)

            def px_mm(n, half, par):
                pe.wait_ge(x_loaded[par], 16 * (half + 1))
                pe.wait_ge(pool_copied, n + 1)
                wait(pe, px_copied, n)
                for ec in range(KC):
                    for k in range(2):
                        last = pe.matmul(ps_px[:, ec, :], x_in[:, par, k, ec * P:(ec + 1) * P],
                                         pooled[:, par, k, :], start=(k == 0), stop=(k == 1))
                last.then_inc(px_done, 1)

            def attn_mm(p):
                pe.wait_ge(px_copied, 2 * p + 2)
                wait(pe, attn_read, p)
                for k in range(KC):
                    last = pe.matmul(ps_attn, px_sb[:, k, :, :].rearrange("p b t -> p (b t)"), wv[:, k, :],
                                     start=(k == 0), stop=(k == KC - 1))
                last.then_inc(attn_done, 1)

            def tr_mm(p):
                pe.wait_ge(xn_ready, p + 1)
                for k in range(KC):
                    last = pe.transpose(ps_tr[:, k, :], xn[:, k * P:(k + 1) * P], c.ident[:])
                last.then_inc(tr_done, 1)

            pe.wait_ge(wqk_copied, 1)
            g_mm(0, 0, 0)
            pe.wait_ge(wv_in, 48)
            pe.wait_ge(id_set, 2)

            def step(n, half, par, inner=False):
                if inner or n < B:
                    s_mm(n, par)
                if inner or 1 <= n <= B:
                    pool_mm(n - 1, 1 - par)
                if par == 0 and (inner or n >= 6):
                    tr_mm(half - 3)
                if inner or n + 1 < B:
                    g_mm(n + 1, half + par, 1 - par)
                if inner or 1 <= n <= B:
                    px_mm(n - 1, half + par - 1, 1 - par)
                if par == 0 and (inner or 2 <= n <= B):
                    attn_mm(half - 1)

            steps(pe, step)

        @block.scalar
        def _(act):
            def copy_g(n, par):
                act.wait_ge(g_done, n + 1)
                wait(act, s_done, n - 1)
                act.copy(g_sb[:, par, :, :], ps_g[par]).then_inc(g_copied, 1)

            def copy_pooled(n, par):
                act.wait_ge(pool_done, n + 1)
                wait(act, px_done, n - 1)
                act.copy(pooled[:, par, :, :], ps_pool).then_inc(pool_copied, 1)

            def exps(n, par):
                act.wait_ge(nb_ready, n + 1)
                wait(act, pool_done, n - 1)
                act.activation(probs[:, par, 0, :], ps_s[par][:, 0, :], ACT.Exp, bias=neg_mx[:, par, 0:1],
                               scale=float(E) ** -0.5, accum_out=row_sum[:, par, 0:1])
                act.activation(probs[:, par, 1, :], ps_s[par][:, 1, :], ACT.Exp, bias=neg_mx[:, par, 1:2],
                               scale=float(E) ** -0.5, accum_out=row_sum[:, par, 1:2]).then_inc(exp_done, 1)

            def step(n, half, par, inner=False):
                if inner or 1 <= n <= B:
                    copy_pooled(n - 1, 1 - par)
                if inner or n < B:
                    exps(n, par)
                if inner or n + 1 < B:
                    copy_g(n + 1, 1 - par)
                if inner or 1 <= n <= B:
                    act.wait_ge(px_done, n)
                    if par == 1:
                        wait(act, attn_done, half)
                    act.copy(px_sb[:, :, 1 - par, :], ps_px).then_inc(px_copied, 1)

            act.wait_ge(g_done, 1)
            act.copy(g_sb[:, 0, :, :], ps_g[0]).then_inc(g_copied, 1)
            steps(act, step)

        @block.vector
        def _(dve):
            chain = Chain(dve, dve_link)
            dve.wait_ge(wqk_done, 1)
            dve.tensor_copy(wqk[:], ps_s[0]).then_inc(wqk_copied, 1)
            chain(dve.memset(var_eps[:], 1.0))
            dve.wait_ge(pw_set, 3)
            dve.wait_ge(wv_in, 48)

            def row_max(n, par):
                dve.wait_ge(s_done, n + 1)
                chain(dve.tensor_reduce(mx[:, par, :], ps_s[par], AX_X, ALU.max))
                dve.tensor_scalar(neg_mx[:, par, :], mx[:, par, :], -float(E) ** -0.5, None,
                                  ALU.mult).then_inc(nb_ready, 1)

            def pool_weights(n, par):
                dve.wait_ge(exp_done, n + 1)
                wait(dve, pool_done, n - 1)
                chain(dve.reciprocal(row_inv[:, par, :], row_sum[:, par, :]))
                dve.tensor_scalar(pool_r[:, par, 0, :], pool_w[:], row_inv[:, par, 0:1], None, ALU.mult)
                dve.tensor_scalar(pool_r[:, par, 1, :], pool_w[:], row_inv[:, par, 1:2], None,
                                  ALU.mult).then_inc(er_ready, 1)

            def moments(w, src):
                chain(dve.bn_stats(stats[:], src))
                touch(dve, nwt)
                chain(dve.bn_aggr(mean_var[:, w, :], stats[:]))
                chain(dve.tensor_scalar(var_eps[:, w:w + 1], mean_var[:, w, 1:2], LN_EPS, None, ALU.add))

            def norms(p, first=True, second=True):
                inverse_sqrt(dve, chain, rstd[:], nwt[:], var_eps[:])
                if first:
                    dve.tensor_scalar(attn_n[:], ps_attn, mean_var[:, 0, 0:1], rstd[:, 0:1], ALU.subtract,
                                      ALU.mult).then_inc(attn_read, 1)
                if second:
                    dve.tensor_scalar(xn[:], z[:], mean_var[:, 1, 0:1], rstd[:, 1:2], ALU.subtract,
                                      ALU.mult).then_inc(xn_ready, 1)

            def affine(p):
                dve.wait_ge(attn_read, p + 1)
                chain(dve.tensor_tensor(h_tmp[:], attn_n[:], gamma[:], ALU.mult))
                chain(dve.tensor_tensor(z[:], h_tmp[:], beta[:], ALU.add))
                moments(1, z[:])
                dve.tensor_tensor(c.h[:, bass.ds(p, 1), :].rearrange("p o e -> p (o e)"), h_tmp[:], beta[:], ALU.add)

            def copy_xnT(p):
                dve.wait_ge(tr_done, p + 1)
                dve.tensor_scalar(c.xnT[:, :, bass.ds(p * P, P)], ps_tr, 1.0, None, ALU.mult).then_inc(tr_copied, 1)

            def step(n, half, par, inner=False):
                if inner or n < B:
                    row_max(n, par)
                if inner or n < B:
                    pool_weights(n, par)
                if par == 1 and (inner or n >= 3):
                    norms(half - 1, first=inner or n <= B + 1, second=inner or n >= 5)
                if par == 0 and (inner or n >= 6):
                    copy_xnT(half - 3)
                if par == 0 and (inner or 4 <= n <= B + 2):
                    affine(half - 2)
                if par == 0 and (inner or 2 <= n <= B):
                    dve.wait_ge(attn_done, half)
                    moments(0, ps_attn)

            steps(dve, step, chain, 2 + 2 + RSQRT_LINKS + 2 + 2 * 3)


SL = 256
SLICES = TOK // SL
ST = SL // P
SB = SL // T
HEADS, HS = 16, 16
LOW_D, LOW = 64, 16
ARRAYS = 5
SCAN_Q, SCAN_A, SCAN_B, SCAN_K, SCAN_V = ROW_Q, ROW_A, ROW_B, ROW_K, ROW_V = range(ARRAYS)
TINY = 1e-24


RATE = float(np.exp(-0.5))
MIX_WEIGHTS = [("maa", "maa", [P, KC, 5]), ("maa_w1", "maa_w1T", [P, KC, P]), ("w_a1", "w_a1T", [P, KC, P]),
               ("w_b1", "w_b1T", [P, KC, 64]), ("w_g1", "w_g1T", [P, KC, P]), ("w_r", "w_rT", [P, KC, E]),
               ("w_k", "w_kT", [P, KC, E]), ("w_v", "w_vT", [P, KC, E]), ("maa_w2", "maa_w2", [P, E]),
               ("w_a2", "w_a2", [P, 3 * E]), ("a_bias", "a_bias", [P, 2]), ("w_b2", "w_b2", [64, 2 * E]),
               ("w_g2", "w_g2", [P, E]), ("faaaa", "faaaa", [P, E])]


def mix_stage(nc, d, c):
    with ExitStack() as ctx:
        sb = lambda name, shape: ctx.enter_context(nc.sbuf_tensor("mix_" + name, shape, F32))
        sem = lambda name: ctx.enter_context(nc.semaphore("mix_" + name))
        maa, maa_w1, w_a1, w_b1, w_g1, w_r, w_k, w_v, maa_w2, w_a2, a_bias, w_b2, w_g2, faaaa = (
            c.mix_w[n] for n, _, _ in MIX_WEIGHTS)
        xx = sb("xx", [P, KC, SL])
        mix = sb("mix", [P, KC, SL])
        lo1 = sb("lo1", [P, SL])
        xm = sb("xm", [P, 4, KC, SL])
        xm_tmp = sb("xm_tmp", [P, 2, SL])
        hid_a = sb("hid_a", [P, SL])
        hid_g = sb("hid_g", [P, SL])
        hid_b = sb("hid_b", [64, SL])

        scan = sb("scan", [P, 2, ST, ARRAYS - 1, E])
        q_raw = sb("q_raw", [P, 2, ST, E])
        v_raw = sb("v_raw", [P, 2, ST, E])
        sums = sb("sums", [P, 2, ST, E])
        cum = sb("cum", [P, 3, ST, E])
        tri = sb("tri", [P, 2, P])
        k_raw = sb("k_raw", [P, 2, ST, E])
        kk = sb("kk", [P, 2, ST, E])
        zd = sb("zd", [P, 2, ST, E])
        za_sig = sb("za_sig", [P, 2, ST, 2, E])
        mam_k = sb("mam_k", [P, 2, ST, 2, E])
        t0 = sb("t0", [P, ST, E])
        t1 = sb("t1", [P, ST, E])
        az = sb("az", [P, ST, E])
        mn = sb("mn", [P, ST, E])
        k2 = sb("k2", [P, ST, E])
        ls = sb("ls", [P, ST, E])
        b_raw = sb("b_raw", [P, ST, E])
        wm = sb("wm", [P, ST, E])
        ss = sb("ss", [P, ST * HEADS])
        rn = sb("rn", [P, ST * HEADS])
        rt = sb("rt", [P, ST * HEADS])
        rk = sb("rk", [P, ST * HEADS])

        ps = ctx.enter_context(nc.psum_tensor("ps_mix", [P, 8, BANK], F32))
        ps_rg, ps_kv, ps_kkk, ps_za, ps_mm = (ps[:, b, :] for b in range(5))
        pc = [ps[:, b, :].rearrange("p (c n) -> p c n", c=KC) for b in (5, 6, 7)]
        ps_lo1, ps_hb = pc[0], pc[0]
        ps_lo2 = [pc[1], pc[2], pc[0], pc[1]]
        ps_hag = pc[2]

        w_in = c.mix_w_in
        mix_ready, lo1_done, lo1_act, lo2_done, xm_ready = (sem(n) for n in ("mix_ready", "lo1_done", "lo1_act", "lo2_done", "xm_ready"))
        hag_done, hag_act, hb_done, hb_act = (sem(n) for n in ("hag_done", "hag_act", "hb_done", "hb_act"))
        rg_done, kv_done, kkk_done, z_done = (sem(n) for n in ("rg_done", "kv_done", "kkk_done", "z_done"))
        rg_read, kv_read, z_read, kk_ready = (sem(n) for n in ("rg_read", "kv_read", "z_read", "kk_ready"))
        az_ready, ls_ready, wm_ready, wide_done = (sem(n) for n in ("az_ready", "ls_ready", "wm_ready", "wide_done"))
        scan_out = [sem("scan_out0"), sem("scan_out1")]
        dve_link, act_link = sem("dve_link"), sem("act_link")
        zeros = sb("zeros", [ARRAYS - 1, E])
        zero_set, tail_out, tri_set = sem("zero_set"), sem("tail_out"), sem("tri_set")
        cum_done, cum_read, decay_ready = sem("cum_done"), sem("cum_read"), sem("decay_ready")
        k3_ready, scan_ready, v_out = sem("k3_ready"), sem("scan_ready"), [sem("v_out0"), sem("v_out1")]
        ps_cum = [ps[:, b, :].rearrange("p (t e) -> p t e", t=ST) for b in (6, 7)]
        STORE = 16 * 2
        block = ctx.enter_context(nc.Block())
        LOOP = SLICES // 2 - 2

        def slices(eng, first, turn, last, chain=None, links=0):
            first()
            turn(0, 0, 0, has_prev=False)
            turn(1, 0, 1)
            with eng.Fori(1, LOOP + 1) as i:
                if chain:
                    chain.enter(i - 1, links)
                turn(2 * i, i, 0)
                turn(2 * i + 1, i, 1)
                if chain:
                    chain.leave(LOOP)
            turn(SLICES - 2, SLICES // 2 - 1, 0)
            turn(SLICES - 1, SLICES // 2 - 1, 1, has_next=False)
            last()

        @block.sync
        def _(sp):
            sp.wait_ge(zero_set, 1)
            sp.dma_start(d["scan"][TOK:TOK + 1, ROW_A:, :].rearrange("o m e -> (o m) e"), zeros[:]).then_inc(tail_out, 16)

            rows = lambda first, a, b, s: d["scan"][first:first + TOK, a:b, :].rearrange(
                "(s t p) m e -> s p t (m e)", p=P, t=ST)[bass.ds(s, 1)].rearrange("o p t f -> (o p) t f")

            def store_v(s, par):
                sp.wait_ge(kv_read, ST * (s + 1))
                sp.dma_start(rows(0, ROW_V, ROW_V + 1, s), v_raw[:, par]).then_inc(v_out[par], 16)

            def store(s, par):
                sp.wait_ge(scan_ready, s + 1)
                sp.dma_start(rows(1, ROW_Q, ROW_Q + 1, s), scan[:, par, :, SCAN_Q, :]).then_inc(scan_out[par], 16)
                sp.dma_start(rows(0, ROW_A, ROW_K + 1, s), scan[:, par, :, SCAN_A:, :].rearrange("p t m e -> p t (m e)")
                             ).then_inc(scan_out[par], 16)

            store_v(0, 0)
            store_v(1, 1)
            store(0, 0)
            with sp.Fori(1, SLICES // 2) as i:
                store_v(2 * i, 0)
                store(2 * i - 1, 1)
                store_v(2 * i + 1, 1)
                store(2 * i, 0)
            store(SLICES - 1, 1)
            for q in scan_out:
                sp.wait_ge(q, STORE * (SLICES // 2))
            for q in v_out:
                sp.wait_ge(q, 16 * (SLICES // 2))
            sp.wait_ge(tail_out, 16)

        @block.gpsimd
        def _(pool):
            pool.memset(zeros[:], 0.0).then_inc(zero_set, 1)
            pool.memset(tri[:], 1.0).then_inc(tri_set, 1)
            pool.wait_ge(tri_set, 1)
            for w in range(2):
                pool.affine_select(out=tri[:, w, :], in_=tri[:, w, :], compare_op=ALU.is_ge, fill=0.0, base=-w,
                                   pattern=[[1, P]], channel_multiplier=-1).then_inc(tri_set, 1)
            pool.wait_ge(tri_set, 3)
            for w in range(2):
                pool.memset(tri[0:T, w, T:P], 0.0).then_inc(tri_set, 1)

            def products(s, half, par):
                pool.wait_ge(k3_ready, s + 1)
                wait(pool, scan_out[par], STORE * half)
                pool.tensor_tensor(scan[:, par, :, SCAN_Q, :], q_raw[:, par], cum[:, 0], ALU.mult)
                pool.tensor_tensor(scan[:, par, :, SCAN_K, :], k2[:], cum[:, 1], ALU.mult)
                pool.tensor_tensor(scan[:, par, :, SCAN_B, :], b_raw[:], cum[:, 1], ALU.mult)
                pool.tensor_tensor(scan[:, par, :, SCAN_A, :], kk[:, par], cum[:, 2], ALU.mult).then_inc(scan_ready, 1)

            for s in range(2):
                products(s, 0, s)
            with pool.Fori(1, SLICES // 2) as i:
                for par in range(2):
                    products(2 * i + par, i, par)

        @block.tensor
        def _(pe):
            def cumulate(s, par):
                pe.wait_ge(z_read, ST * (s + 1))
                for w in range(2):
                    for t in range(ST):
                        last = pe.matmul(ps_cum[w][:, t, :], tri[:, w, :], za_sig[:, par, t, 0, :], start=True, stop=True)
                last.then_inc(cum_done, 1)

            def chan(s, half, par):
                pe.wait_ge(mix_ready, s + 1)
                wait(pe, hb_act, s)
                for k in range(KC):
                    last = pe.matmul(ps_lo1[:, 0, :], maa_w1[:, k, :], mix[:, k, :], start=(k == 0), stop=(k == KC - 1))
                last.then_inc(lo1_done, 1)
                pe.wait_ge(lo1_act, s + 1)
                for g, (free, count) in enumerate(((xm_ready, 4 * s), (hag_act, s), (None, 0), (xm_ready, 4 * s + 1))):
                    if g < 2:
                        wait(pe, cum_read, s - 1)
                    if free is not None:
                        wait(pe, free, count)
                    for k in range(KC):
                        last = pe.matmul(ps_lo2[g][:, k, :], maa_w2[32 * g:32 * g + 32, k * P:(k + 1) * P],
                                         lo1[32 * g:32 * g + 32, :], start=True, stop=True)
                    last.then_inc(lo2_done, 1)
                pe.wait_ge(xm_ready, 4 * s + 2)
                for k in range(KC):
                    pe.matmul(ps_hag[:, 0, :], w_a1[:, k, :], xm[:, 1, k, :], start=(k == 0), stop=(k == KC - 1))
                for k in range(KC):
                    last = pe.matmul(ps_hag[:, 1, :], w_g1[:, k, :], xm[:, 0, k, :], start=(k == 0), stop=(k == KC - 1))
                last.then_inc(hag_done, 1)
                pe.wait_ge(xm_ready, 4 * s + 3)
                for k in range(KC):
                    last = pe.matmul(ps_hb[0:64, 0, :], w_b1[:, k, :], xm[:, 2, k, :], start=(k == 0), stop=(k == KC - 1))
                last.then_inc(hb_done, 1)

            def tiles(s):
                for t in range(ST):
                    j = ST * s + t
                    tok = slice(t * P, (t + 1) * P)
                    if t == 0:
                        pe.wait_ge(hag_act, s + 1)
                    wait(pe, rg_read, j)
                    for k in range(KC):
                        pe.matmul(ps_rg[:, 0:E], xm[:, 0, k, tok], w_r[:, k, :], start=(k == 0), stop=(k == KC - 1))
                    pe.matmul(ps_rg[:, E:2 * E], hid_g[:, tok], w_g2[:], start=True, stop=True).then_inc(rg_done, 1)
                    if t == 0:
                        pe.wait_ge(xm_ready, 4 * s + 4)
                    wait(pe, kv_read, j)
                    for k in range(KC):
                        pe.matmul(ps_kv[:, 0:E], xm[:, 2, k, tok], w_k[:, k, :], start=(k == 0), stop=(k == KC - 1))
                    for k in range(KC):
                        last = pe.matmul(ps_kv[:, E:2 * E], xm[:, 3, k, tok], w_v[:, k, :], start=(k == 0), stop=(k == KC - 1))
                    last.then_inc(kv_done, 1)
                    if t == 0:
                        pe.wait_ge(hb_act, s + 1)
                    if t == 0:
                        wait(pe, kk_ready, s)
                    pe.matmul(ps_kkk[:, t * E:(t + 1) * E], hid_b[0:64, tok], w_b2[0:64, 0:E], start=True, stop=True).then_inc(kkk_done, 1)
                    wait(pe, z_read, j)
                    pe.matmul(ps_za[:, :], hid_a[:, tok], w_a2[:, 0:2 * E], start=True, stop=True)
                    pe.matmul(ps_mm[:, 0:E], hid_a[:, tok], w_a2[:, 2 * E:3 * E], start=True, stop=True)
                    pe.matmul(ps_mm[:, E:2 * E], hid_b[0:64, tok], w_b2[0:64, E:2 * E], start=True, stop=True).then_inc(z_done, 1)

            def turn(s, half, par, has_prev=True, has_next=True):
                tiles(s)
                if has_prev:
                    cumulate(s - 1, 1 - par)
                if has_next:
                    chan(s + 1, half + par, 1 - par)

            pe.wait_ge(w_in, 16 * len(MIX_WEIGHTS))
            pe.wait_ge(tri_set, 5)
            def last():
                pe.wait_ge(cum_read, SLICES - 1)
                cumulate(SLICES - 1, 1)

            slices(pe, lambda: chan(0, 0, 0), turn, last)

        @block.scalar
        def _(act):
            chain = Chain(act, act_link)

            def lows(s):
                act.wait_ge(lo1_done, s + 1)
                act.activation(lo1[:], ps_lo1[:, 0, :], ACT.Tanh, bias=0.0).then_inc(lo1_act, 1)

            def hiddens(s):
                act.wait_ge(hag_done, s + 1)
                act.activation(hid_a[0:64, :], ps_hag[0:64, 0, :], ACT.Tanh, bias=0.0)
                act.activation(hid_a[64:128, :], ps_hag[64:128, 0, :], ACT.Identity, bias=a_bias[64:128, 0:1])
                act.activation(hid_g[:], ps_hag[:, 1, :], ACT.Tanh, bias=0.0).then_inc(hag_act, 1)
                act.wait_ge(hb_done, s + 1)
                act.activation(hid_b[0:32, :], ps_hb[0:32, 0, :], ACT.Tanh, bias=0.0)
                act.activation(hid_b[32:64, :], ps_hb[32:64, 0, :], ACT.Identity, bias=a_bias[32:64, 1:2]).then_inc(hb_act, 1)

            def tiles(s, half, par):
                wait(act, wide_done, s - 1)
                wait(act, scan_ready, s - 1)
                wait(act, v_out[par], 16 * half)
                for t in range(ST):
                    j = ST * s + t
                    act.wait_ge(rg_done, j + 1)
                    act.copy(q_raw[:, par, t, :], ps_rg[:, 0:E])
                    act.copy(c.gate[:, bass.ds(j, 1), :].rearrange("p o e -> p (o e)"), ps_rg[:, E:2 * E]).then_inc(rg_read, 1)
                    act.wait_ge(kv_done, j + 1)
                    act.copy(k_raw[:, par, t, :], ps_kv[:, 0:E])
                    act.copy(v_raw[:, par, t, :], ps_kv[:, E:2 * E]).then_inc(kv_read, 1)
                    act.wait_ge(z_done, j + 1)
                    act.copy(zd[:, par, t, :], ps_za[:, 0:E])
                    act.activation(za_sig[:, par, t].rearrange("p m e -> p (m e)"), ps_za, ACT.Sigmoid, bias=0.0)
                    act.activation(mam_k[:, par, t].rearrange("p m e -> p (m e)"), ps_mm, ACT.Sigmoid, bias=0.0).then_inc(z_read, 1)

            def sig_az(s):
                act.wait_ge(az_ready, s + 1)
                act.activation(az[:], az[:], ACT.Sigmoid, bias=0.0).then_inc(act_link, 1)

            def copy_sums(s):
                act.wait_ge(cum_done, s + 1)
                for w in range(2):
                    last = act.copy(sums[:, w], ps_cum[w])
                last.then_inc(cum_read, 1)

            def wide(s):
                chain.done += 1
                act.wait_ge(act_link, chain.turns + chain.done)
                act.activation(ls[:], az[:], ACT.Ln, bias=0.0).then_inc(ls_ready, 1)
                act.wait_ge(cum_read, s + 1)
                wait(act, scan_ready, s)
                act.activation(cum[:, 0], sums[:, 0], ACT.Exp, scale=-RATE, bias=0.0)
                act.activation(cum[:, 1], sums[:, 0], ACT.Exp, scale=RATE, bias=0.0)
                act.activation(cum[:, 2], sums[:, 1], ACT.Exp, scale=-RATE, bias=0.0)
                act.wait_ge(wm_ready, s + 1)
                act.activation(wm[:], wm[:], ACT.Exp, bias=0.0).then_inc(decay_ready, 1)

            def turn(s, half, par, has_prev=True, has_next=True):
                if has_prev:
                    sig_az(s - 1)
                tiles(s, half, par)
                if has_prev:
                    copy_sums(s - 1)
                if has_next:
                    lows(s + 1)
                if has_prev:
                    wide(s - 1)
                if has_next:
                    hiddens(s + 1)

            def first():
                lows(0)
                hiddens(0)

            def last():
                sig_az(SLICES - 1)
                copy_sums(SLICES - 1)
                wide(SLICES - 1)

            act.wait_ge(w_in, 16 * len(MIX_WEIGHTS))
            slices(act, first, turn, last, chain, 2)

        @block.vector
        def _(dve):
            chain = Chain(dve, dve_link)
            heads = lambda ap: ap.rearrange("p t (h j) -> p t h j", j=HS)
            per_head = lambda ap: ap[:].rearrange("p (t h) -> p t h", t=ST)

            def shift(s):
                x = c.xnT[:, :, bass.ds(s * SL, SL)]
                xb = x.rearrange("p c (b t) -> p c b t", t=T)
                xxb = xx[:].rearrange("p c (b t) -> p c b t", t=T)
                for k in range(KC):
                    dve.tensor_tensor(xxb[:, k, :, 1:T], xb[:, k, :, 0:T - 1], xb[:, k, :, 1:T], ALU.subtract)
                for k in range(KC):
                    chain(dve.tensor_scalar(xxb[:, k, :, 0:1], xb[:, k, :, 0:1], -1.0, None, ALU.mult))
                wait(dve, lo1_done, s)
                for k in range(KC):
                    last = dve.scalar_tensor_tensor(out=mix[:, k, :], in0=xx[:, k, :], scalar=maa[:, k, 4:5],
                                                    in1=x[:, k, :], op0=ALU.mult, op1=ALU.add)
                last.then_inc(mix_ready, 1)

            def mixes(s, which):
                x = c.xnT[:, :, bass.ds(s * SL, SL)]
                for g in which:
                    dve.wait_ge(lo2_done, 4 * s + g + 1)
                    wait(dve, xm_ready, 4 * s + g)
                    for k in range(KC):
                        last = dve.scalar_tensor_tensor(out=xm_tmp[:, k, :], in0=ps_lo2[g][:, k, :], scalar=maa[:, k, g:g + 1],
                                                        in1=xx[:, k, :], op0=ALU.add, op1=ALU.mult)
                    chain(last)
                    dve.tensor_tensor(xm[:, g, :, :], xm_tmp[:], x, ALU.add).then_inc(xm_ready, 1)

            def tiles(s, par):
                dve.wait_ge(kkk_done, ST * (s + 1))
                dve.wait_ge(kv_read, ST * (s + 1))
                wait(dve, scan_ready, s - 1)
                dve.tensor_tensor(kk[:, par], ps_kkk.rearrange("p (t e) -> p t e", t=ST), k_raw[:, par], ALU.add).then_inc(kk_ready, 1)

            def log_sigmoid(s, par):
                dve.wait_ge(z_read, ST * (s + 1))
                dve.scalar_tensor_tensor(out=az[:], in0=zd[:, par], scalar=-1.0, in1=zd[:, par],
                                         op0=ALU.mult, op1=ALU.max).then_inc(az_ready, 1)
                dve.tensor_scalar(mn[:], zd[:, par], 0.0, None, ALU.min)

            def wide_1(s, par):
                a, ma = za_sig[:, par, :, 1, :], mam_k[:, par, :, 0, :]
                dve.wait_ge(kk_ready, s + 1)
                chain(dve.tensor_tensor(t0[:], kk[:, par], kk[:, par], ALU.mult))
                chain(dve.tensor_reduce(per_head(ss), heads(t0[:]), AX_X, ALU.add))
                chain(dve.tensor_scalar(ss[:], ss[:], TINY, None, ALU.max))
                inverse_sqrt(dve, chain, rn[:], rt[:], ss[:])
                chain(dve.tensor_tensor(heads(kk[:, par]), heads(kk[:, par]),
                                        per_head(rn).unsqueeze(3).to_broadcast([P, ST, HEADS, HS]), ALU.mult))
                wait(dve, scan_ready, s)
                dve.scalar_tensor_tensor(out=b_raw[:], in0=kk[:, par], scalar=-1.0,
                                         in1=a, op0=ALU.mult, op1=ALU.mult)
                chain(dve.scalar_tensor_tensor(out=t1[:], in0=ma, scalar=1.0, in1=a, op0=ALU.subtract, op1=ALU.mult))
                chain(dve.tensor_tensor(t1[:], ma, t1[:], ALU.subtract))
                chain(dve.tensor_tensor(k2[:], k_raw[:, par], t1[:], ALU.mult))

            def wide_2(s, par):
                dve.wait_ge(ls_ready, s + 1)
                chain(dve.scalar_tensor_tensor(out=ls[:], in0=ls[:], scalar=-0.5, in1=mn[:], op0=ALU.add, op1=ALU.add))
                dve.tensor_tensor(wm[:], ls[:], mam_k[:, par, :, 1, :], ALU.mult).then_inc(wm_ready, 1)
                chain(dve.tensor_tensor(t0[:], q_raw[:, par],
                                        faaaa[:].unsqueeze(1).to_broadcast([P, ST, E]), ALU.mult))

            def wide_3(s, par):
                dve.wait_ge(decay_ready, s + 1)
                dve.tensor_tensor(k2[:], k2[:], wm[:], ALU.mult).then_inc(k3_ready, 1)
                dve.wait_ge(k3_ready, s + 1)
                chain(dve.tensor_tensor(t0[:], t0[:], k2[:], ALU.mult))
                chain(dve.tensor_reduce(per_head(rk), heads(t0[:]), AX_X, ALU.add))
                dve.tensor_tensor(c.bonus[:, bass.ds(ST * s, ST), :].rearrange("p t (h j) -> p t h j", j=HS),
                                  heads(v_raw[:, par]),
                                  per_head(rk).unsqueeze(3).to_broadcast([P, ST, HEADS, HS]), ALU.mult).then_inc(wide_done, 1)

            def turn(s, half, par, has_prev=True, has_next=True):
                if has_prev:
                    log_sigmoid(s - 1, 1 - par)
                if has_next:
                    shift(s + 1)
                if has_prev:
                    wide_1(s - 1, 1 - par)
                tiles(s, par)
                if has_next:
                    mixes(s + 1, (0,))
                if has_prev:
                    wide_2(s - 1, 1 - par)
                if has_next:
                    mixes(s + 1, (1, 2, 3))
                if has_prev:
                    wide_3(s - 1, 1 - par)

            def first():
                shift(0)
                mixes(0, range(4))

            def last():
                log_sigmoid(SLICES - 1, 1)
                wide_1(SLICES - 1, 1)
                wide_2(SLICES - 1, 1)
                wide_3(SLICES - 1, 1)

            dve.wait_ge(w_in, 16 * len(MIX_WEIGHTS))
            slices(dve, first, turn, last, chain, 2 * (1 + 4 + 3 + RSQRT_LINKS + 1 + 3 + 2 + 3))


CHUNK = 8
CHUNKS = T // CHUNK
HG = 4
GH = HEADS // HG
GC = GH * HS
HALF_I = HS // 2
LOADS = 16 * HG


def scan_stage(nc, d, c):
    with ExitStack() as ctx:
        sb = lambda name, shape: ctx.enter_context(nc.sbuf_tensor("scan_" + name, shape, F32))
        sem = lambda name: ctx.enter_context(nc.semaphore("scan_" + name))
        vec = sb("vec", [P, 2, CHUNK, ARRAYS, GC])
        prod = sb("prod", [P, 4, 2, 2, HALF_I * GC])
        outer = sb("outer", [P, 2, HALF_I * GC])
        kv = sb("kv", [P, 4, HS * GC])
        sa = sb("sa", [P, HS * GH])
        y = sb("y", [P, 2, CHUNK, GC])
        part = sb("part", [P, 3, 2, HALF_I * GH, HS // 2])
        first = sb("first", [P, 2, GC])
        ps = ctx.enter_context(nc.psum_tensor("ps_scan", [P, 2, BANK], F32))
        loaded = [sem("loaded0"), sem("loaded1")]
        stored = [sem("stored0"), sem("stored1")]
        added, o_ready, prod_ready = ([sem(f"{n}{h}") for h in range(2)] for n in ("added", "outer_ready", "prod_ready"))
        kv_ready, y_done, sa_link, outer_zero = sem("kv_ready"), sem("y_done"), sem("sa_link"), sem("outer_zero")
        first_in, head_in, part_link = sem("first_in"), sem("head_in"), sem("part_link")
        HEAD = 2

        def wait_loaded(eng, t, half, par, tau):
            if isinstance(t, int) and t in (0, HEAD):
                eng.wait_ge(head_in if t == 0 else loaded[0], LOADS)
            elif tau == 0:
                eng.wait_ge(loaded[par], LOADS * (half + 1))
        block = ctx.enter_context(nc.Block())
        TURNS = CHUNKS // 2

        rows = lambda ap, g: ap[g * B:(g + 1) * B]

        def steps(eng, step):
            def turn(i):
                for par in range(2):
                    for tau in range(CHUNK):
                        step(i * 2 * CHUNK + par * CHUNK + tau, 2 * i + par, i, par, tau)

            turn(0)
            with eng.Fori(1, TURNS) as i:
                turn(i)

        @block.sync
        def _(sp):
            src = d["scan"][1:TOK + 1].rearrange("(b n t) m (g e) -> n g b t m e", t=CHUNK, n=CHUNKS, g=HG)

            def load(chunk, par):
                if not isinstance(chunk, int):
                    sp.wait_ge(o_ready[1], CHUNK * (chunk - 1) + 1)
                    sp.wait_ge(kv_ready, CHUNK * (chunk - 1) + 1)
                for g in range(HG):
                    sp.dma_start(rows(vec, g)[:, par].rearrange("b t m e -> b t m e"),
                                 src[bass.ds(chunk, 1), g].rearrange("o b t m e -> (o b) t m e")).then_inc(loaded[par], 16)

            heads_0 = d["scan"][0:TOK].rearrange("(b t) m (g e) -> t g b m e", t=T, g=HG)
            for g in range(HG):
                sp.dma_start(rows(first, g), heads_0[0, g, :, ROW_K:ROW_V + 1, :]).then_inc(first_in, 16)
            for part, arrived in ((slice(0, HEAD), head_in), (slice(HEAD, CHUNK), loaded[0])):
                for g in range(HG):
                    sp.dma_start(rows(vec, g)[:, 0, part], src[0, g][:, part]).then_inc(arrived, 16)
            load(1, 1)
            with sp.Fori(1, TURNS) as i:
                load(2 * i, 0)
                load(2 * i + 1, 1)

        @block.scalar
        def _(act):
            dst = d["y"].rearrange("(b n t) (g e) -> n g b t e", t=CHUNK, n=CHUNKS, g=HG)
            with act.Fori(0, TURNS) as i:
                for par in range(2):
                    act.wait_ge(y_done, CHUNK * (2 * i + par + 1) + 1)
                    for g in range(HG):
                        act.dma_start(dst[bass.ds(2 * i + par, 1), g].rearrange("o b t e -> (o b) t e"),
                                      rows(y, g)[:, par]).then_inc(stored[par], 16)
            for q in stored:
                act.wait_ge(q, LOADS * TURNS)

        @block.gpsimd
        def _(pool):
            pool.memset(outer[:], 0.0).then_inc(outer_zero, 1)
            pool.memset(y[:], 0.0).then_inc(y_done, 1)

            def v_outer_k(slot, k, v):
                v = v.rearrange("p (h i) -> p i h", i=HS).unsqueeze(3).to_broadcast([P, HS, GH, HS])
                k = k.rearrange("p (h j) -> p h j", j=HS).unsqueeze(1).to_broadcast([P, HS, GH, HS])
                pool.tensor_tensor(kv[:, slot, :].rearrange("p (i h j) -> p i h j", i=HS, h=GH), v, k,
                                   ALU.mult).then_inc(kv_ready, 1)

            def sum_y(t, half, par, tau):
                pool.wait_ge(prod_ready[1], t + 1)
                if tau == 0:
                    wait(pool, stored[par], LOADS * half)
                src = prod[:, tau % 4, :, 0, :].rearrange("p s (r j) -> p s r j", j=HS)
                n = HS // 2
                for level in range(3):
                    dst = part[:, level, :, :, 0:n]
                    pool.tensor_tensor(dst, src[:, :, :, 0:n], src[:, :, :, n:2 * n], ALU.add).then_inc(part_link, 1)
                    pool.wait_ge(part_link, 3 * t + level + 1)
                    src, n = dst, n // 2
                terms = src.rearrange("p s (i h) j -> p (s i) h j", h=GH)
                pool.tensor_tensor(y[:, par, tau, :].rearrange("p (h i) -> p i h", i=HS), terms[:, :, :, 0],
                                   terms[:, :, :, 1], ALU.add).then_inc(y_done, 1)

            def step(t, chunk, half, par, tau):
                wait_loaded(pool, t, half, par, tau)
                v_outer_k((tau + 1) % 4, vec[:, par, tau, ROW_K, :], vec[:, par, tau, ROW_V, :])
                if tau > 0:
                    sum_y(t - 1, half, par, tau - 1)
                elif not isinstance(t, int) or t > 0:
                    sum_y(t - 1, half + par - 1, 1 - par, CHUNK - 1)

            pool.wait_ge(first_in, LOADS)
            v_outer_k(0, first[:, 0, :], first[:, 1, :])
            steps(pool, step)
            sum_y(T - 1, TURNS - 1, 1, CHUNK - 1)

        @block.tensor
        def _(pe):
            pe.wait_ge(outer_zero, 1)
            for h in range(2):
                pe.matmul(ps[:, h, :], c.ident[:], outer[:, h, :], start=True, stop=True).then_inc(added[h], 1)

            def step(t, chunk, half, par, tau):
                pe.wait_ge(kv_ready, t + 1)
                for h in range(2):
                    wait(pe, prod_ready[h], t)
                    pe.matmul(ps[:, h, :], c.ident[:], kv[:, tau % 4, h * BANK:(h + 1) * BANK], start=False, stop=False,
                              skip_group_check=True)
                    pe.wait_ge(o_ready[h], t + 1)
                    pe.matmul(ps[:, h, :], c.ident[:], outer[:, h, :], start=False, stop=True,
                              skip_group_check=True).then_inc(added[h], 1)

            steps(pe, step)

        @block.vector
        def _(dve):
            def outer_u_b(h, vec_b):
                shape = [P, HALF_I, GH, HS]
                u = sa[:, h * HALF_I * GH:(h + 1) * HALF_I * GH].rearrange("p (i h) -> p i h", h=GH)
                b = vec_b.rearrange("p (h j) -> p h j", j=HS)
                dve.tensor_tensor(outer[:, h, :].rearrange("p (i h j) -> p i h j", h=GH, j=HS),
                                  u.unsqueeze(3).to_broadcast(shape), b.unsqueeze(1).to_broadcast(shape),
                                  ALU.mult).then_inc(o_ready[h], 1)

            for h in range(2):
                dve.wait_ge(outer_zero, 1)
                dve.wait_ge(added[h], 1)
                dve.memset(outer[:, h, :], 0.0).then_inc(o_ready[h], 1)

            def products(t, half, par, tau, h):
                dve.wait_ge(added[h], t + 2)
                if h == 0:
                    wait_loaded(dve, t, half, par, tau)
                wait(dve, y_done, t - 2)
                vecs = vec[:, par, tau, ROW_Q:ROW_A + 1, :].unsqueeze(2).to_broadcast([P, 2, HALF_I, GC])
                state = ps[:, h, :].rearrange("p (i e) -> p i e", e=GC).unsqueeze(1).to_broadcast([P, 2, HALF_I, GC])
                dve.tensor_tensor(prod[:, tau % 4, h].rearrange("p m (i e) -> p m i e", e=GC), state, vecs,
                                  ALU.mult).then_inc(prod_ready[h], 1)

            def sum_a(t, tau, h):
                dve.wait_ge(prod_ready[h], t + 1)
                dve.tensor_reduce(sa[:, h * HALF_I * GH:(h + 1) * HALF_I * GH],
                                  prod[:, tau % 4, h, 1, :].rearrange("p (r j) -> p r j", j=HS), AX_X, ALU.add).then_inc(sa_link, 1)

            def step(t, chunk, half, par, tau):
                products(t, half, par, tau, 0)
                sum_a(t, tau, 0)
                products(t, half, par, tau, 1)
                dve.wait_ge(sa_link, 2 * t + 1)
                outer_u_b(0, vec[:, par, tau, ROW_B, :])
                sum_a(t, tau, 1)
                dve.wait_ge(sa_link, 2 * t + 2)
                outer_u_b(1, vec[:, par, tau, ROW_B, :])

            steps(dve, step)


GROUP = 2
GROUPS = TILES // GROUP
GN_EPS = 0.00064
EXPERTS, FF = 8, 1024
FC = FF // P
JITTER = 0.01
NT = 256
TURNS_X = (2 * TOK - EXPERTS) // NT + EXPERTS
TT = NT // P
SLOT_TILES = TURNS_X * TT
HL, HI, LO = 2, 0, 1
GF = 2
G = FC // GF
ROWS = TOK + NT
U32 = mybir.dt.uint32
I32 = mybir.dt.int32


def load_expert(sp, d, c, j, split=None):
    x = sp.value_load(c.turn_expert[0:1, bass.ds(j, 1)], min_val=0, max_val=EXPERTS - 1)
    for n, name in enumerate(("w1", "w3", "w2")):
        if split:
            sp.wait_ge(split[n], j)
        sp.dma_start(c.raw[n][:], d[name][bass.ds(x, 1)].rearrange("o (k p) f -> p (o k) f", p=P)).then_inc(c.raw_in[n], 16)


def out_stage(nc, d, c):
    with ExitStack() as ctx:
        sb = lambda name, shape, dt=F32: ctx.enter_context(nc.sbuf_tensor("out_" + name, shape, dt))
        sem = lambda name: ctx.enter_context(nc.semaphore("out_" + name))
        y = sb("y", [P, TILES, E])
        sq = sb("sq", [P, GROUP, E])
        yc = sb("yc", [P, GROUP, E])
        h_new = sb("h_new", [P, GROUP, E])
        gated = sb("gated", [P, GROUP, E])
        ln_w, ln_b = sb("ln_w", [P, E]), sb("ln_b", [P, E])
        w_o = sb("w_o", [P, KC, E])
        gate_w = sb("gate_w", [P, KC, EXPERTS])
        NG = GROUP * HEADS
        g_sum, g_mean = sb("g_sum", [P, NG]), sb("g_mean", [P, NG])
        var, rstd, nwt = (sb(n, [P, NG + GROUP]) for n in ("var", "rstd", "nwt"))
        h_rstd, h_shift = sb("h_rstd", [P, GROUP]), sb("h_shift", [P, GROUP])
        yn = sb("yn", [P, GROUP, E])
        words = sb("words", [P, 3])
        root = sb("root", [P, NG + GROUP])
        ygT = sb("ygT", [P, GROUP, KC, P])
        xn = sb("xn", [P, GROUP, E])
        xT = sb("xT", [P, GROUP, KC, P])
        stats = sb("stats", [P, GROUP, 6])
        mean_var = sb("mean_var", [P, GROUP, 2])
        logits = sb("logits", [P, TILES, EXPERTS])
        top = sb("top", [P, TILES, 8])
        top_i = sb("top_i", [P, TILES, 8], mybir.dt.uint32)
        top_f = sb("top_f", [P, TILES, 2])
        expert_no = sb("expert_no", [P, EXPERTS])
        expert_ni = sb("expert_ni", [P, EXPERTS], mybir.dt.int32)
        hot = [sb("hot0", [P, TILES, EXPERTS]), sb("hot1", [P, TILES, EXPERTS])]
        absl, others, products = (sb(n, [P, TILES, EXPERTS]) for n in ("absl", "others", "products"))
        dif, fac, keep, ex = (sb(n, [P, 2, TILES, EXPERTS]) for n in ("dif", "fac", "keep", "ex"))
        half_sum, den = sb("half_sum", [P, 2, TILES, EXPERTS // 2]), sb("den", [P, 2, TILES])
        chosen, rank = sb("chosen", [P, TILES, EXPERTS]), sb("rank", [P, TILES, EXPERTS])
        before = [sb("before0", [P, TILES, EXPERTS]), sb("before1", [P, TILES, EXPERTS])]
        n_i = sb("n_i", [P, EXPERTS], I32)
        turns_of, start, sums = (sb(n, [P, EXPERTS]) for n in ("turns_of", "start", "sums"))
        le = sb("le", [P, TURNS_X, EXPERTS])
        te, turn_no = sb("te", [P, TURNS_X]), sb("turn_no", [P, TURNS_X])
        turn_ni = sb("turn_ni", [P, TURNS_X], I32)
        weight = sb("weight", [P, 2, TILES])
        slot_f, slot_i = sb("slot_f", [P, 2, TILES]), sb("slot_i", [P, 2, TILES], I32)
        place_i, tile_i = sb("place_i", [P, 2, TILES], I32), sb("tile_i", [P, 2, TILES], I32)
        place, tile = sb("place", [P, 2, TILES]), sb("tile", [P, 2, TILES])
        at_place = sb("at_place", [P, 2, TILES, P], F32R)
        of_tile = sb("of_tile", [P, 2, TILES, SLOT_TILES])
        at_tile = sb("at_tile", [P, 2, TILES, 3, SLOT_TILES], F32R)
        w_hi, w_lo = sb("w_hi", [P, 2, TILES], F32R), sb("w_lo", [P, 2, TILES])
        place_no, tile_no, row_no = sb("place_no", [P, P]), sb("tile_no", [P, SLOT_TILES]), sb("row_no", [P, TILES])
        empty_row, taken = sb("empty_row", [P, SLOT_TILES]), sb("taken", [P, SLOT_TILES])
        numbers = sb("numbers", [P, P + SLOT_TILES + TILES + SLOT_TILES], I32)
        zeros = sb("zeros", [P, E])
        tri = sb("tri", [P, P])
        ones = sb("ones", [P, P])
        ps = ctx.enter_context(nc.psum_tensor("ps_out", [P, 6, BANK], F32))
        ps_t = ps[:, 0, :].rearrange("p (t k n) -> p t k n", t=GROUP, k=KC)
        ps_o = ps[:, 1, :].rearrange("p (t e) -> p t e", t=GROUP)
        ps_x = ps[:, 2, :].rearrange("p (t k n) -> p t k n", t=GROUP, k=KC)
        ps_l = ps[:, 3, 0:TILES * EXPERTS].rearrange("p (t x) -> p t x", t=TILES)
        ps_rank, ps_count = (ps[:, 4, w * TILES * EXPERTS:(w + 1) * TILES * EXPERTS].rearrange("p (t x) -> p t x", t=TILES)
                             for w in range(2))
        ps_slots = ps[:, 5, 0:3 * SLOT_TILES].rearrange("p (v a) -> p v a", v=3)
        places_ready, slots_done, tiles_in = sem("places_ready"), sem("slots_done"), sem("y_rest_in")
        zero_set, zero_stored, experts_ready = sem("zero_set"), sem("zero_stored"), sem("experts_ready")
        tiles_ready, tiles_set = sem("tiles_ready"), sem("tiles_set")
        chosen_ready, ranks_done, tri_set = sem("chosen_ready"), sem("ranks_done"), sem("tri_set")
        w_in, y_in = sem("w_in"), sem("y_in")
        yc_ready, sq_ready, yn_ready, yg_ready = (sem(n) for n in ("yc_ready", "sq_ready", "yn_ready", "yg_ready"))
        var_ready, root_ready = sem("var_ready"), sem("root_ready")
        t_done, t_copied, o_done, h_ready, rs_ready = (sem(n) for n in ("t_done", "t_copied", "o_done", "h_ready", "rs_ready"))
        h_stored, xn_stored, pool_link = sem("h_stored"), sem("xn_stored"), sem("pool_link")
        top_ready, hot_ready, den_ready = sem("top_ready"), sem("hot_ready"), sem("den_ready")
        xn_ready, x_done, x_copied, l_done, no_set = (sem(n) for n in ("xn_ready", "x_done", "x_copied", "l_done", "no_set"))
        dve_link, e_asked, e_ready = sem("dve_link"), sem("exp_asked"), sem("exp_ready")
        block = ctx.enter_context(nc.Block())
        FIRST = 5

        def steps(eng, step, chain=None, links=0):
            for n in range(FIRST):
                step(n)
            with eng.Fori(0, GROUPS - FIRST) as i:
                if chain:
                    chain.enter(i, links)
                step(i + FIRST, inner=True)
                if chain:
                    chain.leave(GROUPS - FIRST)
            for n in range(GROUPS, GROUPS + 5):
                step(n)

        runs = lambda n, late, inner: inner or late <= n < GROUPS + late

        @block.sync
        def _(sp):
            rows = d["y"].rearrange("(t p) e -> p t e", p=P)
            sp.dma_start(y[:, 0:GROUP], rows[:, 0:GROUP]).then_inc(y_in, 16)
            sp.dma_start(ln_w[:], d["ln_w"].partition_broadcast(P)).then_inc(w_in, 16)
            sp.dma_start(ln_b[:], d["ln_b"].partition_broadcast(P)).then_inc(w_in, 16)
            sp.dma_start(w_o[:], d["w_oT"].rearrange("(c p) e -> p c e", p=P)).then_inc(w_in, 16)
            sp.dma_start(gate_w[:], d["gate_w"].rearrange("(c p) e -> p c e", p=P)).then_inc(w_in, 16)
            sp.dma_start(y[:, GROUP:], rows[:, GROUP:]).then_inc(tiles_in, 16)
            sp.wait_ge(zero_set, 1)
            for name in ("xn_rows", "sum_rows"):
                for t in range(TT):
                    sp.dma_start(d[name][TOK + t * P:TOK + (t + 1) * P], zeros[:]).then_inc(zero_stored, 16)
            xn_rows, sum_rows = (d[n][0:TOK].rearrange("(t p) e -> p t e", p=P) for n in ("xn_rows", "sum_rows"))
            with sp.Fori(0, GROUPS) as g:
                at = bass.ds(g * GROUP, GROUP)
                sp.wait_ge(h_ready, g + 1)
                sp.dma_start(sum_rows[:, at], h_new[:]).then_inc(h_stored, 16)
                sp.wait_ge(xn_ready, g + 1)
                sp.dma_start(xn_rows[:, at], xn[:]).then_inc(xn_stored, 16)
            sp.wait_ge(zero_stored, 2 * TT * 16)
            sp.wait_ge(h_stored, GROUPS * 16)
            sp.wait_ge(xn_stored, GROUPS * 16)

            sp.wait_ge(experts_ready, 1)
            load_expert(sp, d, c, 0)

        @block.gpsimd
        def _(pool):
            pool.iota(expert_ni[:], pattern=[[1, EXPERTS]], base=0, channel_multiplier=0).then_inc(no_set, 1)
            pool.wait_ge(no_set, 1)
            pool.tensor_copy(expert_no[:], expert_ni[:]).then_inc(no_set, 1)
            pool.iota(turn_ni[:], pattern=[[1, TURNS_X]], base=0, channel_multiplier=0).then_inc(no_set, 1)
            pool.wait_ge(no_set, 3)
            pool.tensor_copy(turn_no[:], turn_ni[:]).then_inc(no_set, 1)
            pool.memset(zeros[:], 0.0).then_inc(zero_set, 1)
            at = 0
            for n, start, step_p, pattern in ((P, 0, 0, [[1, P]]), (SLOT_TILES, 0, 0, [[1, SLOT_TILES]]),
                                              (TILES, 1, 1, [[P, TILES]]), (SLOT_TILES, TOK + 1, 1, [[0, TURNS_X], [P, TT]])):
                last = pool.iota(numbers[:, at:at + n], pattern=pattern, base=start, channel_multiplier=step_p)
                at += n
            last.then_inc(no_set, 1)
            pool.wait_ge(no_set, 5)
            at = 0
            for to in (place_no, tile_no, row_no, empty_row):
                n = to.shape[1]
                last = pool.tensor_copy(to[:], numbers[:, at:at + n])
                at += n
            last.then_inc(no_set, 1)
            pool.memset(ones[:], 1.0).then_inc(tri_set, 1)
            pool.memset(tri[:], 1.0).then_inc(tri_set, 1)
            pool.wait_ge(tri_set, 2)
            pool.affine_select(out=tri[:], in_=tri[:], compare_op=ALU.is_ge, fill=0.0, base=-1,
                               pattern=[[1, P]], channel_multiplier=-1).then_inc(tri_set, 1)

            chain = Chain(pool, pool_link)

            def touch_word(n):
                pool.tensor_tensor(words[:, n:n + 1], ones[:, 0:1], ones[:, 0:1], ALU.mult)

            def gate(g):
                at = bass.ds(g * GROUP, GROUP)
                tiled = lambda ap: ap[:].unsqueeze(1).to_broadcast([P, GROUP, E])
                pool.wait_ge(yn_ready, g + 1)
                chain(pool.tensor_tensor(yn[:], yn[:], tiled(ln_w), ALU.mult))
                chain(pool.tensor_tensor(yn[:], yn[:], tiled(ln_b), ALU.add))
                touch_word(0)
                chain(pool.tensor_tensor(yn[:], yn[:], c.bonus[:, at, :], ALU.add))
                wait(pool, t_done, g)
                touch_word(1)
                pool.tensor_tensor(gated[:], yn[:], c.gate[:, at, :], ALU.mult).then_inc(yg_ready, 1)

            def step(n, inner=False):
                if runs(n, 0, inner):
                    gate(n)

            pool.wait_ge(w_in, 64)
            pool.wait_ge(tri_set, 3)
            steps(pool, step, chain, 3)

            all_x = lambda ap: ap.to_broadcast([P, TILES, EXPERTS])
            pool.wait_ge(top_ready, 1)
            pool.wait_ge(yg_ready, GROUPS)
            for w in range(2):
                chain(pool.tensor_tensor(dif[:, w], logits[:], all_x(top[:, :, w:w + 1]), ALU.subtract))
                pool.tensor_scalar(ex[:, w], dif[:, w], 0.0, None, ALU.min).then_inc(e_asked, 1)
            chain(pool.tensor_scalar(fac[:], fac[:], 2.0 * JITTER, None, ALU.mult))
            chain(pool.tensor_tensor(keep[:], dif[:], fac[:], ALU.add))
            chain(pool.tensor_scalar(keep[:], keep[:], 0.0, None, ALU.is_ge))
            pool.wait_ge(hot_ready, 1)
            chain(pool.tensor_scalar(others[:], hot[0][:], -1.0, 1.0, ALU.mult, ALU.add))
            chain(pool.tensor_tensor(keep[:, 1], keep[:, 1], others[:], ALU.mult))
            pool.wait_ge(e_ready, 2)
            chain(pool.tensor_tensor(keep[:], keep[:], ex[:], ALU.mult))
            chain(pool.tensor_tensor(half_sum[:], keep[:, :, :, 0:4], keep[:, :, :, 4:8], ALU.add))
            chain(pool.tensor_tensor(half_sum[:, :, :, 0:2], half_sum[:, :, :, 0:2], half_sum[:, :, :, 2:4], ALU.add))
            pool.tensor_tensor(den[:], half_sum[:, :, :, 0], half_sum[:, :, :, 1], ALU.add).then_inc(den_ready, 1)
            pool.wait_ge(tiles_set, 3)
            for w in range(2):
                for v, part in ((1, w_hi), (2, w_lo)):
                    last = pool.tensor_tensor(at_tile[:, w, :, v, :], of_tile[:, w],
                                              part[:, w, :].unsqueeze(2).to_broadcast([P, TILES, SLOT_TILES]), ALU.mult)
                last.then_inc(tiles_ready, 1)

        @block.tensor
        def _(pe):
            def turn_y(g):
                pe.wait_ge(yg_ready, g + 1)
                wait(pe, t_copied, g)
                for t in range(GROUP):
                    for k in range(KC):
                        last = pe.transpose(ps_t[:, t, k, :], gated[:, t, k * P:(k + 1) * P], c.ident[:])
                last.then_inc(t_done, 1)

            def project(g):
                pe.wait_ge(t_copied, g + 1)
                wait(pe, h_ready, g)
                for t in range(GROUP):
                    for k in range(KC):
                        last = pe.matmul(ps_o[:, t, :], ygT[:, t, k, :], w_o[:, k, :], start=(k == 0), stop=(k == KC - 1))
                last.then_inc(o_done, 1)

            def gate(g):
                pe.wait_ge(xn_ready, g + 1)
                wait(pe, x_copied, g)
                for t in range(GROUP):
                    for k in range(KC):
                        last = pe.transpose(ps_x[:, t, k, :], xn[:, t, k * P:(k + 1) * P], c.ident[:])
                last.then_inc(x_done, 1)
                pe.wait_ge(x_copied, g + 1)
                for t in range(GROUP):
                    for k in range(KC):
                        last = pe.matmul(ps_l[:, bass.ds(g * GROUP + t, 1), :].rearrange("p o x -> p (o x)"),
                                         xT[:, t, k, :], gate_w[:, k, :], start=(k == 0), stop=(k == KC - 1))
                last.then_inc(l_done, 1)

            pe.wait_ge(w_in, 64)
            def step(n, inner=False):
                if runs(n, 2, inner):
                    project(n - 2)
                if runs(n, 1, inner):
                    turn_y(n - 1)
                if runs(n, 3, inner):
                    gate(n - 3)

            steps(pe, step)
            pe.wait_ge(tri_set, 3)
            pe.wait_ge(chosen_ready, 1)
            flat = chosen[:].rearrange("p t x -> p (t x)")
            pe.matmul(ps_rank.rearrange("p t x -> p (t x)"), tri[:], flat, start=True, stop=True)
            pe.matmul(ps_count.rearrange("p t x -> p (t x)"), ones[:], flat, start=True, stop=True).then_inc(ranks_done, 1)
            pe.wait_ge(tiles_ready, 4)
            for w in range(2):
                pe.wait_ge(places_ready, w + 1)
                for t in range(TILES):
                    last = pe.matmul(ps[:, 5, 0:3 * SLOT_TILES], at_place[:, w, t, :],
                                     at_tile[:, w, t].rearrange("p v a -> p (v a)"),
                                     start=(w == 0 and t == 0), stop=(w == 1 and t == TILES - 1))
            last.then_inc(slots_done, 1)

        @block.scalar
        def _(act):
            def copy_t(g):
                act.wait_ge(t_done, g + 1)
                wait(act, o_done, g)
                act.copy(ygT[:], ps_t).then_inc(t_copied, 1)

            def copy_x(g):
                act.wait_ge(x_done, g + 1)
                wait(act, l_done, g)
                act.copy(xT[:], ps_x).then_inc(x_copied, 1)

            def squares(g):
                act.wait_ge(yc_ready, g + 1)
                wait(act, yn_ready, g)
                act.activation(sq[:], yc[:], ACT.Square, bias=0.0).then_inc(sq_ready, 1)

            def roots(n):
                act.wait_ge(var_ready, n + 1)
                act.activation(root[:], var[:], ACT.Sqrt, bias=0.0).then_inc(root_ready, 1)

            def norm_h(g):
                act.wait_ge(rs_ready, g + 1)
                wait(act, x_done, g)
                wait(act, xn_stored, 16 * g)
                for t in range(GROUP):
                    last = act.activation(xn[:, t, :], h_new[:, t, :], ACT.Identity, scale=h_rstd[:, t:t + 1], bias=h_shift[:, t:t + 1])
                last.then_inc(xn_ready, 1)

            def step(n, inner=False):
                if runs(n, 0, inner):
                    squares(n)
                if runs(n, 4, inner):
                    copy_x(n - 4)
                if runs(n, 2, inner):
                    copy_t(n - 2)
                if runs(n, 0, inner) or runs(n, 3, inner):
                    roots(n)
                if runs(n, 3, inner):
                    norm_h(n - 3)

            steps(act, step)
            for w in range(2):
                act.wait_ge(e_asked, w + 1)
                act.activation(ex[:, w], ex[:, w], ACT.Exp, bias=0.0).then_inc(e_ready, 1)

        @block.vector
        def _(dve):
            chain = Chain(dve, dve_link)
            heads = lambda ap: ap.rearrange("p t (h j) -> p t h j", j=HS)
            per_head = lambda ap: ap.rearrange("p (t h) -> p t h", t=GROUP)
            spread = lambda ap: per_head(ap).unsqueeze(3).to_broadcast([P, GROUP, HEADS, HS])
            tiled = lambda ap: ap[:].unsqueeze(1).to_broadcast([P, GROUP, E])

            def center_y(g):
                yg = y[:, bass.ds(g * GROUP, GROUP), :]
                chain(dve.tensor_reduce(per_head(g_sum[:]), heads(yg), AX_X, ALU.add))
                chain(dve.tensor_scalar(g_mean[:], g_sum[:], 1.0 / HS, None, ALU.mult))
                dve.tensor_tensor(heads(yc[:]), heads(yg), spread(g_mean[:]), ALU.subtract).then_inc(yc_ready, 1)

            def add_h(g):
                dve.wait_ge(o_done, g + 1)
                wait(dve, h_stored, 16 * g)
                wait(dve, xn_ready, g)
                dve.tensor_tensor(h_new[:], c.h[:, bass.ds(g * GROUP, GROUP), :], ps_o, ALU.add).then_inc(h_ready, 1)
                dve.wait_ge(h_ready, g + 1)
                for t in range(GROUP):
                    last = dve.bn_stats(stats[:, t, :], h_new[:, t, :])
                chain(last)
                touch(dve, nwt)
                for t in range(GROUP):
                    last = dve.bn_aggr(mean_var[:, t, :], stats[:, t, :])
                chain(last)
                chain(dve.tensor_scalar(var[:, NG:], mean_var[:, :, 1], LN_EPS, None, ALU.add))

            def step(n, inner=False):
                if runs(n, 0, inner):
                    if not inner and n == 1:
                        dve.wait_ge(tiles_in, 16)
                    center_y(n)
                if runs(n, 3, inner):
                    add_h(n - 3)
                if runs(n, 0, inner):
                    dve.wait_ge(sq_ready, n + 1)
                    chain(dve.tensor_reduce(per_head(g_sum[:]), heads(sq[:]), AX_X, ALU.add))
                    dve.tensor_scalar(var[:, 0:NG], g_sum[:], 1.0 / HS, GN_EPS, ALU.mult, ALU.add).then_inc(var_ready, 1)
                elif runs(n, 3, inner):
                    touch(dve, g_mean).then_inc(var_ready, 1)
                if runs(n, 0, inner) or runs(n, 3, inner):
                    dve.wait_ge(var_ready, n + 1)
                    dve.wait_ge(root_ready, n + 1)
                    chain(dve.reciprocal(rstd[:], root[:]))
                    newton(dve, chain, rstd[:], nwt[:], var[:])
                if runs(n, 0, inner):
                    wait(dve, yg_ready, n)
                    dve.tensor_tensor(heads(yn[:]), heads(yc[:]), spread(rstd[:, 0:NG]), ALU.mult).then_inc(yn_ready, 1)
                if runs(n, 3, inner):
                    dve.tensor_copy(h_rstd[:], rstd[:, NG:])
                    dve.scalar_tensor_tensor(out=h_shift[:], in0=mean_var[:, :, 0], scalar=-1.0, in1=rstd[:, NG:],
                                             op0=ALU.mult, op1=ALU.mult).then_inc(rs_ready, 1)

            dve.wait_ge(y_in, 16)
            chain(dve.memset(var[:], 1.0))
            steps(dve, step, chain, 2 + 3 + 1 + 1 + 4)

            dve.wait_ge(l_done, GROUPS)
            chain(dve.tensor_copy(logits[:], ps_l))
            for t in range(TILES):
                last = dve.max(top[:, t, :], logits[:, t, :])
            chain(dve.scalar_tensor_tensor(out=absl[:], in0=logits[:], scalar=-1.0, in1=logits[:], op0=ALU.mult, op1=ALU.max))
            for w in range(2):
                last = dve.tensor_tensor(fac[:, w], absl[:], top[:, :, w:w + 1].to_broadcast([P, TILES, EXPERTS]), ALU.max)
            last.then_inc(top_ready, 1)
            dve.wait_ge(top_ready, 1)
            for t in range(TILES):
                last = dve.max_index(top_i[:, t, :], top[:, t, :], logits[:, t, :])
            chain(last)
            dve.wait_ge(no_set, 6)
            chain(dve.tensor_copy(top_f[:], top_i[:, :, 0:2]))
            all_x = lambda ap: ap.to_broadcast([P, TILES, EXPERTS])
            for w in range(2):
                dve.tensor_tensor(hot[w][:], expert_no[:].unsqueeze(1).to_broadcast([P, TILES, EXPERTS]),
                                  all_x(top_f[:, :, w:w + 1]), ALU.is_equal).then_inc(hot_ready, 1)
            dve.wait_ge(hot_ready, 2)

            dve.tensor_tensor(chosen[:], hot[0][:], hot[1][:], ALU.add).then_inc(chosen_ready, 1)
            dve.wait_ge(ranks_done, 1)
            chain(dve.tensor_copy(rank[:], ps_rank))
            chain(dve.tensor_copy(before[0][:], ps_count))
            src = 0
            for step in (1, 2, 4, 8):
                a, b = before[src], before[1 - src]
                dve.tensor_copy(b[:, 0:step, :], a[:, 0:step, :])
                chain(dve.tensor_tensor(b[:, step:, :], a[:, step:, :], a[:, 0:TILES - step, :], ALU.add))
                src = 1 - src
            total = before[src]
            chain(dve.tensor_scalar(n_i[:], total[:, TILES - 1, :], float(NT - 1), None, ALU.add))
            chain(dve.tensor_scalar(n_i[:], n_i[:], NT.bit_length() - 1, None, ALU.logical_shift_right))
            chain(dve.tensor_copy(turns_of[:], n_i[:]))
            chain(dve.memset(start[:, 0:1], 0.0))
            chain(dve.tensor_copy(start[:, 1:], turns_of[:, 0:EXPERTS - 1]))
            a, b = start, sums
            for step in (1, 2, 4):
                dve.tensor_copy(b[:, 0:step], a[:, 0:step])
                chain(dve.tensor_tensor(b[:, step:], a[:, step:], a[:, 0:EXPERTS - step], ALU.add))
                a, b = b, a
            start_of, base = a, b
            chain(dve.tensor_tensor(le[:], start_of[:].unsqueeze(1).to_broadcast([P, TURNS_X, EXPERTS]),
                                    turn_no[:].unsqueeze(2).to_broadcast([P, TURNS_X, EXPERTS]), ALU.is_le))
            chain(dve.tensor_reduce(te[:], le[:], AX_X, ALU.add))
            chain(dve.tensor_scalar(te[:], te[:], -1.0, None, ALU.add))
            dve.tensor_copy(c.turn_expert[:], te[:]).then_inc(experts_ready, 1)
            chain(dve.tensor_tensor(rank[:, 1:, :], rank[:, 1:, :], total[:, 0:TILES - 1, :], ALU.add))
            chain(dve.tensor_scalar(base[:], start_of[:], float(NT), None, ALU.mult))
            chain(dve.tensor_tensor(rank[:], rank[:], base[:].unsqueeze(1).to_broadcast([P, TILES, EXPERTS]), ALU.add))
            for w in range(2):
                chain(dve.tensor_tensor(products[:], rank[:], hot[w][:], ALU.mult))
                chain(dve.tensor_reduce(slot_f[:, w, :], products[:], AX_X, ALU.add))
            chain(dve.tensor_copy(slot_i[:], slot_f[:]))
            dve.tensor_scalar(place_i[:], slot_i[:], P - 1, None, ALU.bitwise_and)
            chain(dve.tensor_scalar(tile_i[:], slot_i[:], P.bit_length() - 1, None, ALU.logical_shift_right))
            dve.tensor_copy(place[:], place_i[:])
            chain(dve.tensor_copy(tile[:], tile_i[:]))
            over_tiles = lambda ap: ap.unsqueeze(2).to_broadcast([P, TILES, SLOT_TILES])
            for w in range(2):
                dve.tensor_tensor(of_tile[:, w], tile_no[:].unsqueeze(1).to_broadcast([P, TILES, SLOT_TILES]),
                                  over_tiles(tile[:, w, :]), ALU.is_equal).then_inc(tiles_set, 1)
            dve.wait_ge(den_ready, 1)
            chain(dve.reciprocal(weight[:], den[:]))
            chain(dve.tensor_copy(w_hi[:], weight[:]))
            dve.tensor_tensor(w_lo[:], weight[:], w_hi[:], ALU.subtract).then_inc(tiles_set, 1)
            dve.wait_ge(tiles_set, 3)
            for w in range(2):
                dve.tensor_tensor(at_tile[:, w, :, 0, :], of_tile[:, w], over_tiles(row_no[:]), ALU.mult).then_inc(tiles_ready, 1)
            for w in range(2):
                dve.tensor_tensor(at_place[:, w], place_no[:].unsqueeze(1).to_broadcast([P, TILES, P]),
                                  place[:, w, :].unsqueeze(2).to_broadcast([P, TILES, P]), ALU.is_equal).then_inc(places_ready, 1)
            dve.wait_ge(slots_done, 1)
            chain(dve.tensor_scalar(taken[:], ps_slots[:, 0, :], 0.5, None, ALU.is_gt))
            chain(dve.tensor_copy(c.weight_at[:], ps_slots[:, 1, :]))
            chain(dve.tensor_tensor(c.weight_at[:], c.weight_at[:], ps_slots[:, 2, :], ALU.add))
            chain(dve.tensor_scalar(taken[:], taken[:], -1.0, 1.0, ALU.mult, ALU.add))
            chain(dve.tensor_tensor(taken[:], taken[:], empty_row[:], ALU.mult))
            chain(dve.tensor_tensor(taken[:], taken[:], ps_slots[:, 0, :], ALU.add))
            chain(dve.tensor_scalar(taken[:], taken[:], -1.0, None, ALU.add))
            chain(dve.tensor_copy(c.token_at[:], taken[:]))


def ffn_stage(nc, d, c, out):
    with ExitStack() as ctx:
        sb = lambda name, shape, dt=F32: ctx.enter_context(nc.sbuf_tensor("ffn_" + name, shape, dt))
        sem = lambda name: ctx.enter_context(nc.semaphore("ffn_" + name))
        raw, raw_in = c.raw, c.raw_in
        w1, w3 = sb("w1", [P, 2, HL, KC, FF], F32R), sb("w3", [P, 2, HL, KC, FF], F32R)
        w2 = sb("w2", [P, 2, HL, FC, E], F32R)
        x_in = [sb(f"x_in{i}{t}", [P, E]) for i in range(2) for t in range(TT)]
        xT = sb("xT", [P, 2, HL, KC, NT], F32R)
        silu = sb("silu", [P, 2, GF, NT])
        hid_f = sb("hid_f", [P, 2, GF, NT])
        hid = sb("hid", [P, HL, FC, NT], F32R)
        y_out = [sb(f"y_out{i}{t}", [P, E]) for i in range(2) for t in range(TT)]
        row_in, row_out = sb("row_in", [P, 2, TT], U32), sb("row_out", [P, 2, TT], U32)
        weight = sb("weight", [P, 2, TT])
        words = sb("words", [P, 3, 2])
        ps = ctx.enter_context(nc.psum_tensor("ps_ffn", [P, 6, BANK], F32))
        ps_up = ps[:, 0:4, :].rearrange("p (b f) n -> p b f n", b=2)
        ps_y = ps[:, 4, :].rearrange("p (t e) -> p t e", t=TT)
        ps_t = ps[:, 5, :].rearrange("p (k n) -> p k n", k=KC)
        hi_done = [sem("w1_hi_done"), sem("w3_hi_done"), sem("w2_hi_done")]
        lo_done = [sem("w1_lo_done"), sem("w3_lo_done"), sem("w2_lo_done")]
        gathered = [sem("gathered0"), sem("gathered1")]
        added = [sem("added0"), sem("added1")]
        row_in_set, xt_done, x_hi_done, x_lo_done = (sem(n) for n in ("row_in_set", "xt_done", "x_hi_done", "x_lo_done"))
        up_done, silu_done, hid_f_done, hid_ready = (sem(n) for n in ("up_done", "silu_done", "hid_f_done", "hid_ready"))
        down_done, y_ready, copied, link = (sem(n) for n in ("down_done", "y_ready", "copied", "dve_link"))
        block = ctx.enter_context(nc.Block())
        parts = (w1, w3, w2)
        W1, W3, W2 = range(3)

        def turns(eng, step, chain=None, links=0):
            for j in range(3):
                step(j, j // 2, j % 2)
            pairs = (TURNS_X - 5) // 2
            with eng.Fori(1, 1 + pairs) as i:
                if chain:
                    chain.enter(i - 1, links)
                step(2 * i + 1, i, 1)
                step(2 * i + 2, i + 1, 0)
                if chain:
                    chain.leave(pairs)
            for j in range(3 + 2 * pairs, TURNS_X):
                step(j, j // 2, j % 2)

        is_turn = lambda j: not isinstance(j, int) or j < TURNS_X

        @block.sync
        def _(sp):
            with sp.Fori(1, TURNS_X) as j:
                load_expert(sp, d, c, j, lo_done)
            for par in range(2):
                sp.wait_ge(added[par], 16 * TT * ((TURNS_X + 1 - par) // 2))
            PIECES = 8
            for n in range(PIECES):
                at = slice(n * TOK // PIECES, (n + 1) * TOK // PIECES)
                sp.dma_start(out[at], d["sum_rows"][at]).then_inc(copied, 16)
            sp.wait_ge(copied, 16 * PIECES)

        @block.gpsimd
        def _(pool):
            def split_lo(n, j, par):
                pool.wait_ge(hi_done[n], j + 1)
                pool.tensor_tensor(parts[n][:, par, LO], raw[n][:], parts[n][:, par, HI], ALU.subtract).then_inc(lo_done[n], 1)

            def gather(j, par, word=0):
                pool.wait_ge(row_in_set, j + 1)
                wait(pool, xt_done, j - 1)
                pool.tensor_tensor(words[:, word, par:par + 1], c.ident[:, 0:1], c.ident[:, 0:1], ALU.mult)
                for t in range(TT):
                    pool.indirect_dma_start(x_in[par * TT + t][:], None, d["xn_rows"],
                                            bass.IndirectOffsetOnAxis(ap=row_in[:, par, t:t + 1], axis=0)
                                            ).then_inc(gathered[par], 16)

            def add(j, half, par):
                pool.wait_ge(y_ready, j + 1)
                wait(pool, added[1 - par], 16 * TT * (half + par))
                pool.tensor_tensor(words[:, 1, par:par + 1], c.ident[:, 0:1], c.ident[:, 0:1], ALU.mult)
                for t in range(TT):
                    pool.indirect_dma_start(d["sum_rows"], bass.IndirectOffsetOnAxis(ap=row_out[:, par, t:t + 1], axis=0),
                                            y_out[par * TT + t][:], None, compute_op=ALU.add).then_inc(added[par], 16)

            def step(j, half, par):
                if is_turn(j + 1):
                    split_lo(W1, j + 1, 1 - par)
                if not isinstance(j, int) or j > 0:
                    add(j - 1, half + par - 1, 1 - par)
                if is_turn(j + 2):
                    gather(j + 2, par)
                if is_turn(j + 1):
                    split_lo(W2, j + 1, 1 - par)

            for j in range(2):
                gather(j, j, word=2)
            split_lo(W2, 0, 0)
            turns(pool, step)
            add(TURNS_X - 1, (TURNS_X - 1) // 2, (TURNS_X - 1) % 2)

        @block.tensor
        def _(pe):
            PASSES = ((HI, HI), (HI, LO), (LO, HI))

            def transposes(j, half, par):
                pe.wait_ge(gathered[par], 16 * TT * (half + 1))
                for k in range(KC):
                    for t in range(TT):
                        last = pe.transpose(ps_t[:, k, t * P:(t + 1) * P], x_in[par * TT + t][:, k * P:(k + 1) * P], c.ident[:])
                last.then_inc(xt_done, 1)

            def up(j, par, g):
                n = j * G + g
                if g == 0:
                    for q in (x_lo_done, lo_done[W1], lo_done[W3]):
                        pe.wait_ge(q, j + 1)
                if not isinstance(j, int) or n >= 2:
                    pe.wait_ge(hid_f_done, n - 1)
                for f in range(g * GF, (g + 1) * GF):
                    for m, w in enumerate((w1, w3)):
                        for k in range(KC):
                            for q, (a, b) in enumerate(PASSES):
                                last = pe.matmul(ps_up[:, g % 2, f % GF, m * NT:(m + 1) * NT], w[:, par, a, k, f * P:(f + 1) * P],
                                                 xT[:, par, b, k, :], start=(k == 0 and q == 0), stop=(k == KC - 1 and q == 2))
                last.then_inc(up_done, 1)

            def down(j, par):
                pe.wait_ge(lo_done[W2], j + 1)
                pe.wait_ge(hid_ready, (j + 1) * G)
                wait(pe, y_ready, j)
                for t in range(TT):
                    for f in range(FC):
                        for q, (a, b) in enumerate(PASSES):
                            last = pe.matmul(ps_y[:, t, :], hid[:, a, f, t * P:(t + 1) * P], w2[:, par, b, f, :],
                                             start=(f == 0 and q == 0), stop=(f == FC - 1 and q == 2))
                last.then_inc(down_done, 1)

            def step(j, half, par):
                up(j, par, 0)
                if not isinstance(j, int) or j > 0:
                    down(j - 1, 1 - par)
                up(j, par, 1)
                if is_turn(j + 1):
                    transposes(j + 1, half + par, 1 - par)
                for g in range(2, G):
                    up(j, par, g)

            transposes(0, 0, 0)
            turns(pe, step)
            down(TURNS_X - 1, (TURNS_X - 1) % 2)

        @block.scalar
        def _(act):
            def split_hi(n, j, par):
                act.wait_ge(raw_in[n], 16 * (j + 1))
                if n == W2:
                    wait(act, down_done, j - 1)
                act.copy(parts[n][:, par, HI], raw[n][:]).then_inc(hi_done[n], 1)

            def x_hi(j, par):
                act.wait_ge(xt_done, j + 1)
                act.copy(xT[:, par, HI], ps_t).then_inc(x_hi_done, 1)

            def silus(j, g):
                n = j * G + g
                act.wait_ge(up_done, n + 1)
                if not isinstance(j, int) or n >= 2:
                    act.wait_ge(hid_f_done, n - 1)
                act.activation(silu[:, g % 2], ps_up[:, g % 2, :, 0:NT], ACT.Silu, bias=0.0).then_inc(silu_done, 1)

            def step(j, half, par):
                silus(j, 0)
                if is_turn(j + 1):
                    split_hi(W3, j + 1, 1 - par)
                    split_hi(W1, j + 1, 1 - par)
                silus(j, 1)
                if is_turn(j + 1):
                    x_hi(j + 1, 1 - par)
                    split_hi(W2, j + 1, 1 - par)
                silus(j, 2)
                silus(j, 3)

            split_hi(W1, 0, 0)
            split_hi(W3, 0, 0)
            x_hi(0, 0)
            split_hi(W2, 0, 0)
            turns(act, step)

        @block.vector
        def _(dve):
            chain = Chain(dve, link)

            def split_lo(n, j, par):
                dve.wait_ge(hi_done[n], j + 1)
                dve.tensor_tensor(parts[n][:, par, LO], raw[n][:], parts[n][:, par, HI], ALU.subtract).then_inc(lo_done[n], 1)

            def x_lo(j, par):
                dve.wait_ge(x_hi_done, j + 1)
                dve.tensor_tensor(xT[:, par, LO], ps_t, xT[:, par, HI], ALU.subtract).then_inc(x_lo_done, 1)

            def set_rows_in(j, par):
                dve.tensor_copy(row_in[:, par, :], c.token_at[:, bass.ds(j * TT, TT)]).then_inc(row_in_set, 1)

            def gate_up(j, g):
                dve.wait_ge(silu_done, j * G + g + 1)
                dve.tensor_tensor(hid_f[:, g % 2], ps_up[:, g % 2, :, NT:2 * NT], silu[:, g % 2], ALU.mult).then_inc(hid_f_done, 1)

            def split_hid(j, g):
                at = slice(g * GF, (g + 1) * GF)
                dve.wait_ge(hid_f_done, j * G + g + 1)
                chain(dve.tensor_copy(hid[:, HI, at], hid_f[:, g % 2]))
                dve.tensor_tensor(hid[:, LO, at], hid_f[:, g % 2], hid[:, HI, at], ALU.subtract).then_inc(hid_ready, 1)

            def results(j, half, par):
                dve.wait_ge(down_done, j + 1)
                wait(dve, added[par], 16 * TT * half)
                dve.tensor_copy(row_out[:, par, :], c.token_at[:, bass.ds(j * TT, TT)])
                chain(dve.tensor_copy(weight[:, par, :], c.weight_at[:, bass.ds(j * TT, TT)]))
                for t in range(TT):
                    last = dve.tensor_scalar(y_out[par * TT + t][:], ps_y[:, t, :], weight[:, par, t:t + 1], None, ALU.mult)
                last.then_inc(y_ready, 1)

            def step(j, half, par):
                gate_up(j, 0)
                if is_turn(j + 1):
                    split_lo(W3, j + 1, 1 - par)
                if is_turn(j + 2):
                    set_rows_in(j + 2, par)
                if not isinstance(j, int) or j > 0:
                    results(j - 1, half + par - 1, 1 - par)
                split_hid(j, 0)
                gate_up(j, 1)
                split_hid(j, 1)
                if is_turn(j + 1):
                    x_lo(j + 1, 1 - par)
                for g in (2, 3):
                    gate_up(j, g)
                    split_hid(j, g)

            for j in range(2):
                set_rows_in(j, j)
            split_lo(W1, 0, 0)
            split_lo(W3, 0, 0)
            x_lo(0, 0)
            turns(dve, step, chain, 2 * (G + 1))
            j = TURNS_X - 1
            results(j, j // 2, j % 2)


class Kept:
    pass


def audio_tower(nc, d):
    rows = lambda name, *shape: nc.dram_tensor(name, list(shape), F32, kind="Internal").ap()
    d["scan"] = rows("scan_rows", TOK + 1, ARRAYS, E)
    d["y"] = rows("y_rows", TOK, E)
    d["xn_rows"] = rows("xn_rows", ROWS, E)
    d["sum_rows"] = rows("sum_rows", ROWS, E)
    c = Kept()
    with ExitStack() as ctx:
        sb = lambda name, shape, dt=F32: ctx.enter_context(nc.sbuf_tensor(name, shape, dt))
        c.ident = sb("ident", [P, P])
        c.turn_expert = sb("turn_expert", [P, TURNS_X], I32)
        c.token_at = sb("token_at", [P, SLOT_TILES], U32)
        c.weight_at = sb("weight_at", [P, SLOT_TILES])
        c.raw = [sb("raw1", [P, KC, FF]), sb("raw3", [P, KC, FF]), sb("raw2", [P, FC, E])]
        c.raw_in = [ctx.enter_context(nc.semaphore(n)) for n in ("raw1_in", "raw3_in", "raw2_in")]
        with ExitStack() as inner:
            keep = lambda name, shape: inner.enter_context(nc.sbuf_tensor(name, shape, F32))
            c.h = keep("h", [P, TILES, E])
            c.xnT = keep("xnT", [P, KC, TOK])
            c.mix_w = {name: keep("mix_" + name, shape) for name, _, shape in MIX_WEIGHTS}
            c.mix_w_in = inner.enter_context(nc.semaphore("mix_w_in"))
            tok_stage(nc, d, c)
            c.gate = keep("gate", [P, TILES, E])
            c.bonus = keep("bonus", [P, TILES, E])
            mix_stage(nc, d, c)
            scan_stage(nc, d, c)
            out_stage(nc, d, c)
        ffn_stage(nc, d, c, d["out"].rearrange("b t e -> (b t) e"))


def layout(i):
    g = lambda n: np.asarray(i[n])
    t = lambda a: np.ascontiguousarray(np.swapaxes(a, -1, -2))
    z = lambda *s: np.zeros(s, np.float32)
    tok, att, ffn = "L0_tok_", "L0_attn_", "L0_ffn_"
    a = lambda n: g(att + n)
    w_a1T = np.concatenate([t(a("decay_w1")), t(a("aaa_w1")), z(256, 16), t(a("ma_w1")), z(256, 16)], 1)
    w_a2 = np.concatenate([
        np.concatenate([a("decay_w2"), z(64, 512)], 1),
        np.concatenate([z(16, 256), a("aaa_w2"), z(16, 256)], 1), z(16, 768),
        np.concatenate([z(16, 512), a("ma_w2")], 1),
        np.concatenate([a("time_decay"), a("time_aaaaa"), a("time_misc_a")])[None], z(15, 768)], 0)
    w_b1T = np.concatenate([t(a("kkk_w1")), z(256, 16), t(a("mk_w1")), z(256, 16)], 1)
    w_b2 = np.concatenate([
        np.concatenate([a("kkk_w2"), z(16, 256)], 1), z(16, 512),
        np.concatenate([z(16, 256), a("mk_w2")], 1),
        np.concatenate([z(256), a("time_misc_k")])[None], z(15, 512)], 0)
    ones = z(128, 2)
    ones[112, 0] = 1.0
    ones[48, 1] = 1.0
    maa = np.concatenate([t(a("time_maa").reshape(4, 256)), a("time_maa_x")[:, None]], 1)
    c = np.ascontiguousarray
    return {
        "x": g("x"), "xT": t(g("x")), "wqT": t(g(tok + "Wq")), "wkT": t(g(tok + "Wk")), "wv": g(tok + "Wv"),
        "gamma": g(tok + "gamma"), "beta": g(tok + "beta"),
        "maa": c(maa), "maa_w1T": t(a("maa_w1")), "maa_w2": a("maa_w2").reshape(128, 256),
        "w_rT": t(a("Wr")), "w_kT": t(a("Wk")), "w_vT": t(a("Wv")), "w_oT": t(a("Wo")),
        "w_a1T": c(w_a1T), "w_a2": c(w_a2), "w_b1T": c(w_b1T), "w_b2": c(w_b2), "a_bias": ones,
        "w_g1T": t(a("gate_w1")), "w_g2": a("gate_w2"), "faaaa": a("time_faaaa"),
        "ln_w": a("ln_w"), "ln_b": a("ln_b"),
        "gate_w": g(ffn + "gate_w"), "w1": g(ffn + "w1"), "w2": g(ffn + "w2"), "w3": g(ffn + "w3"),
    }


def kernel(**inputs):
    from concourse import bacc
    from concourse.bass_utils import run_bass_kernel_spmd

    nc = bacc.Bacc("TRN2", target_bir_lowering=False, num_devices=1)
    arrays = layout(inputs)
    d = {name: nc.dram_tensor(f"in_{name}", a.shape, mybir.dt.from_np(a.dtype), kind="ExternalInput").ap()
         for name, a in arrays.items()}
    d["out"] = nc.dram_tensor("out_0", (B, T, E), F32, kind="ExternalOutput").ap()
    audio_tower(nc, d)
    ran = run_bass_kernel_spmd(nc, [{f"in_{name}": a for name, a in arrays.items()}], core_ids=[0])
    return ran.results[0]["out_0"]
```
